# Optimizing a Trainium2 kernel written in Bass

```python
import numpy as np
import jax
import jax.numpy as jnp

def _softmax(x, axis=-1):
    return jax.nn.softmax(x, axis=axis)

def _gelu(x):
    return jax.nn.gelu(x, approximate=True)

def _silu(x):
    return jax.nn.silu(x)

def _sigmoid(x):
    return jax.nn.sigmoid(x)

def _layernorm(x, axis=-1, eps=1e-05):
    m = jnp.mean(x, axis=axis, keepdims=True)
    v = jnp.var(x, axis=axis, keepdims=True)
    return (x - m) / jnp.sqrt(v + eps)

def _scatter_add(tgt, idx, src, axis=0):
    return tgt.at[idx].add(src)

def _segment_sum(src, seg, n):
    return jax.ops.segment_sum(src, seg, n)
kernel_name = 'mk_gnn_resnorm_d2_gnn_r8_c67f00'

def setup_inputs(seed: int=0):
    np.random.seed(seed)
    _w = jnp.asarray

    def _rec_inputs():
        import jax
        import jax.numpy as jnp
        _gk = jax.random.key(seed)
        x = -0.000202 + 1 * jax.random.normal(jax.random.fold_in(_gk, 1), (12500, 64), jnp.float32)
        _s = jax.random.randint(jax.random.fold_in(_gk, 2), (100000,), 0, 12500, jnp.int32)
        _d = jax.random.randint(jax.random.fold_in(_gk, 3), (100000,), 0, 12500, jnp.int32)
        _loop = jnp.arange(12500, dtype=jnp.int32)
        src = jnp.concatenate([_s, _d, _loop])
        dst = jnp.concatenate([_d, _s, _loop])
        _o = jnp.argsort(dst, stable=True)
        src = src[_o]
        dst = dst[_o]
        return (x, src, dst)
    x, src, dst = _rec_inputs()

    def _L0_gnn_setup():
        import jax, jax.numpy as jnp
        import numpy as np
        N_NODES = 12500
        N_EDGES = 200000
        F_DIM = 64
        H_DIM = 256
        K_CLUSTERS = 64
        key = jax.random.key(seed)
        ks = jax.random.split(key, 9)
        X = jax.random.normal(ks[0], (N_NODES, F_DIM), dtype=jnp.float32)
        ei_feat = jax.random.randint(ks[1], (2, N_EDGES), 0, N_NODES, dtype=jnp.int64)
        batch = jnp.zeros((N_NODES,), dtype=jnp.int64)
        h2 = H_DIM // 2
        W_nuc = jax.random.normal(ks[2], (32, h2), dtype=jnp.float32) / np.sqrt(32.0)
        b_nuc = jnp.zeros((h2,), dtype=jnp.float32)
        W_surf = jax.random.normal(ks[3], (32, h2), dtype=jnp.float32) / np.sqrt(32.0)
        b_surf = jnp.zeros((h2,), dtype=jnp.float32)
        W_fuse = jax.random.normal(ks[4], (H_DIM, K_CLUSTERS), dtype=jnp.float32) / np.sqrt(float(H_DIM))
        b_fuse = jnp.zeros((K_CLUSTERS,), dtype=jnp.float32)
        return {'X': X, 'ei_feat': ei_feat, 'batch': batch, 'W_nuc': W_nuc, 'b_nuc': b_nuc, 'W_surf': W_surf, 'b_surf': b_surf, 'W_fuse': W_fuse, 'b_fuse': b_fuse}
    _L0_gnn_all = _L0_gnn_setup()
    _L0_gnn_in = {k: v for k, v in _L0_gnn_all.items() if k in ('W_nuc', 'b_nuc', 'W_surf', 'b_surf', 'W_fuse', 'b_fuse')}
    del _L0_gnn_all

    def _L1_gnn_setup():
        import jax, jax.numpy as jnp
        import numpy as np
        N, E = (12500, 200000)
        D_NODE, D_HID_M, D_OUT_M = (64, 128, 64)
        D_HID_U, D_OUT_U = (128, 64)

        def _glorot(key, shape):
            fan_in, fan_out = shape
            lim = (6.0 / (fan_in + fan_out)) ** 0.5
            return jax.random.uniform(key, shape, jnp.float32, -lim, lim)

        def _mlp3(x, W1, b1, W2, b2, W3, b3):
            h = jax.nn.relu(x @ W1 + b1)
            h = jax.nn.relu(h @ W2 + b2)
            return h @ W3 + b3
        key = jax.random.key(seed)
        ks = jax.random.split(key, 16)
        node_features = jax.random.normal(ks[0], (N, D_NODE), jnp.float32)
        edge_index = jax.random.randint(ks[1], (2, E), 0, N, jnp.int64)
        d_in_U = D_NODE + D_OUT_M
        return {'node_features': node_features, 'edge_index': edge_index, 'WM1': _glorot(ks[2], (D_NODE, D_HID_M)), 'bM1': jnp.zeros((D_HID_M,), jnp.float32), 'WM2': _glorot(ks[3], (D_HID_M, D_HID_M)), 'bM2': jnp.zeros((D_HID_M,), jnp.float32), 'WM3': _glorot(ks[4], (D_HID_M, D_OUT_M)), 'bM3': jnp.zeros((D_OUT_M,), jnp.float32), 'WU1': _glorot(ks[5], (d_in_U, D_HID_U)), 'bU1': jnp.zeros((D_HID_U,), jnp.float32), 'WU2': _glorot(ks[6], (D_HID_U, D_HID_U)), 'bU2': jnp.zeros((D_HID_U,), jnp.float32), 'WU3': _glorot(ks[7], (D_HID_U, D_OUT_U)), 'bU3': jnp.zeros((D_OUT_U,), jnp.float32)}
    _L1_gnn_all = _L1_gnn_setup()
    _L1_gnn_in = {k: v for k, v in _L1_gnn_all.items() if k in ('WM1', 'bM1', 'WM2', 'bM2', 'WM3', 'bM3', 'WU1', 'bU1', 'WU2', 'bU2', 'WU3', 'bU3')}
    del _L1_gnn_all
    return {'x': x, 'src': src, 'dst': dst, 'L0_gnn_W_nuc': _L0_gnn_in['W_nuc'], 'L0_gnn_b_nuc': _L0_gnn_in['b_nuc'], 'L0_gnn_W_surf': _L0_gnn_in['W_surf'], 'L0_gnn_b_surf': _L0_gnn_in['b_surf'], 'L0_gnn_W_fuse': _L0_gnn_in['W_fuse'], 'L0_gnn_b_fuse': _L0_gnn_in['b_fuse'], 'L1_gnn_WM1': _L1_gnn_in['WM1'], 'L1_gnn_bM1': _L1_gnn_in['bM1'], 'L1_gnn_WM2': _L1_gnn_in['WM2'], 'L1_gnn_bM2': _L1_gnn_in['bM2'], 'L1_gnn_WM3': _L1_gnn_in['WM3'], 'L1_gnn_bM3': _L1_gnn_in['bM3'], 'L1_gnn_WU1': _L1_gnn_in['WU1'], 'L1_gnn_bU1': _L1_gnn_in['bU1'], 'L1_gnn_WU2': _L1_gnn_in['WU2'], 'L1_gnn_bU2': _L1_gnn_in['bU2'], 'L1_gnn_WU3': _L1_gnn_in['WU3'], 'L1_gnn_bU3': _L1_gnn_in['bU3']}

def reference(x, src, dst, L0_gnn_W_nuc, L0_gnn_b_nuc, L0_gnn_W_surf, L0_gnn_b_surf, L0_gnn_W_fuse, L0_gnn_b_fuse, L1_gnn_WM1, L1_gnn_bM1, L1_gnn_WM2, L1_gnn_bM2, L1_gnn_WM3, L1_gnn_bM3, L1_gnn_WU1, L1_gnn_bU1, L1_gnn_WU2, L1_gnn_bU2, L1_gnn_WU3, L1_gnn_bU3):
    import jax
    import jax.numpy as jnp

    def _L0_gnn_ref(X, ei_feat, batch, W_nuc, b_nuc, W_surf, b_surf, W_fuse, b_fuse):
        import jax, jax.numpy as jnp
        import numpy as np
        N_NODES = 12500
        N_EDGES = 200000
        F_DIM = 64
        H_DIM = 256
        K_CLUSTERS = 64
        N = X.shape[0]
        loop = jnp.arange(N)
        src = jnp.concatenate([ei_feat[0], loop])
        dst = jnp.concatenate([ei_feat[1], loop])
        deg = jax.ops.segment_sum(jnp.ones(src.shape[0], X.dtype), dst, num_segments=N)
        dinv = jnp.where(deg > 0, jax.lax.rsqrt(jnp.maximum(deg, 1.0)), 0.0)
        norm = dinv[src] * dinv[dst]

        def gcn(h, W, b):
            m = (h @ W)[src] * norm[:, None]
            return jax.ops.segment_sum(m, dst, num_segments=N) + b
        h_nuc = jax.nn.elu(gcn(X[:, :32], W_nuc, b_nuc))
        h_surf = jax.nn.elu(gcn(X[:, 32:], W_surf, b_surf))
        h_fused = jnp.concatenate([h_nuc, h_surf], axis=1)
        return jax.nn.softmax(gcn(h_fused, W_fuse, b_fuse), axis=1)

    def _L1_gnn_ref(node_features, edge_index, WM1, bM1, WM2, bM2, WM3, bM3, WU1, bU1, WU2, bU2, WU3, bU3):
        import jax, jax.numpy as jnp
        import numpy as np
        N, E = (12500, 200000)
        D_NODE, D_HID_M, D_OUT_M = (64, 128, 64)
        D_HID_U, D_OUT_U = (128, 64)

        def _glorot(key, shape):
            fan_in, fan_out = shape
            lim = (6.0 / (fan_in + fan_out)) ** 0.5
            return jax.random.uniform(key, shape, jnp.float32, -lim, lim)

        def _mlp3(x, W1, b1, W2, b2, W3, b3):
            h = jax.nn.relu(x @ W1 + b1)
            h = jax.nn.relu(h @ W2 + b2)
            return h @ W3 + b3
        source, destination = (edge_index[0], edge_index[1])
        message = node_features[source]
        y = _mlp3(message, WM1, bM1, WM2, bM2, WM3, bM3)
        z = jax.ops.segment_sum(y, destination, num_segments=node_features.shape[0])
        return _mlp3(jnp.concatenate([node_features, z], axis=-1), WU1, bU1, WU2, bU2, WU3, bU3)
    edge_index = jnp.stack([src, dst])
    batch0 = jnp.zeros((12500,), jnp.int32)
    x = _layernorm(x + _L0_gnn_ref(x, edge_index, batch0, L0_gnn_W_nuc, L0_gnn_b_nuc, L0_gnn_W_surf, L0_gnn_b_surf, L0_gnn_W_fuse, L0_gnn_b_fuse), axis=-1)
    x = _layernorm(x + _L1_gnn_ref(x, edge_index, L1_gnn_WM1, L1_gnn_bM1, L1_gnn_WM2, L1_gnn_bM2, L1_gnn_WM3, L1_gnn_bM3, L1_gnn_WU1, L1_gnn_bU1, L1_gnn_WU2, L1_gnn_bU2, L1_gnn_WU3, L1_gnn_bU3), axis=-1)
    return x

_drawn_inputs = setup_inputs


def setup_inputs(seed=0):
    import zlib

    import numpy as np

    out = dict(_drawn_inputs(seed))
    spreads = {'L0_gnn_b_nuc': (0.0, 0.8),
     'L0_gnn_b_surf': (0.0, 0.8),
     'L0_gnn_b_fuse': (0.0, 2.0),
     'L1_gnn_bM1': (0.0, 0.1),
     'L1_gnn_bM2': (0.0, 0.1),
     'L1_gnn_bM3': (0.0, 0.1),
     'L1_gnn_bU1': (0.0, 0.273),
     'L1_gnn_bU2': (0.0, 0.1),
     'L1_gnn_bU3': (0.0, 0.1)}
    factors = {'L0_gnn_W_nuc': 8.0, 'L0_gnn_W_surf': 8.0, 'L0_gnn_W_fuse': 8.0}
    for name, (base, spread) in spreads.items():
        noise = np.random.default_rng([zlib.crc32(name.encode()), seed]).standard_normal(out[name].shape)
        drawn = base * np.exp(spread * noise) if base else spread * noise
        out[name] = jnp.asarray(drawn.astype(out[name].dtype))
    for name, factor in factors.items():
        out[name] = (out[name] * factor).astype(out[name].dtype)
    return out
```

```python
from contextlib import ExitStack

import concourse.bass as bass
from concourse import mybir

ALU = mybir.AluOpType
ACT = mybir.ActivationFunctionType
F32 = mybir.dt.float32
F16 = mybir.dt.float16
BF16 = mybir.dt.bfloat16
F8 = mybir.dt.float8e4
I32 = mybir.dt.int32
U32 = mybir.dt.uint32
U8 = mybir.dt.uint8
AX = mybir.AxisListType.X

P = 128
NODES = 12500
EDGES = 212500
F = 64
H = 128
NB = -(-NODES // P)
LAST = NODES - (NB - 1) * P
TILES = 1664
WN = 4
WB = P // WN
NBW = -(-NB // 4) * 4
GROUPS = NBW * WB // P
GC = 5
KEYS = NB * WN
PAD_DST = 16383
SINK = PAD_DST + 1
SUMROWS = SINK + P
DP = 2 * P
NP = NB // 2
PW = 2 * WB
MAXCOUNT = 16
REACH = 12
NEAR = MAXCOUNT - (P - 1 - MAXCOUNT) // REACH
EXP1 = 1 << 23
FAR = float(1 << 22)
MIDDLE = (WN - 1) / 2
UB = 7
UNITS = NB // UB
UN = UB * P
MLP_BYTES = 4 * (UB * F + 4 * UN)
GCN_BYTES = 4 * (UB * F + 7 * UN)
EPS = 1e-5


class Chain:

    def __init__(self, eng, sem, base=0):
        self.eng, self.sem, self.base, self.n = eng, sem, base, 0

    def link(self, ins):
        self.n += 1
        ins.then_inc(self.sem, 1)
        self.eng.wait_ge(self.sem, self.base + self.n)


def stagger(eng, stages, count):
    depth = max(k for k, _ in stages)
    early = (depth + 3) // 2 * 2

    def step(s, odd, low, high):
        for k, body in stages:
            if low <= k <= high:
                body(s - k, (odd - k) % 2)

    for s in range(early):
        step(s, s % 2, 0, s)
    with eng.Fori(early // 2, count // 2) as i:
        for odd in range(2):
            step(2 * i + odd, odd, 0, depth)
    for s in range(count, count + depth):
        step(s, s % 2, s - count + 1, depth)


def wait_apart(eng, *waits):
    for _, value in waits:
        eng.compute_val(value)
    eng.wait_ge(waits[0][0], 1)
    for sem, value in waits:
        eng.wait_ge(sem, value)


def wait_past(eng, sem, value):
    if not (isinstance(value, int) and value < 1):
        eng.wait_ge(sem, value)


def over(col):
    return col.unsqueeze(2).broadcast_to((P, col.shape[1], F))


def each(row, blocks):
    return row[:, :].unsqueeze(1).broadcast_to((P, blocks, F))


def build(nc, a, out):
    with ExitStack() as ctx:
        def sb(name, shape, dt):
            return ctx.enter_context(nc.sbuf_tensor(name, shape, dt))

        def sem(name):
            return ctx.enter_context(nc.semaphore(name))

        counts_dram = nc.dram_tensor("counts_dram", (NP, P, NB * DP), U8).ap()
        feat_dram = nc.dram_tensor("feat_dram", (NB * P, F), F32).ap()
        sum_dram = nc.dram_tensor("sum_dram", (SUMROWS, F), F32).ap()

        X = sb("X", [P, NB, F], F32)
        Hf = sb("Hf", [P, NB, F], F32)
        HL = sb("HL", [P, NB, 2 * F], F16)
        region = sb("region", [P, 3, NB * DP], U8)
        keyT = sb("keyT", [P, GROUPS * P], F32)
        loT = sb("loT", [P, GROUPS * P], F16)
        deg = sb("deg", [P, NBW], F32)
        dinv = sb("dinv", [P, NB], F32)
        stat = sb("stat", [P, 3, NB], F32)
        ident = sb("ident", [P, P], F32)
        ones = sb("ones", [P, P], F32)
        iota_k = sb("iota_k", [P, KEYS], F16)
        stack = sb("stack", [P, F], F32)
        scales = sb("scales", [P, 2], F32)
        merge = sb("merge", [P, F], F32)
        flag = sb("flag", [1, 1], I32)
        w_fuse = sb("w_fuse", [P, 2, F], F32)
        w_gcn = sb("w_gcn", [F, 2 * H], F32)
        b_gcn = sb("b_gcn", [P, 2], F32)
        b_fuse = sb("b_fuse", [P, F], F32)
        wm1 = sb("wm1", [F, H], F32)
        wm2 = sb("wm2", [H, H], F32)
        wm3 = sb("wm3", [H, F], F32)
        wu1 = sb("wu1", [2 * F, H], F32)
        wu2 = sb("wu2", [H, H], F32)
        wu3 = sb("wu3", [H, F], F32)
        b_hid = sb("b_hid", [P, 4], F32)
        b_m3 = sb("b_m3", [P, F], F32)
        b_u3 = sb("b_u3", [P, F], F32)

        counts8 = [region[:, b, :].bitcast(F8).rearrange("p (h d) -> p h d", d=DP) for b in range(3)]
        flat = region[:, :, :].rearrange("p a b -> p (a b)")

        def scratch(at, n, dt):
            return flat[:, at:at + 4 * n].bitcast(dt)

        def share(*shapes, start=0):
            at, views = start, []
            for rows, *dims in shapes:
                n = 1
                for d in dims:
                    n *= d
                view = scratch(at, n, F32)[0:rows, :]
                if len(dims) == 2:
                    view = view.rearrange("p (a b) -> p a b", b=dims[1])
                views.append(view)
                at += 4 * n
            return views

        x_blocks = a["x_blocks"].rearrange("(j p) f -> p j f", p=P)
        feat_blocks = feat_dram.rearrange("(j p) f -> p j f", p=P)
        sum_blocks = sum_dram[0:NB * P, :].rearrange("(j p) f -> p j f", p=P)

        iota_i = Hf[:, 0:7, :].bitcast(I32).rearrange("p a b -> p (a b)")
        tri_i = Hf[:, 7:9, :].bitcast(I32).rearrange("p a b -> p (a b)")
        sel_i = Hf[:, 9:11, :].bitcast(I32).rearrange("p a b -> p (a b)")
        base_i = Hf[:, 11:12, 0:GROUPS].bitcast(I32).rearrange("p a b -> p (a b)")
        before = sb("before", [P, P], F32)
        first = sb("first", [P, GROUPS], F32)
        base = sb("base", [P, GROUPS], F32)
        trash = sb("trash", [P, 1], F32)
        LANES = 4
        iota_l = sb("iota_l", [P, P, LANES], F16)

        def prepare():
            loads = [(w_fuse[:, 0, :], a["W_fuse"][0:P, :]), (w_fuse[:, 1, :], a["W_fuse"][P:2 * P, :]),
                     (w_gcn[0:32, 0:H], a["W_nuc"]), (w_gcn[32:64, H:2 * H], a["W_surf"]),
                     (wm1[:, :], a["WM1"]), (wm2[:, :], a["WM2"]), (wm3[:, :], a["WM3"]),
                     (wu1[:, :], a["WU1"]), (wu2[:, :], a["WU2"]), (wu3[:, :], a["WU3"])]
            columns = [(b_gcn[:, 0:1], "b_nuc"), (b_gcn[:, 1:2], "b_surf"), (b_hid[:, 0:1], "bM1"),
                       (b_hid[:, 1:2], "bM2"), (b_hid[:, 2:3], "bU1"), (b_hid[:, 3:4], "bU2")]
            rows = [(b_fuse, "b_fuse"), (b_m3, "bM3"), (b_u3, "bU3")]
            CHUNKS = GROUPS // GC
            N = GC * P
            row_i = scratch(0, TILES, I32)
            row_f = scratch(4 * TILES, TILES, F32)
            below = scratch(8 * TILES, TILES // 2, F32).bitcast(BF16)
            at = 10 * TILES
            got = [scratch(at + c * 4 * 4 * N, 4 * N, I32).rearrange("p (g r e) -> p g r e", g=GC, r=4)
                   for c in range(2)]
            at += 32 * N
            rel = scratch(at, 2 * N, F32).rearrange("p (g r e) -> p g r e", g=GC, r=2)
            pen = scratch(at + 8 * N, 2 * N, F32).rearrange("p (g r e) -> p g r e", g=GC, r=2)
            low_i = scratch(at + 16 * N, 2 * N, I32).rearrange("p (g r e) -> p g r e", g=GC, r=2)
            low_half = scratch(at + 16 * N, 2 * N, F32).bitcast(mybir.dt.uint16) \
                .rearrange("p (g r e h) -> p g r e h", g=GC, r=2, h=2)[:, :, 0, :, 0]
            at += 24 * N
            select = scratch(at, 16 * P, F32).rearrange("p (k e) -> p k e", e=P)
            at += 64 * P
            masks = scratch(at, 2 * N, F32).bitcast(BF16).rearrange("p (k m) -> p k m", k=WN)
            code = Hf[:, 16:16 + 2 * 2 * GC, :].rearrange("p (c g a) b -> p c g (a b)", c=2, g=GC)
            parts = HL[:, :, :].rearrange("p a b -> p (a b)")
            same = parts[:, 0:REACH * N].bitcast(BF16).rearrange("p (t g e) -> p t g e", t=REACH, g=GC)
            code_16 = parts[:, REACH * N:(REACH + 1) * N].bitcast(mybir.dt.uint16) \
                .rearrange("p (g e) -> p g e", g=GC)
            with nc.psum_tensor("ps_key", [P, 2, 2, 512], F32) as ps_key, \
                    nc.psum_tensor("ps_win", [P, 512], F32) as ps_win, \
                    nc.psum_tensor("ps_deg", [P, 512], F32) as ps_deg, \
                    nc.psum_tensor("ps_bad", [P, 512], F32) as ps_bad, \
                    nc.sbuf_tensor("rows_below", [P, GROUPS], F32) as rows_below, \
                    nc.sbuf_tensor("win_deg", [P, GROUPS * WN], F32) as win_deg, \
                    nc.sbuf_tensor("ones_16", [P, 2], BF16) as ones_16, \
                    nc.sbuf_tensor("pairs", [P, GROUPS // GC], F32) as pairs, \
                    nc.sbuf_tensor("bad", [P, 3], F32) as bad, nc.sbuf_tensor("sums", [1, 4], F32) as sums, \
                    nc.sbuf_tensor("row_of", [P, GROUPS], U32) as row_of:
                rows_loaded, x_loaded, weights_loaded = sem("rows_loaded"), sem("x_loaded"), sem("weights_loaded")
                iotas_made, zeroed, ones_made = sem("iotas_made"), sem("zeroed"), sem("ones_made")
                rows_ready, step_p = sem("rows_ready"), sem("step_p")
                gathered = [sem(f"gathered{c}") for c in range(CHUNKS)]
                codes_made, turned, codes_read = sem("codes_made"), sem("turned"), sem("codes_read")
                same_made, same_read, masks_made, masks_read = (
                    sem(n) for n in ("same_made", "same_read", "masks_made", "masks_read"))
                win_ready, deg_made, bad_made, bad_summed = (
                    sem(n) for n in ("win_ready", "deg_made", "bad_made", "bad_summed"))

                with nc.Block() as block:
                    @block.sync
                    def _(sp):
                        sp.dma_start(row_i, a["row_first"].partition_broadcast(P)).then_inc(rows_loaded, 16)
                        sp.wait_ge(zeroed, 1)
                        for to, what in loads:
                            sp.dma_start(to, what).then_inc(weights_loaded, 16)
                        for to, name in columns:
                            sp.dma_start(to, a[name].rearrange("(p o) -> p o", o=1)).then_inc(weights_loaded, 16)
                        for to, name in rows:
                            sp.dma_start(to[:, :], a[name].partition_broadcast(P)).then_inc(weights_loaded, 16)
                        sp.dma_start(X[:, :, :], x_blocks).then_inc(x_loaded, 16)
                        sp.wait_ge(x_loaded, 16)
                        sp.wait_ge(weights_loaded, 16 * (len(loads) + len(columns) + len(rows)))

                    @block.gpsimd
                    def _(pool):
                        nc.gpsimd.iota(base_i, pattern=[[WN * P, GROUPS]], base=0,
                                       channel_multiplier=WN).then_inc(iotas_made, 1)
                        nc.gpsimd.iota(iota_i[:, 0:KEYS], pattern=[[1, KEYS]], base=0,
                                       channel_multiplier=0).then_inc(iotas_made, 1)
                        nc.gpsimd.iota(tri_i[:, 0:P], pattern=[[1, P]], base=0,
                                       channel_multiplier=-1).then_inc(iotas_made, 1)
                        nc.gpsimd.iota(sel_i[:, 0:P], pattern=[[-1, P]], base=0,
                                       channel_multiplier=WN).then_inc(iotas_made, 1)
                        nc.gpsimd.memset(w_gcn[:, :], 0.0).then_inc(zeroed, 1)
                        nc.gpsimd.memset(ones[:, :], 1.0).then_inc(ones_made, 1)
                        nc.gpsimd.memset(ones_16[:, :], 1.0).then_inc(ones_made, 1)
                        nc.gpsimd.memset(same, 0.0).then_inc(ones_made, 1)
                        for c in range(CHUNKS):
                            pool.wait_ge(rows_ready, c + 1)
                            if c >= 2:
                                pool.wait_ge(codes_made, c - 1)
                            for g in range(GC):
                                nc.gpsimd.indirect_dma_start(
                                    out=got[c % 2][:, g, :, :].rearrange("p r e -> p (r e)"), out_offset=None,
                                    in_=a["edge_rows"],
                                    in_offset=bass.IndirectOffsetOnAxis(
                                        ap=row_of[:, GC * c + g:GC * c + g + 1], axis=0)).then_inc(gathered[c], 16)

                    @block.scalar
                    def _(act):
                        for c in range(CHUNKS):
                            act.wait_ge(same_made, c + 1)
                            nc.scalar.activation(same[:, :, :, :], same[:, :, :, :], ACT.Copy,
                                                 accum_out=pairs[:, c:c + 1]).then_inc(same_read, 1)

                    @block.tensor
                    def _(pe):
                        for c in range(CHUNKS):
                            pe.wait_ge(codes_made, c + 1)
                            if c >= 2:
                                pe.wait_ge(codes_read, c - 1)
                            for g in range(GC):
                                last = nc.tensor.transpose(
                                    ps_key[:, c % 2, g // 4, g % 4 * P:g % 4 * P + P], code[:, c % 2, g, :],
                                    ident[:, :])
                            last.then_inc(turned, 1)
                            pe.wait_ge(masks_made, c + 1)
                            if c == 0:
                                pe.wait_ge(ones_made, 2)
                            for g in range(GC):
                                for k in range(WN):
                                    col = WN * (GC * c + g) + k
                                    last = nc.tensor.matmul(ps_win[:, col:col + 1], masks[:, k, P * g:P * g + P],
                                                            ones_16[:, 0:1], start=True, stop=True)
                            last.then_inc(masks_read, 1)
                        pe.wait_ge(win_ready, 1)
                        by_place = win_deg[:, :].rearrange("p (g k) -> p k g", k=WN)
                        for q in range(4):
                            for k in range(WN):
                                last = nc.tensor.matmul(ps_deg[:, 32 * q:32 * q + GROUPS], select[:, 4 * q + k, :],
                                                        by_place[:, k, :], start=k == 0, stop=k == WN - 1)
                        last.then_inc(deg_made, 1)
                        pe.wait_ge(bad_made, 1)
                        nc.tensor.matmul(ps_bad[:, 0:2], ones[:, :], bad[:, 0:2], start=True,
                                         stop=True).then_inc(bad_summed, 1)

                    @block.vector
                    def _(dve):
                        chain = Chain(dve, step_p)
                        dve.wait_ge(iotas_made, 4)
                        nc.vector.tensor_scalar(base[:, :], base_i, MIDDLE, None, ALU.add)
                        nc.vector.tensor_scalar(trash[:, :], base_i[:, 0:1], 1.0 / WN, float(SINK), ALU.mult, ALU.add)
                        nc.vector.tensor_copy(first[:, :], base_i)
                        dve.wait_ge(rows_loaded, 16)
                        chain.link(nc.vector.tensor_copy(row_f, row_i))

                        def find_rows(c):
                            for n in range(GC * c, GC * c + GC):
                                chain.link(nc.vector.tensor_scalar(below, row_f, first[:, n:n + 1], 0.0, ALU.is_lt,
                                                                   ALU.add, accum_out=rows_below[:, n:n + 1]))
                            own = slice(GC * c, GC * c + GC)
                            nc.vector.tensor_scalar(row_of[:, own], rows_below[:, own], -1.0, 0.0, ALU.add,
                                                    ALU.max).then_inc(rows_ready, 1)

                        def make_codes(c):
                            src = got[c % 2][:, :, 0:4:2, :]
                            dst = got[c % 2][:, :, 1:4:2, :]
                            dve.wait_ge(gathered[c], 16 * GC)
                            for g in range(GC):
                                n = GC * c + g
                                last = nc.vector.tensor_scalar(rel[:, g, :, :], dst[:, g, :, :], base[:, n:n + 1],
                                                               None, ALU.subtract)
                            chain.link(last)
                            chain.link(nc.vector.tensor_tensor(pen[:, :, :, :], rel[:, :, :, :], rel[:, :, :, :],
                                                               ALU.mult))
                            chain.link(nc.vector.tensor_scalar(pen[:, :, :, :], pen[:, :, :, :], MIDDLE * MIDDLE, FAR,
                                                               ALU.is_gt, ALU.mult))
                            chain.link(nc.vector.scalar_tensor_tensor(rel[:, :, :, :], rel[:, :, :, :], float(P),
                                                                      pen[:, :, :, :], ALU.mult, ALU.add))
                            chain.link(nc.vector.tensor_scalar(low_i, src, 127, None, ALU.bitwise_and))
                            chain.link(nc.vector.scalar_tensor_tensor(rel[:, :, :, :], low_i, -(WN - 1.0),
                                                                      rel[:, :, :, :], ALU.mult, ALU.add))
                            chain.link(nc.vector.scalar_tensor_tensor(rel[:, :, :, :], src, float(WN),
                                                                      rel[:, :, :, :], ALU.mult, ALU.add))
                            nc.vector.tensor_tensor(code[:, c % 2, :, :], rel[:, :, 0, :], rel[:, :, 1, :],
                                                    ALU.min).then_inc(codes_made, 1)
                            dve.wait_ge(codes_made, c + 1)

                        def compare_codes(c):
                            ci = low_i[:, :, 0, :]
                            if c == 0:
                                dve.wait_ge(ones_made, 3)
                            chain.link(nc.vector.tensor_scalar(ci, code[:, c % 2, :, :], 0.0, None, ALU.add))
                            chain.link(nc.vector.tensor_copy(code_16, low_half))
                            if c:
                                dve.wait_ge(same_read, c)
                            for t in range(REACH):
                                last = nc.vector.tensor_tensor(same[:, t, :, 0:P - 1 - t],
                                                               code_16[:, :, 0:P - 1 - t],
                                                               code_16[:, :, t + 1:P], ALU.is_equal)
                            last.then_inc(same_made, 1)

                        def split_codes(c):
                            to = slice(N * c, N * c + N)
                            dve.wait_ge(turned, c + 1)
                            ci = low_i.rearrange("p g r e -> p (g r e)")
                            for h, n in ((0, 4), (1, GC - 4)):
                                last = nc.vector.tensor_scalar(ci[:, 4 * P * h:4 * P * h + n * P],
                                                               ps_key[:, c % 2, h, 0:n * P], MIDDLE * P, None,
                                                               ALU.add)
                            last.then_inc(codes_read, 1)
                            dve.wait_ge(codes_read, c + 1)
                            cj = ci[:, N:2 * N]
                            ci = ci[:, 0:N]
                            chain.link(nc.vector.tensor_scalar(cj, ci, 127, None, ALU.bitwise_and))
                            chain.link(nc.vector.tensor_copy(loT[:, to], cj))
                            chain.link(nc.vector.tensor_scalar(cj, ci, 7, None, ALU.logical_shift_right))
                            nc.vector.tensor_copy(keyT[:, to], cj)
                            chain.link(nc.vector.tensor_scalar(ci, cj, -1 - (P * WN - WN), None, ALU.bitwise_and))
                            if c:
                                dve.wait_ge(masks_read, c)
                            for k in range(WN):
                                last = nc.vector.tensor_scalar(masks[:, k, :], ci, float(k), None, ALU.is_equal)
                            last.then_inc(masks_made, 1)
                            dve.wait_ge(masks_made, c + 1)

                        find_rows(0)
                        nc.vector.tensor_copy(iota_k[:, :], iota_i[:, 0:KEYS])
                        for q in range(LANES):
                            nc.vector.tensor_copy(iota_l[:, :, q], iota_i[:, 0:P])
                        chain.link(nc.vector.tensor_scalar(ident[:, :], tri_i[:, 0:P], 0.0, None, ALU.is_equal))
                        nc.vector.tensor_tensor(stack[:, :], ident[:, 0:F], ident[:, F:2 * F], ALU.add)
                        nc.vector.tensor_scalar(before[:, :], tri_i[:, 0:P], 0.0, None, ALU.is_lt)
                        for q in range(4):
                            for k in range(WN):
                                chain.link(nc.vector.tensor_scalar(select[:, 4 * q + k, :], sel_i[:, 0:P],
                                                                   float(P * q - k), None, ALU.is_equal))
                        for c in range(CHUNKS):
                            if c + 1 < CHUNKS:
                                find_rows(c + 1)
                            make_codes(c)
                            compare_codes(c)
                            split_codes(c)

                        dve.wait_ge(masks_read, CHUNKS)
                        nc.vector.tensor_copy(win_deg[:, :], ps_win[:, 0:GROUPS * WN]).then_inc(win_ready, 1)
                        dve.wait_ge(deg_made, 1)
                        chain.link(nc.vector.tensor_copy(
                            deg[:, :].rearrange("p (g q) -> p q g", q=4),
                            ps_deg[:, 0:P].rearrange("p (q g) -> p q g", q=4)[:, :, 0:GROUPS]))
                        chain.link(nc.vector.tensor_reduce(bad[:, 0:1], deg[:, :], AX, ALU.add))
                        dve.wait_ge(same_read, CHUNKS)
                        chain.link(nc.vector.tensor_reduce(bad[:, 2:3], pairs[:, :], AX, ALU.max))
                        nc.vector.tensor_scalar(bad[:, 1:2], bad[:, 2:3], NEAR - 0.5, None,
                                                ALU.is_gt).then_inc(bad_made, 1)
                        dve.wait_ge(bad_summed, 1)
                        chain.link(nc.vector.tensor_copy(sums[:, 0:2], ps_bad[0:1, 0:2]))
                        chain.link(nc.vector.tensor_scalar(sums[:, 2:3], sums[:, 0:1], float(EDGES), None,
                                                           ALU.not_equal))
                        chain.link(nc.vector.tensor_tensor(sums[:, 3:4], sums[:, 1:2], sums[:, 2:3], ALU.add))
                        chain.link(nc.vector.tensor_copy(flag[:, :], sums[:, 3:4]))

        def general_degrees():
            dst_i = scratch(0, TILES, I32)
            lo_i = scratch(4 * TILES, TILES, I32)
            lo_f = scratch(8 * TILES, TILES, F32)
            hi_f = scratch(12 * TILES, TILES, F32)
            at = 16 * TILES
            hot_lo = scratch(at, 8 * P, F32).bitcast(BF16).rearrange("p (s n) -> p s n", s=16)
            hot_hi = scratch(at + 32 * P, 8 * NBW, F32).bitcast(BF16).rearrange("p (s n) -> p s n", s=16)
            dst_loaded, hot_made, hot_used, step_d = (sem(n) for n in ("dst_loaded", "hot_made", "hot_used", "step_d"))
            with nc.psum_tensor("ps_all", [P, 512], F32) as ps_all:
                with nc.Block() as block:
                    @block.sync
                    def _(sp):
                        sp.dma_start(dst_i, a["dst_grid"]).then_inc(dst_loaded, 16)

                    @block.vector
                    def _(dve):
                        chain = Chain(dve, step_d)
                        dve.wait_ge(dst_loaded, 16)
                        chain.link(nc.vector.tensor_scalar(lo_i, dst_i, 127, None, ALU.bitwise_and))
                        chain.link(nc.vector.tensor_copy(lo_f, lo_i))
                        chain.link(nc.vector.tensor_scalar(lo_i, dst_i, 7, None, ALU.logical_shift_right))
                        chain.link(nc.vector.tensor_copy(hi_f, lo_i))

                        def one_hots(i, begin):
                            for g in range(4):
                                if not begin:
                                    dve.wait_ge(hot_used, 4 * i + g - 3)
                                for s in range(4 * g, 4 * g + 4):
                                    col = 16 * i + s
                                    nc.vector.tensor_scalar(hot_lo[:, s, :], iota_k[:, 0:P],
                                                            lo_f[:, bass.ds(col, 1)], None, ALU.is_equal)
                                    last = nc.vector.tensor_scalar(hot_hi[:, s, :], iota_k[:, 0:NBW],
                                                                   hi_f[:, bass.ds(col, 1)], None, ALU.is_equal)
                                last.then_inc(hot_made, 1)

                        one_hots(0, True)
                        with dve.Fori(1, TILES // 16) as i:
                            one_hots(i, False)
                        dve.wait_ge(hot_used, TILES // 4)
                        nc.vector.tensor_copy(deg[:, :], ps_all[:, 0:NBW])

                    @block.tensor
                    def _(pe):
                        def count(i, begin, end):
                            for g in range(4):
                                pe.wait_ge(hot_made, 4 * i + g + 1)
                                for s in range(4 * g, 4 * g + 4):
                                    mm = nc.tensor.matmul(ps_all[:, 0:NBW], hot_lo[:, s, :], hot_hi[:, s, :],
                                                          start=begin and s == 0, stop=end and s == 15,
                                                          skip_group_check=True)
                                mm.then_inc(hot_used, 1)

                        count(0, True, False)
                        with pe.Fori(1, TILES // 16 - 1) as i:
                            count(i, False, False)
                        count(TILES // 16 - 1, False, True)

        def normalise():
            var_ready, std_ready, step_v = sem("var_ready"), sem("std_ready"), sem("step_v")
            with nc.Block() as block:
                @block.scalar
                def _(act):
                    act.wait_ge(var_ready, 1)
                    nc.scalar.activation(stat[:, 1, :], stat[:, 0, :], ACT.Sqrt).then_inc(std_ready, 1)

                @block.vector
                def _(dve):
                    chain = Chain(dve, step_v)
                    nc.vector.tensor_scalar(stat[:, 0, :], deg[:, 0:NB], 1.0, None, ALU.add).then_inc(var_ready, 1)
                    dve.wait_ge(std_ready, 1)
                    chain.link(nc.vector.reciprocal(dinv[:, :], stat[:, 1, :]))
                    chain.link(nc.vector.tensor_tensor(Hf[:, :, :], X[:, :, :], over(dinv[:, :]), ALU.mult))

        def load_pair(sp, j, b, loaded):
            sp.dma_start(region[:, b, :], counts_dram[bass.ds(j, 1), :, :].rearrange("o p n -> (o p) n")) \
                .then_inc(loaded[b], 16)

        def two_parts(tag, loaded):
            worst, spread, powers, sent, hi_made, low_made, step_t = (
                sem(n + tag) for n in ("worst", "spread", "powers", "sent", "hi", "low", "step_t"))
            cuts = [(UB * 2 * k, UB * 2 * (k + 1)) for k in range(UNITS // 2)]
            with nc.psum_tensor("ps_max" + tag, [P, 512], F32) as ps_max, \
                    nc.psum_tensor("ps_pow" + tag, [P, 512], F32) as ps_pow, \
                    nc.sbuf_tensor("tops" + tag, [P, 1], F32) as tops, \
                    nc.sbuf_tensor("bits" + tag, [1, 5], I32) as bits:
                with nc.Block() as block:
                    if loaded:
                        @block.sync
                        def _(sp):
                            for b in range(3):
                                load_pair(sp, b, b, loaded)

                    @block.tensor
                    def _(pe):
                        pe.wait_ge(worst, 1)
                        nc.tensor.transpose(ps_max[0:1, 0:P], tops[:, :], ident[:, :]).then_inc(spread, 1)
                        pe.wait_ge(powers, 1)
                        nc.tensor.matmul(ps_pow[:, 0:2], ones[0:1, :], bits[:, 3:5].bitcast(F32), start=True,
                                         stop=True).then_inc(sent, 1)

                    @block.scalar
                    def _(act):
                        act.wait_ge(step_t, 5)
                        for lo, up in cuts:
                            nc.scalar.activation(HL[:, lo:up, 0:F], Hf[:, lo:up, :], ACT.Copy,
                                                 scale=scales[:, 0:1]).then_inc(hi_made, 1)

                    @block.vector
                    def _(dve):
                        chain = Chain(dve, step_t)
                        nc.vector.tensor_reduce(tops[:, :], Hf[:, :, :].rearrange("p a b -> p (a b)"), AX, ALU.max,
                                                apply_absolute_value=True).then_inc(worst, 1)
                        dve.wait_ge(spread, 1)
                        chain.link(nc.vector.tensor_reduce(bits[:, 0:1].bitcast(F32), ps_max[0:1, 0:P], AX, ALU.max))
                        chain.link(nc.vector.tensor_scalar(bits[:, 1:2], bits[:, 0:1], 255 * EXP1, None,
                                                           ALU.bitwise_and))
                        chain.link(nc.vector.tensor_scalar(bits[:, 2:3], bits[:, 1:2], 30.0 * EXP1, None, ALU.max))
                        chain.link(nc.vector.tensor_scalar(bits[:, 3:4], bits[:, 2:3], -1.0, 268.0 * EXP1, ALU.mult,
                                                           ALU.add))
                        nc.vector.tensor_scalar(bits[:, 4:5], bits[:, 2:3], -14.0 * EXP1, None,
                                                ALU.add).then_inc(powers, 1)
                        dve.wait_ge(sent, 1)
                        chain.link(nc.vector.tensor_copy(scales[:, :], ps_pow[:, 0:2]))
                        nc.vector.tensor_scalar(merge[:, :], stack[:, :], scales[:, 1:2], None, ALU.mult)
                        for k, (lo, up) in enumerate(cuts):
                            dve.wait_ge(hi_made, k + 1)
                            nc.vector.scalar_tensor_tensor(HL[:, lo:up, F:2 * F], Hf[:, lo:up, :], scales[:, 0:1],
                                                           HL[:, lo:up, 0:F], ALU.mult,
                                                           ALU.subtract).then_inc(low_made, 1)

        def every_pair(eng, body):
            for b in range(3):
                body(b, 0, b)
            with eng.Fori(1, NP // 3) as i:
                for b in range(3):
                    body(3 * i + b, i, b)
            for b in range(NP % 3):
                body(NP // 3 * 3 + b, NP // 3, b)

        def add_pair(j, sums, add):
            mine = Hf[:, bass.ds(2 * j, 2), :]
            got = sums.rearrange("p (a f) -> p a f", f=F)
            if add:
                return nc.vector.tensor_tensor(mine, mine, got, ALU.add)
            return nc.vector.tensor_copy(mine, got)

        def merge_parts(to, sums_t):
            for c in range(2):
                mm = nc.tensor.matmul(to[:, F * c:F * c + F], sums_t[:, P * c:P * c + P], merge[:, :], start=True,
                                      stop=True)
            return mm

        def first_sum():
            RING, HOTS, LAG, GAP = 3, 16, 8, 3
            SLOTS = PW - GAP
            BATCH = 16
            DUOS = PW // 2
            DVE_DUOS = [9, 25]
            BEHIND = 11
            ACT_DUOS = [k for k in range(DUOS) if k not in DVE_DUOS]
            with nc.psum_tensor("ps_cnt", [P, 2 * RING, 512], F32) as ps_cnt, \
                    nc.psum_tensor("ps_out", [P, 512], F32) as ps_out, \
                    nc.psum_tensor("ps_node", [P, 512], F32) as ps_node, \
                    nc.sbuf_tensor("hot_k", [P, HOTS, KEYS], BF16) as hot_k, \
                    nc.sbuf_tensor("hot_l", [P, 2, BATCH // LANES, P, LANES], BF16) as hot_l, \
                    nc.sbuf_tensor("win_lo", [P, PW], F16) as win_lo, \
                    nc.sbuf_tensor("win_key", [P, PW], F32) as win_key, \
                    nc.sbuf_tensor("sums_t", [P, DP], F32) as sums_t:
                cols_copied, hots_made, duos_made = sem("cols_copied"), sem("hots_made"), sem("duos_made")
                act_evicted, dve_evicted = sem("act_evicted"), sem("dve_evicted")
                stored = [sem(f"counts_stored{b}") for b in range(3)]
                summed, copied, merged, added = (
                    sem("pair_" + n) for n in ("summed", "copied", "merged", "added"))

                def duo_in(b, k):
                    r = (DUOS * b + k) % RING
                    return ps_cnt[:, 2 * r:2 * r + 2, 0:KEYS].rearrange("p w (h d) -> p w h d", d=WN)

                def duo_out(b, k):
                    return counts8[b].rearrange("p h (w d) -> p w h d", d=WN)[:, 2 * k:2 * k + 2, :, :]

                def buffer_free(eng, j, i, b):
                    wait_past(eng, stored[b], 16 * i)
                    wait_past(eng, summed, j - 2)

                with nc.Block() as block:
                    @block.sync
                    def _(sp):
                        def store(j, i, b):
                            wait_apart(sp, (act_evicted, len(ACT_DUOS) * (j + 1)),
                                       (dve_evicted, len(DVE_DUOS) * (j + 1)))
                            sp.dma_start(counts_dram[bass.ds(j, 1), :, :].rearrange("o p n -> (o p) n"),
                                         region[:, b, :]).then_inc(stored[b], 16)

                        every_pair(sp, store)
                        for b in range(3):
                            sp.wait_ge(stored[b], 16 * (NP // 3 + (b < NP % 3)))

                    @block.vector
                    def _(dve):
                        def take(j):
                            dve.wait_ge(merged, j + 1)
                            add_pair(j, ps_node[:, 0:2 * F], True).then_inc(added, 1)

                        def evict(j, b, k):
                            wait_apart(dve, (duos_made, DUOS * j + k + 1))
                            nc.vector.tensor_scalar(duo_out(b, k), duo_in(b, k), 1.0, None, ALU.mult,
                                                    saturate=False).then_inc(dve_evicted, 1)

                        def make(j, i, b):
                            early = isinstance(j, int) and j == 0
                            if not early:
                                dve.wait_ge(hots_made, PW * j)
                            nc.vector.tensor_copy(win_lo[:, :], loT[:, bass.ds(PW * j, PW)])
                            nc.vector.tensor_copy(win_key[:, :], keyT[:, bass.ds(PW * j, PW)]) \
                                .then_inc(cols_copied, 1)
                            dve.wait_ge(cols_copied, j + 1)
                            buffer_free(dve, j, i, b)
                            for k in range(PW):
                                if k % 2 == 0 and not (early and k < HOTS):
                                    dve.wait_ge(duos_made, DUOS * j + k // 2 + 1 - HOTS // 2)
                                if k % BATCH == 0:
                                    n = BATCH // LANES
                                    nc.vector.tensor_tensor(
                                        hot_l[:, k // BATCH % 2, :, :, :],
                                        win_lo[:, k:k + BATCH].rearrange("p (a q) -> p a q", q=LANES)
                                        .unsqueeze(2).broadcast_to((P, n, P, LANES)),
                                        iota_l[:, :, :].unsqueeze(1).broadcast_to((P, n, P, LANES)), ALU.is_equal)
                                nc.vector.tensor_scalar(hot_k[:, k % HOTS, :], iota_k[:, :], win_key[:, k:k + 1],
                                                        None, ALU.is_equal).then_inc(hots_made, 1)
                                if k % 2 and (k - BEHIND) // 2 in DVE_DUOS:
                                    evict(j, b, (k - BEHIND) // 2)
                                if k == PW // 2 and not (isinstance(j, int) and j < 2):
                                    take(j - 2)

                        every_pair(dve, make)
                        take(NP - 2)
                        take(NP - 1)

                    @block.scalar
                    def _(act):
                        def copy(j):
                            act.wait_ge(summed, j + 1)
                            wait_past(act, merged, j)
                            nc.scalar.activation(sums_t[:, :], ps_out[:, 0:DP], ACT.Copy).then_inc(copied, 1)

                        def evict(j, i, b):
                            buffer_free(act, j, i, b)
                            for k in ACT_DUOS:
                                if k == LAG // 2 - 1 and not (isinstance(j, int) and j < 2):
                                    copy(j - 2)
                                wait_apart(act, (duos_made, DUOS * j + k + 1))
                                nc.scalar.activation(duo_out(b, k), duo_in(b, k), ACT.Copy,
                                                     saturate=False).then_inc(act_evicted, 1)

                        every_pair(act, evict)
                        copy(NP - 2)
                        copy(NP - 1)

                    @block.tensor
                    def _(pe):
                        def wait_evicted(j, n):
                            k = n % DUOS
                            for duos, evicted in ((ACT_DUOS, act_evicted), (DVE_DUOS, dve_evicted)):
                                if k in duos:
                                    pe.wait_ge(evicted, len(duos) * (j + n // DUOS) + duos.index(k) + 1)

                        def start_sums(j):
                            taken = [] if isinstance(j, int) and j < 1 else [(copied, j)]
                            wait_apart(pe, (act_evicted, len(ACT_DUOS) * (j + 1)),
                                       (dve_evicted, len(DVE_DUOS) * (j + 1)), *taken)

                        def slot(n):
                            return range(NB * n // SLOTS, NB * (n + 1) // SLOTS)

                        def sums(j, b, part):
                            for h in part:
                                mm = nc.tensor.matmul(ps_out[:, 0:DP], HL[:, h, :], counts8[b][:, h, :],
                                                      start=h == 0, stop=h == NB - 1, skip_group_check=True)
                                if h == NB - 1:
                                    mm.then_inc(summed, 1)

                        def turn(j):
                            pe.wait_ge(copied, j + 1)
                            wait_past(pe, added, j)
                            merge_parts(ps_node, sums_t).then_inc(merged, 1)

                        def make(j, i, b):
                            early = isinstance(j, int) and j == 0
                            for k in range(PW):
                                n = k // 2
                                if k % 2 == 0 and not (early and n < RING):
                                    wait_evicted(j, n - RING)
                                pe.wait_ge(hots_made, PW * j + k + 1)
                                mm = nc.tensor.matmul(
                                    ps_cnt[:, 2 * ((DUOS * b + n) % RING) + k % 2, 0:KEYS],
                                    hot_l[:, k // BATCH % 2, k % BATCH // LANES, :, k % LANES],
                                    hot_k[:, k % HOTS, :], start=True, stop=True)
                                if k % 2:
                                    mm.then_inc(duos_made, 1)
                                if k == LAG and not early:
                                    start_sums(j - 1)
                                if k >= LAG and not early:
                                    sums(j - 1, (b - 1) % 3, slot(k - LAG))
                                if k < LAG - GAP and not (isinstance(j, int) and j < 2):
                                    sums(j - 2, (b - 2) % 3, slot(k + PW - LAG))
                                if k == LAG + 8 and not (isinstance(j, int) and j < 2):
                                    turn(j - 2)

                        every_pair(pe, make)
                        sums(NP - 2, (NP - 2) % 3, range(NB * (PW - LAG) // SLOTS, NB))
                        start_sums(NP - 1)
                        turn(NP - 2)
                        sums(NP - 1, (NP - 1) % 3, range(NB))
                        turn(NP - 1)

        def later_sum(tag, add, loaded):
            with nc.psum_tensor("ps_sum" + tag, [P, 3, 512], F32) as ps_sum, \
                    nc.psum_tensor("ps_node" + tag, [P, 3, 512], F32) as ps_node, \
                    nc.sbuf_tensor("sums_t" + tag, [P, 3, DP], F32) as sums_t:
                summed, copied, merged, added = (
                    sem("pair_" + n + tag) for n in ("summed", "copied", "merged", "added"))

                with nc.Block() as block:
                    @block.sync
                    def _(sp):
                        def load(j, i, b):
                            if not isinstance(j, int) or j >= 3:
                                wait_apart(sp, (summed, j - 2))
                                load_pair(sp, j, b, loaded)

                        every_pair(sp, load)

                    @block.tensor
                    def _(pe):
                        def turn(j, b):
                            pe.wait_ge(copied, j + 1)
                            wait_past(pe, added, j - 2)
                            merge_parts(ps_node[:, b, :], sums_t[:, b, :]).then_inc(merged, 1)

                        def sums(j, i, b):
                            if isinstance(j, int) and j < 3:
                                pe.wait_ge(loaded[b], 16)
                            else:
                                wait_apart(pe, (loaded[b], 16 * (i + 1)), (copied, j - 2))
                            for h in range(NB):
                                mm = nc.tensor.matmul(ps_sum[:, b, 0:DP], HL[:, h, :], counts8[b][:, h, :],
                                                      start=h == 0, stop=h == NB - 1)
                            mm.then_inc(summed, 1)
                            if not isinstance(j, int) or j > 0:
                                turn(j - 1, (b - 1) % 3)

                        every_pair(pe, sums)
                        turn(NP - 1, (NP - 1) % 3)

                    @block.scalar
                    def _(act):
                        def copy(j, i, b):
                            act.wait_ge(summed, j + 1)
                            wait_past(act, merged, j - 2)
                            nc.scalar.activation(sums_t[:, b, :], ps_sum[:, b, 0:DP], ACT.Copy).then_inc(copied, 1)

                        every_pair(act, copy)

                    @block.vector
                    def _(dve):
                        def take(j, i, b):
                            dve.wait_ge(merged, j + 1)
                            add_pair(j, ps_node[:, b, 0:2 * F], add).then_inc(added, 1)

                        every_pair(dve, take)

        def general_sum(tag, add):
            src_i = scratch(0, TILES, I32)
            own = []

            def sem(name):
                own.append(nc.alloc_semaphore(name=name))
                return own[-1]

            dst_i = scratch(4 * TILES, TILES, I32)
            sum_thirds = sum_dram.rearrange("(c p n) f -> c p (n f)", c=3, p=P)
            zero = scratch(8 * TILES, SUMROWS // 3 // P * F, F32)
            with nc.psum_tensor("ps_dst" + tag, [P, 512], F32) as ps_dst, \
                    nc.psum_tensor("ps_rows" + tag, [P, 512], F32) as ps_rows, \
                    nc.sbuf_tensor("rows_in" + tag, [P, F], F32) as rows_in, \
                    nc.sbuf_tensor("rows_out" + tag, [P, F], F32) as rows_out, \
                    nc.sbuf_tensor("diag" + tag, [P, P], F32) as diag, \
                    nc.sbuf_tensor("same" + tag, [P, P], F32) as same, \
                    nc.sbuf_tensor("earlier" + tag, [P, P], F32) as earlier, \
                    nc.sbuf_tensor("cols" + tag, [P, 5], F32) as cols, \
                    nc.sbuf_tensor("src_col" + tag, [P, 1], U32) as src_col, \
                    nc.sbuf_tensor("to_col" + tag, [P, 1], U32) as to_col:
                tables_ready, zero_made = sem("tables_ready" + tag), sem("zero_made" + tag)
                gathered, scattered = sem("rows_gathered" + tag), sem("rows_scattered" + tag)
                src_ready, diag_ready, dst_spread = (sem(n + tag) for n in ("src_ready", "diag_ready", "dst_spread"))
                same_ready, to_ready, summed = (sem(n + tag) for n in ("same_ready", "to_ready", "summed"))
                rows_ready, step_g = sem("rows_ready" + tag), sem("step_g" + tag)
                with nc.Block() as block:
                    @block.sync
                    def _(sp):
                        sp.dma_start(src_i, a["src_grid"]).then_inc(tables_ready, 16)
                        sp.dma_start(dst_i, a["dst_grid"]).then_inc(tables_ready, 16)
                        sp.dma_start(feat_blocks, Hf[:, :, :]).then_inc(tables_ready, 16)
                        sp.wait_ge(zero_made, 1)
                        for c in range(3):
                            sp.dma_start(sum_thirds[c], zero).then_inc(tables_ready, 16)
                        sp.wait_ge(tables_ready, 16 * 6)

                    @block.vector
                    def _(dve):
                        nc.vector.memset(zero, 0.0).then_inc(zero_made, 1)

                with nc.Block() as block:
                    @block.vector
                    def _(dve):
                        def tile(t):
                            chain = Chain(dve, step_g, 6 * t)
                            dve.wait_ge(gathered, 16 * t)
                            dve.wait_ge(scattered, 16 * t)
                            dve.wait_ge(summed, t)
                            nc.vector.tensor_copy(src_col[:, :].bitcast(I32), src_i[:, bass.ds(t, 1)]) \
                                .then_inc(src_ready, 1)
                            chain.link(nc.vector.tensor_copy(cols[:, 0:1], dst_i[:, bass.ds(t, 1)]))
                            nc.vector.tensor_scalar(diag[:, :], ident[:, :], cols[:, 0:1], None,
                                                    ALU.mult).then_inc(diag_ready, 1)
                            dve.wait_ge(dst_spread, t + 1)
                            nc.vector.tensor_scalar(same[:, :], ps_dst[:, 0:P], cols[:, 0:1], None,
                                                    ALU.is_equal).then_inc(same_ready, 1)
                            dve.wait_ge(same_ready, t + 1)
                            chain.link(nc.vector.tensor_tensor(earlier[:, :], same[:, :], before[:, :], ALU.mult))
                            chain.link(nc.vector.tensor_reduce(cols[:, 1:2], earlier[:, :], AX, ALU.max))
                            chain.link(nc.vector.tensor_tensor(cols[:, 2:3], trash[:, :], cols[:, 0:1], ALU.subtract))
                            chain.link(nc.vector.tensor_tensor(cols[:, 3:4], cols[:, 2:3], cols[:, 1:2], ALU.mult))
                            chain.link(nc.vector.tensor_tensor(cols[:, 4:5], cols[:, 3:4], cols[:, 0:1], ALU.add))
                            nc.vector.tensor_copy(to_col[:, :], cols[:, 4:5]).then_inc(to_ready, 1)
                            assert chain.n == 6

                        tile(0)
                        with dve.Fori(1, TILES) as t:
                            tile(t)

                    @block.gpsimd
                    def _(pool):
                        def tile(t):
                            wait_apart(pool, (src_ready, t + 1), (summed, t))
                            nc.gpsimd.indirect_dma_start(
                                out=rows_in[:, :], out_offset=None, in_=feat_dram,
                                in_offset=bass.IndirectOffsetOnAxis(ap=src_col[:, :], axis=0)).then_inc(gathered, 16)
                            wait_apart(pool, (rows_ready, t + 1), (to_ready, t + 1), (scattered, 16 * t))
                            nc.gpsimd.indirect_dma_start(
                                out=sum_dram, out_offset=bass.IndirectOffsetOnAxis(ap=to_col[:, :], axis=0),
                                in_=rows_out[:, :], in_offset=None, compute_op=ALU.add).then_inc(scattered, 16)

                        tile(0)
                        with pool.Fori(1, TILES) as t:
                            tile(t)
                        pool.wait_ge(scattered, 16 * TILES)

                    @block.tensor
                    def _(pe):
                        def tile(t):
                            pe.wait_ge(diag_ready, t + 1)
                            nc.tensor.matmul(ps_dst[:, 0:P], ones[:, :], diag[:, :], start=True,
                                             stop=True).then_inc(dst_spread, 1)
                            pe.wait_ge(same_ready, t + 1)
                            pe.wait_ge(gathered, 16 * (t + 1))
                            pe.wait_ge(rows_ready, t)
                            nc.tensor.matmul(ps_rows[:, 0:F], same[:, :], rows_in[:, :], start=True,
                                             stop=True).then_inc(summed, 1)

                        tile(0)
                        with pe.Fori(1, TILES) as t:
                            tile(t)

                    @block.scalar
                    def _(act):
                        def tile(t):
                            act.wait_ge(summed, t + 1)
                            act.wait_ge(scattered, 16 * t)
                            nc.scalar.activation(rows_out[:, :], ps_rows[:, 0:F], ACT.Copy).then_inc(rows_ready, 1)

                        tile(0)
                        with act.Fori(1, TILES) as t:
                            tile(t)

                fetched, totalled = sem("fetched" + tag), sem("totalled" + tag)
                got = scratch(0, NB * F, F32).rearrange("p (j f) -> p j f", f=F)
                with nc.Block() as block:
                    @block.sync
                    def _(sp):
                        sp.dma_start(got if add else Hf[:, :, :], sum_blocks).then_inc(fetched, 16)
                        sp.wait_ge(fetched, 16)

                    @block.vector
                    def _(dve):
                        if add:
                            dve.wait_ge(fetched, 16)
                            nc.vector.tensor_tensor(Hf[:, :, :], Hf[:, :, :], got, ALU.add).then_inc(totalled, 1)

            nc.clear_and_free_semaphores(own)
            nc.all_engine_barrier()

        def gcn_dense():
            with nc.psum_tensor("ps_t", [P, 2, 512], F32) as ps_t, \
                    nc.psum_tensor("ps_h", [P, 2, 2, 512], F32) as ps_h, \
                    nc.psum_tensor("ps_f", [P, 512], F32) as ps_f:
                bufs = [share((P, UB, F), (F, UN), (P, 2, UN), (P, 2, UN), (P, 2, UN), start=c * GCN_BYTES)
                        for c in range(2)]
                agg, agg_t, neg, lin, hid = zip(*bufs)
                scaled, turned, copied, hidden = sem("d_scaled"), sem("d_turned"), sem("d_copied"), sem("d_hidden")
                neg_made, exp_made, lin_made = sem("neg_made"), sem("exp_made"), sem("lin_made")
                elu_made, fused, out_made = sem("elu_made"), sem("fused"), sem("fused_out")
                halves = ((0, 512), (512, UN))

                with nc.Block() as block:
                    @block.gpsimd
                    def _(pool):
                        def scale(u, c):
                            wait_past(pool, turned, u - 1)
                            nc.gpsimd.tensor_tensor(agg[c], Hf[:, bass.ds(UB * u, UB), :],
                                                    over(dinv[:, bass.ds(UB * u, UB)]),
                                                    ALU.mult).then_inc(scaled, 1)

                        stagger(pool, [(0, scale)], UNITS)

                    @block.vector
                    def _(dve):
                        def negative(u, c):
                            wait_past(dve, elu_made, 2 * u - 2)
                            for m in range(2):
                                dve.wait_ge(lin_made, 2 * u + m + 1)
                                nc.vector.tensor_scalar(neg[c][:, m, :], lin[c][:, m, :], 0.0, None,
                                                        ALU.min).then_inc(neg_made, 1)

                        def elu(u, c):
                            wait_past(dve, fused, u - 1)
                            for m in range(2):
                                dve.wait_ge(exp_made, 2 * u + m + 1)
                                nc.vector.scalar_tensor_tensor(hid[c][:, m, :], neg[c][:, m, :], -1.0,
                                                               lin[c][:, m, :], ALU.add,
                                                               ALU.max).then_inc(elu_made, 1)

                        def leave(u, c):
                            dve.wait_ge(fused, u + 1)
                            nc.vector.tensor_tensor(Hf[:, bass.ds(UB * u, UB), :],
                                                    ps_f[:, 0:UB * F].rearrange("p (j f) -> p j f", f=F),
                                                    over(dinv[:, bass.ds(UB * u, UB)]),
                                                    ALU.mult).then_inc(out_made, 1)

                        stagger(dve, [(3, elu), (4, leave), (2, negative)], UNITS)

                    @block.tensor
                    def _(pe):
                        def turn(u, c):
                            wait_apart(pe, (scaled, u + 1), *([(copied, u)] if not isinstance(u, int) or u else []))
                            for k in range(UB):
                                mm = nc.tensor.transpose(ps_t[0:F, k // 4, k % 4 * P:k % 4 * P + P], agg[c][:, k, :],
                                                         ident[:, :])
                            mm.then_inc(turned, 1)

                        def hide(u, c):
                            pe.wait_ge(copied, u + 1)
                            for m in range(2):
                                wait_past(pe, lin_made, 2 * u - 1 + m)
                                for h, (lo, up) in enumerate(halves):
                                    mm = nc.tensor.matmul(ps_h[:, m, h, 0:up - lo], w_gcn[:, m * H:(m + 1) * H],
                                                          agg_t[c][:, lo:up], start=True, stop=True)
                                mm.then_inc(hidden, 1)

                        def fuse(u, c):
                            pe.wait_ge(elu_made, 2 * u + 2)
                            wait_past(pe, out_made, u)
                            for k in range(UB):
                                for m in range(2):
                                    mm = nc.tensor.matmul(ps_f[:, F * k:F * k + F], hid[c][:, m, P * k:P * k + P],
                                                          w_fuse[:, m, :], start=m == 0, stop=m == 1)
                            mm.then_inc(fused, 1)

                        stagger(pe, [(4, fuse), (0, turn), (1, hide)], UNITS)

                    @block.scalar
                    def _(act):
                        def copy(u, c):
                            act.wait_ge(turned, u + 1)
                            wait_past(act, hidden, 2 * u - 2)
                            nc.scalar.activation(agg_t[c], ps_t[0:F, :, :].rearrange("p a b -> p (a b)")[:, 0:UN],
                                                 ACT.Copy).then_inc(copied, 1)

                        def linear(u, c):
                            wait_past(act, elu_made, 2 * u - 2)
                            for m in range(2):
                                act.wait_ge(hidden, 2 * u + m + 1)
                                nc.scalar.activation(
                                    lin[c][:, m, :], ps_h[:, m, :, :].rearrange("p a b -> p (a b)")[:, 0:UN],
                                    ACT.Identity, bias=b_gcn[:, m:m + 1]).then_inc(lin_made, 1)

                        def exp(u, c):
                            for m in range(2):
                                act.wait_ge(neg_made, 2 * u + m + 1)
                                nc.scalar.activation(neg[c][:, m, :], neg[c][:, m, :], ACT.Exp).then_inc(exp_made, 1)

                        stagger(act, [(1, copy), (3, exp), (2, linear)], UNITS)

        cuts = [(2 * UB * k, 2 * UB * (k + 1)) for k in range(UNITS // 2)]

        def softmax_residual():
            exped, shifted, added, normed, step_s = (sem(n) for n in ("exped", "shifted", "added", "normed", "step_s"))
            with nc.Block() as block:
                @block.vector
                def _(dve):
                    chain = Chain(dve, step_s)
                    for lo, up in cuts:
                        part = Hf[:, lo:up, :]
                        chain.link(nc.vector.tensor_tensor(part, part, over(dinv[:, lo:up]), ALU.mult))
                        chain.link(nc.vector.tensor_tensor(
                            part, part, each(b_fuse, up - lo), ALU.add))
                        chain.link(nc.vector.tensor_reduce(stat[:, 0, lo:up], part, AX, ALU.max))
                        nc.vector.tensor_tensor(part, part, over(stat[:, 0, lo:up]), ALU.subtract).then_inc(shifted, 1)
                    for k, (lo, up) in enumerate(cuts):
                        part = Hf[:, lo:up, :]
                        dve.wait_ge(exped, k + 1)
                        chain.link(nc.vector.tensor_reduce(stat[:, 1, lo:up], part, AX, ALU.add))
                        chain.link(nc.vector.reciprocal(stat[:, 2, lo:up], stat[:, 1, lo:up]))
                        nc.vector.tensor_tensor(part, part, over(stat[:, 2, lo:up]), ALU.mult).then_inc(normed, 1)

                @block.scalar
                def _(act):
                    for k, (lo, up) in enumerate(cuts):
                        act.wait_ge(shifted, k + 1)
                        nc.scalar.activation(Hf[:, lo:up, :], Hf[:, lo:up, :], ACT.Exp).then_inc(exped, 1)

                @block.gpsimd
                def _(pool):
                    for k, (lo, up) in enumerate(cuts):
                        pool.wait_ge(normed, k + 1)
                        nc.gpsimd.tensor_tensor(X[:, lo:up, :], X[:, lo:up, :], Hf[:, lo:up, :],
                                                ALU.add).then_inc(added, 1)

        def layer_norm(tag, store):
            centred, squared, var_made, std_made, step_n = (
                sem(n + tag) for n in ("centred", "squared", "var_made", "std_made", "step_n"))
            finished, stored = sem("finished" + tag), sem("result_stored" + tag)
            square = scratch(0, NB * F, F32).rearrange("p (j f) -> p j f", f=F)
            with nc.Block() as block:
                @block.vector
                def _(dve):
                    chain = Chain(dve, step_n)
                    for lo, up in cuts:
                        part = X[:, lo:up, :]
                        chain.link(nc.vector.tensor_reduce(stat[:, 0, lo:up], part, AX, ALU.add))
                        chain.link(nc.vector.tensor_scalar(stat[:, 0, lo:up], stat[:, 0, lo:up], 1.0 / F, None,
                                                           ALU.mult))
                        nc.vector.tensor_tensor(part, part, over(stat[:, 0, lo:up]), ALU.subtract).then_inc(centred, 1)
                    for k, (lo, up) in enumerate(cuts):
                        dve.wait_ge(squared, k + 1)
                        last = nc.vector.tensor_reduce(stat[:, 1, lo:up], square[:, lo:up, :], AX, ALU.add)
                    chain.link(last)
                    nc.vector.tensor_scalar(stat[:, 1, :], stat[:, 1, :], 1.0 / F, EPS, ALU.mult,
                                            ALU.add).then_inc(var_made, 1)
                    dve.wait_ge(std_made, 1)
                    chain.link(nc.vector.reciprocal(stat[:, 0, :], stat[:, 2, :]))
                    for lo, up in cuts:
                        nc.vector.tensor_tensor(X[:, lo:up, :], X[:, lo:up, :], over(stat[:, 0, lo:up]),
                                                ALU.mult).then_inc(finished, 1)

                @block.scalar
                def _(act):
                    for k, (lo, up) in enumerate(cuts):
                        act.wait_ge(centred, k + 1)
                        nc.scalar.activation(square[:, lo:up, :], X[:, lo:up, :], ACT.Square).then_inc(squared, 1)
                    act.wait_ge(var_made, 1)
                    nc.scalar.activation(stat[:, 2, :], stat[:, 1, :], ACT.Sqrt).then_inc(std_made, 1)

                if store:
                    full = out[0:(NB - 1) * P, :].rearrange("(j p) f -> p j f", p=P)

                    @block.sync
                    def _(sp):
                        for k, (lo, up) in enumerate(cuts):
                            sp.wait_ge(finished, k + 1)
                            up = min(up, NB - 1)
                            sp.dma_start(full[:, lo:up, :], X[:, lo:up, :]).then_inc(stored, 16)
                        sp.dma_start(out[(NB - 1) * P:NODES, :], X[0:LAST, NB - 1, :]).then_inc(stored, 16)
                        sp.wait_ge(stored, 16 * (len(cuts) + 1))

        def mlp(tag, width, w1, w2, w3, hb, b3, residual):
            with nc.psum_tensor("ps_t" + tag, [P, 2, 512], F32) as ps_t, \
                    nc.psum_tensor("ps_1" + tag, [P, 2, 512], F32) as ps_1, \
                    nc.psum_tensor("ps_2" + tag, [P, 2, 512], F32) as ps_2, \
                    nc.psum_tensor("ps_3" + tag, [P, 512], F32) as ps_3:
                bufs = [share((P, UB, width), (width, UN), (P, UN), (P, UN), (P, UB, F), start=c * MLP_BYTES)
                        for c in range(2)]
                into, into_t, hid_1, hid_2, res = zip(*bufs)
                taken, turned, copied = (sem(n + tag) for n in ("m_taken", "m_turned", "m_copied"))
                one, one_act, two, two_act = (sem(n + tag) for n in ("m_one", "m_one_act", "m_two", "m_two_act"))
                three, biased, out_made = (sem(n + tag) for n in ("m_three", "m_biased", "m_out"))
                halves = ((0, 512), (512, UN))

                def layer(ps, w, src):
                    for c, (lo, up) in enumerate(halves):
                        mm = nc.tensor.matmul(ps[:, c, 0:up - lo], w[:, :], src[:, lo:up], start=True, stop=True)
                    return mm

                def whole(ps, rows=P):
                    return ps[0:rows, :, :].rearrange("p a b -> p (a b)")[:, 0:UN]

                with nc.Block() as block:
                    @block.gpsimd
                    def _(pool):
                        def take(u, c):
                            wait_past(pool, turned, u - 1)
                            if width == 2 * F:
                                nc.gpsimd.tensor_copy(into[c][:, :, F:2 * F], Hf[:, bass.ds(UB * u, UB), :])
                            nc.gpsimd.tensor_copy(into[c][:, :, 0:F], X[:, bass.ds(UB * u, UB), :]).then_inc(taken, 1)

                        stagger(pool, [(0, take)], UNITS)

                    @block.tensor
                    def _(pe):
                        def turn(u, c):
                            wait_apart(pe, (taken, u + 1), *([(copied, u)] if not isinstance(u, int) or u else []))
                            for k in range(UB):
                                mm = nc.tensor.transpose(ps_t[0:width, k // 4, k % 4 * P:k % 4 * P + P],
                                                         into[c][:, k, :], ident[:, :])
                            mm.then_inc(turned, 1)

                        def first(u, c):
                            pe.wait_ge(copied, u + 1)
                            wait_past(pe, one_act, u)
                            layer(ps_1, w1, into_t[c]).then_inc(one, 1)

                        def second(u, c):
                            pe.wait_ge(one_act, u + 1)
                            wait_past(pe, two_act, u)
                            layer(ps_2, w2, hid_1[c]).then_inc(two, 1)

                        def third(u, c):
                            pe.wait_ge(two_act, u + 1)
                            wait_past(pe, biased, u)
                            for k in range(UB):
                                mm = nc.tensor.matmul(ps_3[:, F * k:F * k + F], hid_2[c][:, P * k:P * k + P], w3[:, :],
                                                      start=True, stop=True)
                            mm.then_inc(three, 1)

                        stagger(pe, [(4, third), (0, turn), (2, second), (1, first)], UNITS)

                    @block.scalar
                    def _(act):
                        def copy(u, c):
                            act.wait_ge(turned, u + 1)
                            wait_past(act, one, u - 1)
                            nc.scalar.activation(into_t[c], whole(ps_t, width), ACT.Copy).then_inc(copied, 1)

                        def relu(u, c):
                            act.wait_ge(one, u + 1)
                            wait_past(act, two, u - 1)
                            nc.scalar.activation(hid_1[c], whole(ps_1), ACT.Relu,
                                                 bias=b_hid[:, hb:hb + 1]).then_inc(one_act, 1)

                        stagger(act, [(1, copy), (2, relu)], UNITS)

                    @block.vector
                    def _(dve):
                        def relu(u, c):
                            dve.wait_ge(two, u + 1)
                            wait_past(dve, three, u - 1)
                            nc.vector.tensor_scalar(hid_2[c], whole(ps_2), b_hid[:, hb + 1:hb + 2], 0.0, ALU.add,
                                                    ALU.max).then_inc(two_act, 1)

                        def leave(u, c):
                            dve.wait_ge(three, u + 1)
                            if residual:
                                wait_past(dve, out_made, u - 1)
                            mine = (X if residual else Hf)[:, bass.ds(UB * u, UB), :]
                            to = res[c] if residual else mine
                            nc.vector.tensor_tensor(to, ps_3[:, 0:UB * F].rearrange("p (j f) -> p j f", f=F),
                                                    each(b3, UB), ALU.add).then_inc(biased, 1)
                            if residual:
                                dve.wait_ge(biased, u + 1)
                                nc.vector.tensor_tensor(mine, mine, res[c], ALU.add).then_inc(out_made, 1)

                        stagger(dve, [(3, relu), (4, leave)], UNITS)

        prepare()
        general = nc.alloc_registers("general")
        nc.regs_load(general, flag[0:1, 0:1])
        with nc.If_ne(general, 0):
            nc.all_engine_barrier()
            general_degrees()
        normalise()
        with nc.If_ne(general, 0):
            nc.all_engine_barrier()
            general_sum("_g1", True)
        with nc.Else():
            nc.all_engine_barrier()
            two_parts("_1", None)
            first_sum()
        gcn_dense()
        with nc.If_ne(general, 0):
            nc.all_engine_barrier()
            general_sum("_g2", True)
        with nc.Else():
            nc.all_engine_barrier()
            loaded = [sem(f"counts_loaded{b}_2") for b in range(3)]
            two_parts("_2", loaded)
            later_sum("_2", True, loaded)
        softmax_residual()
        layer_norm("_1", False)
        mlp("_m", F, wm1, wm2, wm3, 0, b_m3, False)
        with nc.If_ne(general, 0):
            nc.all_engine_barrier()
            general_sum("_g3", False)
        with nc.Else():
            nc.all_engine_barrier()
            loaded = [sem(f"counts_loaded{b}_3") for b in range(3)]
            two_parts("_3", loaded)
            later_sum("_3", False, loaded)
        mlp("_u", 2 * F, wu1, wu2, wu3, 2, b_u3, True)
        layer_norm("_2", True)


WEIGHTS = ["L0_gnn_W_nuc", "L0_gnn_b_nuc", "L0_gnn_W_surf", "L0_gnn_b_surf", "L0_gnn_W_fuse", "L0_gnn_b_fuse",
           "L1_gnn_WM1", "L1_gnn_bM1", "L1_gnn_WM2", "L1_gnn_bM2", "L1_gnn_WM3", "L1_gnn_bM3",
           "L1_gnn_WU1", "L1_gnn_bU1", "L1_gnn_WU2", "L1_gnn_bU2", "L1_gnn_WU3", "L1_gnn_bU3"]


def kernel(**inputs):
    import numpy as np
    import concourse.bacc as bacc
    from concourse.bass_utils import run_bass_kernel_spmd

    x, src, dst = (np.asarray(inputs[n]) for n in ("x", "src", "dst"))
    edges = TILES * P
    src_pad = (np.arange(edges + P) % NODES).astype(src.dtype)
    dst_pad = np.full(edges + P, PAD_DST, dst.dtype)
    src_pad[:EDGES], dst_pad[:EDGES] = src, dst
    rows = np.stack([src_pad.reshape(-1, P), dst_pad.reshape(-1, P)], axis=1)
    x_blocks = np.zeros((NB * P, F), x.dtype)
    x_blocks[:NODES] = x
    arrays = {
        "x_blocks": x_blocks,
        "src_grid": np.ascontiguousarray(src_pad[:edges].reshape(P, TILES)),
        "dst_grid": np.ascontiguousarray(dst_pad[:edges].reshape(P, TILES)),
        "row_first": np.ascontiguousarray(dst_pad[:edges:P]),
        "edge_rows": np.ascontiguousarray(np.concatenate([rows[:-1], rows[1:]], axis=1).reshape(TILES, 4 * P)),
    }
    for name in WEIGHTS:
        arrays[name.split("gnn_")[1]] = np.ascontiguousarray(inputs[name])
    nc = bacc.Bacc("TRN2", target_bir_lowering=False, num_devices=1)
    aps = {n: nc.dram_tensor(n + "_in", v.shape, mybir.dt.from_np(v.dtype), kind="ExternalInput").ap()
           for n, v in arrays.items()}
    out = nc.dram_tensor("out_dram", (NODES, F), F32, kind="ExternalOutput").ap()
    build(nc, aps, out)
    r = run_bass_kernel_spmd(nc, [{n + "_in": v for n, v in arrays.items()}], core_ids=[0])
    return r.results[0]["out_dram"]
```

```python
from contextlib import ExitStack

import concourse.bass as bass
from concourse import mybir

ALU = mybir.AluOpType
ACT = mybir.ActivationFunctionType
F32 = mybir.dt.float32
F16 = mybir.dt.float16
BF16 = mybir.dt.bfloat16
F8 = mybir.dt.float8e4
I32 = mybir.dt.int32
U32 = mybir.dt.uint32
U8 = mybir.dt.uint8
AX = mybir.AxisListType.X

P = 128
NODES = 12500
EDGES = 212500
F = 64
H = 128
NB = -(-NODES // P)
LAST = NODES - (NB - 1) * P
TILES = 1664
WN = 4
WB = P // WN
NBW = -(-NB // 4) * 4
GROUPS = NBW * WB // P
GC = 5
KEYS = NB * WN
PAD_DST = 16383
SINK = PAD_DST + 1
SUMROWS = SINK + P
DP = 2 * P
NP = NB // 2
PW = 2 * WB
MAXCOUNT = 16
REACH = 12
NEAR = MAXCOUNT - (P - 1 - MAXCOUNT) // REACH
EXP1 = 1 << 23
FAR = float(1 << 22)
MIDDLE = (WN - 1) / 2
UB = 7
UNITS = NB // UB
UN = UB * P
EVEN = (UB + 1) // 2
MLP_BYTES = 4 * (UB * F + 4 * UN + 4 * UB)
GCN_BYTES = 4 * (2 * EVEN * F + EVEN * P + 6 * UN)
EPS = 1e-5


class Chain:

    def __init__(self, eng, sem, base=0):
        self.eng, self.sem, self.base, self.n = eng, sem, base, 0

    def link(self, ins):
        self.n += 1
        ins.then_inc(self.sem, 1)
        self.eng.wait_ge(self.sem, self.base + self.n)


def stagger(eng, stages, count):
    depth = max(k for k, _ in stages)
    early = (depth + 3) // 2 * 2

    def step(s, odd, low, high):
        for k, body in stages:
            if low <= k <= high:
                body(s - k, (odd - k) % 2)

    for s in range(early):
        step(s, s % 2, 0, s)
    with eng.Fori(early // 2, count // 2) as i:
        for odd in range(2):
            step(2 * i + odd, odd, 0, depth)
    for s in range(count, count + depth):
        step(s, s % 2, s - count + 1, depth)


def wait_apart(eng, *waits):
    for _, value in waits:
        eng.compute_val(value)
    eng.wait_ge(waits[0][0], 1)
    for sem, value in waits:
        eng.wait_ge(sem, value)


def wait_past(eng, sem, value):
    if not (isinstance(value, int) and value < 1):
        eng.wait_ge(sem, value)


def place(k):
    return P * (k // 2 + k % 2 * EVEN)


def over(col):
    return col.unsqueeze(2).broadcast_to((P, col.shape[1], F))


def each(row, blocks):
    return row[:, :].unsqueeze(1).broadcast_to((P, blocks, F))


def build(nc, a, out):
    with ExitStack() as ctx:
        def sb(name, shape, dt):
            return ctx.enter_context(nc.sbuf_tensor(name, shape, dt))

        def sem(name):
            return ctx.enter_context(nc.semaphore(name))

        counts_dram = nc.dram_tensor("counts_dram", (NP, P, NB * DP), U8).ap()
        feat_dram = nc.dram_tensor("feat_dram", (NB * P, F), F32).ap()
        sum_dram = nc.dram_tensor("sum_dram", (SUMROWS, F), F32).ap()

        X = sb("X", [P, NB, F], F32)
        Hf = sb("Hf", [P, NB, F], F32)
        HL = sb("HL", [P, NB, 2 * F], F16)
        region = sb("region", [P, 3, NB * DP], U8)
        keyT = sb("keyT", [P, GROUPS * P], F32)
        loT = sb("loT", [P, GROUPS * P], F16)
        deg = sb("deg", [P, NBW], F32)
        dinv = sb("dinv", [P, NB], F32)
        stat = sb("stat", [P, 3, NB], F32)
        ident = sb("ident", [P, P], F32)
        ones = sb("ones", [P, P], F32)
        iota_k = sb("iota_k", [P, KEYS], F16)
        stack = sb("stack", [P, F], F32)
        scales = sb("scales", [P, 2], F32)
        tops = sb("tops", [P, UNITS], F32)
        soft = sb("soft", [P, 3, 2, F], F32)
        soft_sums = sb("soft_sums", [P, 3, 4, 2], F32)
        merge = sb("merge", [P, F], F32)
        flag = sb("flag", [1, 1], I32)
        w_fuse = sb("w_fuse", [P, 2, F], F32)
        w_gcn = sb("w_gcn", [P, 2, 2 * H], F32)
        b_gcn = sb("b_gcn", [P, 2], F32)
        b_fuse = sb("b_fuse", [P, F], F32)
        wm1 = sb("wm1", [P, 2, H], F32)
        wm2 = sb("wm2", [H, H], F32)
        wm3 = sb("wm3", [H, F], F32)
        wu1 = sb("wu1", [2 * F, H], F32)
        wu2 = sb("wu2", [H, H], F32)
        wu3 = sb("wu3", [H, F], F32)
        b_hid = sb("b_hid", [P, 4], F32)
        b_m3 = sb("b_m3", [P, F], F32)
        b_u3 = sb("b_u3", [P, F], F32)

        counts8 = [region[:, b, :].bitcast(F8).rearrange("p (h d) -> p h d", d=DP) for b in range(3)]
        flat = region[:, :, :].rearrange("p a b -> p (a b)")

        def scratch(at, n, dt):
            return flat[:, at:at + 4 * n].bitcast(dt)

        def share(*shapes, start=0):
            at, views = start, []
            for rows, *dims in shapes:
                n = 1
                for d in dims:
                    n *= d
                view = scratch(at, n, F32)[0:rows, :]
                if len(dims) == 2:
                    view = view.rearrange("p (a b) -> p a b", b=dims[1])
                views.append(view)
                at += 4 * n
            return views

        x_blocks = a["x_blocks"].rearrange("(j p) f -> p j f", p=P)
        feat_blocks = feat_dram.rearrange("(j p) f -> p j f", p=P)
        sum_blocks = sum_dram[0:NB * P, :].rearrange("(j p) f -> p j f", p=P)

        iota_i = Hf[:, 0:7, :].bitcast(I32).rearrange("p a b -> p (a b)")
        tri_i = Hf[:, 7:9, :].bitcast(I32).rearrange("p a b -> p (a b)")
        sel_i = Hf[:, 9:11, :].bitcast(I32).rearrange("p a b -> p (a b)")
        base_i = Hf[:, 11:12, 0:GROUPS].bitcast(I32).rearrange("p a b -> p (a b)")
        before = sb("before", [P, P], F32)
        first = sb("first", [P, GROUPS], F32)
        base = sb("base", [P, GROUPS], F32)
        trash = sb("trash", [P, 1], F32)
        LANES = 4
        iota_l = sb("iota_l", [P, P, LANES], F16)

        def prepare():
            loads = [(w_fuse[:, 0, :], a["W_fuse"][0:P, :]), (w_fuse[:, 1, :], a["W_fuse"][P:2 * P, :]),
                     (w_gcn[0:32, 0, 0:H], a["W_nuc"]), (w_gcn[32:64, 0, H:2 * H], a["W_surf"]),
                     (w_gcn[64:96, 1, 0:H], a["W_nuc"]), (w_gcn[96:128, 1, H:2 * H], a["W_surf"]),
                     (wm1[0:F, 0, :], a["WM1"]), (wm1[F:P, 1, :], a["WM1"]), (wm2[:, :], a["WM2"]), (wm3[:, :], a["WM3"]),
                     (wu1[:, :], a["WU1"]), (wu2[:, :], a["WU2"]), (wu3[:, :], a["WU3"])]
            columns = [(b_gcn[:, 0:1], "b_nuc"), (b_gcn[:, 1:2], "b_surf"), (b_hid[:, 0:1], "bM1"),
                       (b_hid[:, 1:2], "bM2"), (b_hid[:, 2:3], "bU1"), (b_hid[:, 3:4], "bU2")]
            rows = [(b_fuse, "b_fuse"), (b_m3, "bM3"), (b_u3, "bU3")]
            CHUNKS = GROUPS // GC
            N = GC * P
            row_i = scratch(0, TILES, I32)
            row_f = scratch(4 * TILES, TILES, F32)
            below = scratch(8 * TILES, TILES // 2, F32).bitcast(BF16)
            at = 10 * TILES
            got = [scratch(at + c * 4 * 4 * N, 4 * N, I32).rearrange("p (g r e) -> p g r e", g=GC, r=4)
                   for c in range(2)]
            at += 32 * N
            rel = scratch(at, 2 * N, F32).rearrange("p (g r e) -> p g r e", g=GC, r=2)
            pen = scratch(at + 8 * N, 2 * N, F32).rearrange("p (g r e) -> p g r e", g=GC, r=2)
            low_i = scratch(at + 16 * N, 2 * N, I32).rearrange("p (g r e) -> p g r e", g=GC, r=2)
            low_half = scratch(at + 16 * N, 2 * N, F32).bitcast(mybir.dt.uint16) \
                .rearrange("p (g r e h) -> p g r e h", g=GC, r=2, h=2)[:, :, 0, :, 0]
            at += 24 * N
            select = scratch(at, 16 * P, F32).rearrange("p (k e) -> p k e", e=P)
            at += 64 * P
            masks = scratch(at, 2 * N, F32).bitcast(BF16).rearrange("p (k m) -> p k m", k=WN)
            code = Hf[:, 16:16 + 2 * 2 * GC, :].rearrange("p (c g a) b -> p c g (a b)", c=2, g=GC)
            parts = HL[:, :, :].rearrange("p a b -> p (a b)")
            same = parts[:, 0:REACH * N].bitcast(BF16).rearrange("p (t g e) -> p t g e", t=REACH, g=GC)
            code_16 = parts[:, REACH * N:(REACH + 1) * N].bitcast(mybir.dt.uint16) \
                .rearrange("p (g e) -> p g e", g=GC)
            with nc.psum_tensor("ps_key", [P, 2, 2, 512], F32) as ps_key, \
                    nc.psum_tensor("ps_win", [P, 512], F32) as ps_win, \
                    nc.psum_tensor("ps_deg", [P, 512], F32) as ps_deg, \
                    nc.psum_tensor("ps_bad", [P, 512], F32) as ps_bad, \
                    nc.sbuf_tensor("rows_below", [P, GROUPS], F32) as rows_below, \
                    nc.sbuf_tensor("win_deg", [P, GROUPS * WN], F32) as win_deg, \
                    nc.sbuf_tensor("ones_16", [P, 2], BF16) as ones_16, \
                    nc.sbuf_tensor("pairs", [P, GROUPS // GC], F32) as pairs, \
                    nc.sbuf_tensor("bad", [P, 3], F32) as bad, nc.sbuf_tensor("sums", [1, 4], F32) as sums, \
                    nc.sbuf_tensor("row_of", [P, GROUPS], U32) as row_of:
                rows_loaded, x_loaded, weights_loaded = sem("rows_loaded"), sem("x_loaded"), sem("weights_loaded")
                iotas_made, zeroed, ones_made = sem("iotas_made"), sem("zeroed"), sem("ones_made")
                rows_ready, step_p = sem("rows_ready"), sem("step_p")
                gathered = [sem(f"gathered{c}") for c in range(CHUNKS)]
                codes_made, turned, codes_read = sem("codes_made"), sem("turned"), sem("codes_read")
                same_made, same_read, masks_made, masks_read = (
                    sem(n) for n in ("same_made", "same_read", "masks_made", "masks_read"))
                win_ready, deg_made, bad_made, bad_summed = (
                    sem(n) for n in ("win_ready", "deg_made", "bad_made", "bad_summed"))

                with nc.Block() as block:
                    @block.sync
                    def _(sp):
                        sp.dma_start(row_i, a["row_first"].partition_broadcast(P)).then_inc(rows_loaded, 16)
                        sp.wait_ge(zeroed, 2)
                        for to, what in loads:
                            sp.dma_start(to, what).then_inc(weights_loaded, 16)
                        for to, name in columns:
                            sp.dma_start(to, a[name].rearrange("(p o) -> p o", o=1)).then_inc(weights_loaded, 16)
                        for to, name in rows:
                            sp.dma_start(to[:, :], a[name].partition_broadcast(P)).then_inc(weights_loaded, 16)
                        sp.dma_start(X[:, :, :], x_blocks).then_inc(x_loaded, 16)
                        sp.wait_ge(x_loaded, 16)
                        sp.wait_ge(weights_loaded, 16 * (len(loads) + len(columns) + len(rows)))

                    @block.gpsimd
                    def _(pool):
                        nc.gpsimd.iota(base_i, pattern=[[WN * P, GROUPS]], base=0,
                                       channel_multiplier=WN).then_inc(iotas_made, 1)
                        nc.gpsimd.iota(iota_i[:, 0:KEYS], pattern=[[1, KEYS]], base=0,
                                       channel_multiplier=0).then_inc(iotas_made, 1)
                        nc.gpsimd.iota(tri_i[:, 0:P], pattern=[[1, P]], base=0,
                                       channel_multiplier=-1).then_inc(iotas_made, 1)
                        nc.gpsimd.iota(sel_i[:, 0:P], pattern=[[-1, P]], base=0,
                                       channel_multiplier=WN).then_inc(iotas_made, 1)
                        nc.gpsimd.memset(w_gcn[:, :, :], 0.0).then_inc(zeroed, 1)
                        nc.gpsimd.memset(wm1[:, :, :], 0.0).then_inc(zeroed, 1)
                        nc.gpsimd.memset(ones[:, :], 1.0).then_inc(ones_made, 1)
                        nc.gpsimd.memset(ones_16[:, :], 1.0).then_inc(ones_made, 1)
                        nc.gpsimd.memset(same, 0.0).then_inc(ones_made, 1)
                        for c in range(CHUNKS):
                            pool.wait_ge(rows_ready, c + 1)
                            if c >= 2:
                                pool.wait_ge(codes_made, c - 1)
                            for g in range(GC):
                                nc.gpsimd.indirect_dma_start(
                                    out=got[c % 2][:, g, :, :].rearrange("p r e -> p (r e)"), out_offset=None,
                                    in_=a["edge_rows"],
                                    in_offset=bass.IndirectOffsetOnAxis(
                                        ap=row_of[:, GC * c + g:GC * c + g + 1], axis=0)).then_inc(gathered[c], 16)

                    @block.scalar
                    def _(act):
                        for c in range(CHUNKS):
                            act.wait_ge(same_made, c + 1)
                            nc.scalar.activation(same[:, :, :, :], same[:, :, :, :], ACT.Copy,
                                                 accum_out=pairs[:, c:c + 1]).then_inc(same_read, 1)

                    @block.tensor
                    def _(pe):
                        for c in range(CHUNKS):
                            pe.wait_ge(codes_made, c + 1)
                            if c >= 2:
                                pe.wait_ge(codes_read, c - 1)
                            for g in range(GC):
                                last = nc.tensor.transpose(
                                    ps_key[:, c % 2, g // 4, g % 4 * P:g % 4 * P + P], code[:, c % 2, g, :],
                                    ident[:, :])
                            last.then_inc(turned, 1)
                            pe.wait_ge(masks_made, c + 1)
                            if c == 0:
                                pe.wait_ge(ones_made, 2)
                            for g in range(GC):
                                for k in range(WN):
                                    col = WN * (GC * c + g) + k
                                    last = nc.tensor.matmul(ps_win[:, col:col + 1], masks[:, k, P * g:P * g + P],
                                                            ones_16[:, 0:1], start=True, stop=True)
                            last.then_inc(masks_read, 1)
                        pe.wait_ge(win_ready, 1)
                        by_place = win_deg[:, :].rearrange("p (g k) -> p k g", k=WN)
                        for q in range(4):
                            for k in range(WN):
                                last = nc.tensor.matmul(ps_deg[:, 32 * q:32 * q + GROUPS], select[:, 4 * q + k, :],
                                                        by_place[:, k, :], start=k == 0, stop=k == WN - 1)
                        last.then_inc(deg_made, 1)
                        pe.wait_ge(bad_made, 1)
                        nc.tensor.matmul(ps_bad[:, 0:2], ones[:, :], bad[:, 0:2], start=True,
                                         stop=True).then_inc(bad_summed, 1)

                    @block.vector
                    def _(dve):
                        chain = Chain(dve, step_p)
                        dve.wait_ge(iotas_made, 4)
                        nc.vector.tensor_scalar(base[:, :], base_i, MIDDLE, None, ALU.add)
                        nc.vector.tensor_scalar(trash[:, :], base_i[:, 0:1], 1.0 / WN, float(SINK), ALU.mult, ALU.add)
                        nc.vector.tensor_copy(first[:, :], base_i)
                        dve.wait_ge(rows_loaded, 16)
                        chain.link(nc.vector.tensor_copy(row_f, row_i))

                        def find_rows(c):
                            for n in range(GC * c, GC * c + GC):
                                chain.link(nc.vector.tensor_scalar(below, row_f, first[:, n:n + 1], 0.0, ALU.is_lt,
                                                                   ALU.add, accum_out=rows_below[:, n:n + 1]))
                            own = slice(GC * c, GC * c + GC)
                            nc.vector.tensor_scalar(row_of[:, own], rows_below[:, own], -1.0, 0.0, ALU.add,
                                                    ALU.max).then_inc(rows_ready, 1)

                        def make_codes(c):
                            src = got[c % 2][:, :, 0:4:2, :]
                            dst = got[c % 2][:, :, 1:4:2, :]
                            dve.wait_ge(gathered[c], 16 * GC)
                            for g in range(GC):
                                n = GC * c + g
                                last = nc.vector.tensor_scalar(rel[:, g, :, :], dst[:, g, :, :], base[:, n:n + 1],
                                                               None, ALU.subtract)
                            chain.link(last)
                            chain.link(nc.vector.tensor_tensor(pen[:, :, :, :], rel[:, :, :, :], rel[:, :, :, :],
                                                               ALU.mult))
                            chain.link(nc.vector.tensor_scalar(pen[:, :, :, :], pen[:, :, :, :], MIDDLE * MIDDLE, FAR,
                                                               ALU.is_gt, ALU.mult))
                            chain.link(nc.vector.scalar_tensor_tensor(rel[:, :, :, :], rel[:, :, :, :], float(P),
                                                                      pen[:, :, :, :], ALU.mult, ALU.add))
                            chain.link(nc.vector.tensor_scalar(low_i, src, 127, None, ALU.bitwise_and))
                            chain.link(nc.vector.scalar_tensor_tensor(rel[:, :, :, :], low_i, -(WN - 1.0),
                                                                      rel[:, :, :, :], ALU.mult, ALU.add))
                            chain.link(nc.vector.scalar_tensor_tensor(rel[:, :, :, :], src, float(WN),
                                                                      rel[:, :, :, :], ALU.mult, ALU.add))
                            nc.vector.tensor_tensor(code[:, c % 2, :, :], rel[:, :, 0, :], rel[:, :, 1, :],
                                                    ALU.min).then_inc(codes_made, 1)
                            dve.wait_ge(codes_made, c + 1)

                        def compare_codes(c):
                            ci = low_i[:, :, 0, :]
                            if c == 0:
                                dve.wait_ge(ones_made, 3)
                            chain.link(nc.vector.tensor_scalar(ci, code[:, c % 2, :, :], 0.0, None, ALU.add))
                            chain.link(nc.vector.tensor_copy(code_16, low_half))
                            if c:
                                dve.wait_ge(same_read, c)
                            for t in range(REACH):
                                last = nc.vector.tensor_tensor(same[:, t, :, 0:P - 1 - t],
                                                               code_16[:, :, 0:P - 1 - t],
                                                               code_16[:, :, t + 1:P], ALU.is_equal)
                            last.then_inc(same_made, 1)

                        def split_codes(c):
                            to = slice(N * c, N * c + N)
                            dve.wait_ge(turned, c + 1)
                            ci = low_i.rearrange("p g r e -> p (g r e)")
                            for h, n in ((0, 4), (1, GC - 4)):
                                last = nc.vector.tensor_scalar(ci[:, 4 * P * h:4 * P * h + n * P],
                                                               ps_key[:, c % 2, h, 0:n * P], MIDDLE * P, None,
                                                               ALU.add)
                            last.then_inc(codes_read, 1)
                            dve.wait_ge(codes_read, c + 1)
                            cj = ci[:, N:2 * N]
                            ci = ci[:, 0:N]
                            chain.link(nc.vector.tensor_scalar(cj, ci, 127, None, ALU.bitwise_and))
                            chain.link(nc.vector.tensor_copy(loT[:, to], cj))
                            chain.link(nc.vector.tensor_scalar(cj, ci, 7, None, ALU.logical_shift_right))
                            nc.vector.tensor_copy(keyT[:, to], cj)
                            chain.link(nc.vector.tensor_scalar(ci, cj, -1 - (P * WN - WN), None, ALU.bitwise_and))
                            if c:
                                dve.wait_ge(masks_read, c)
                            for k in range(WN):
                                last = nc.vector.tensor_scalar(masks[:, k, :], ci, float(k), None, ALU.is_equal)
                            last.then_inc(masks_made, 1)
                            dve.wait_ge(masks_made, c + 1)

                        find_rows(0)
                        nc.vector.tensor_copy(iota_k[:, :], iota_i[:, 0:KEYS])
                        for q in range(LANES):
                            nc.vector.tensor_copy(iota_l[:, :, q], iota_i[:, 0:P])
                        chain.link(nc.vector.tensor_scalar(ident[:, :], tri_i[:, 0:P], 0.0, None, ALU.is_equal))
                        nc.vector.tensor_tensor(stack[:, :], ident[:, 0:F], ident[:, F:2 * F], ALU.add)
                        nc.vector.tensor_scalar(before[:, :], tri_i[:, 0:P], 0.0, None, ALU.is_lt)
                        for q in range(4):
                            for k in range(WN):
                                chain.link(nc.vector.tensor_scalar(select[:, 4 * q + k, :], sel_i[:, 0:P],
                                                                   float(P * q - k), None, ALU.is_equal))
                        for c in range(CHUNKS):
                            if c + 1 < CHUNKS:
                                find_rows(c + 1)
                            make_codes(c)
                            compare_codes(c)
                            split_codes(c)

                        dve.wait_ge(masks_read, CHUNKS)
                        nc.vector.tensor_copy(win_deg[:, :], ps_win[:, 0:GROUPS * WN]).then_inc(win_ready, 1)
                        dve.wait_ge(deg_made, 1)
                        chain.link(nc.vector.tensor_copy(
                            deg[:, :].rearrange("p (g q) -> p q g", q=4),
                            ps_deg[:, 0:P].rearrange("p (q g) -> p q g", q=4)[:, :, 0:GROUPS]))
                        chain.link(nc.vector.tensor_reduce(bad[:, 0:1], deg[:, :], AX, ALU.add))
                        dve.wait_ge(same_read, CHUNKS)
                        chain.link(nc.vector.tensor_reduce(bad[:, 2:3], pairs[:, :], AX, ALU.max))
                        nc.vector.tensor_scalar(bad[:, 1:2], bad[:, 2:3], NEAR - 0.5, None,
                                                ALU.is_gt).then_inc(bad_made, 1)
                        dve.wait_ge(bad_summed, 1)
                        chain.link(nc.vector.tensor_copy(sums[:, 0:2], ps_bad[0:1, 0:2]))
                        chain.link(nc.vector.tensor_scalar(sums[:, 2:3], sums[:, 0:1], float(EDGES), None,
                                                           ALU.not_equal))
                        chain.link(nc.vector.tensor_tensor(sums[:, 3:4], sums[:, 1:2], sums[:, 2:3], ALU.add))
                        chain.link(nc.vector.tensor_copy(flag[:, :], sums[:, 3:4]))

        def general_degrees():
            dst_i = scratch(0, TILES, I32)
            lo_i = scratch(4 * TILES, TILES, I32)
            lo_f = scratch(8 * TILES, TILES, F32)
            hi_f = scratch(12 * TILES, TILES, F32)
            at = 16 * TILES
            hot_lo = scratch(at, 8 * P, F32).bitcast(BF16).rearrange("p (s n) -> p s n", s=16)
            hot_hi = scratch(at + 32 * P, 8 * NBW, F32).bitcast(BF16).rearrange("p (s n) -> p s n", s=16)
            dst_loaded, hot_made, hot_used, step_d = (sem(n) for n in ("dst_loaded", "hot_made", "hot_used", "step_d"))
            with nc.psum_tensor("ps_all", [P, 512], F32) as ps_all:
                with nc.Block() as block:
                    @block.sync
                    def _(sp):
                        sp.dma_start(dst_i, a["dst_grid"]).then_inc(dst_loaded, 16)

                    @block.vector
                    def _(dve):
                        chain = Chain(dve, step_d)
                        dve.wait_ge(dst_loaded, 16)
                        chain.link(nc.vector.tensor_scalar(lo_i, dst_i, 127, None, ALU.bitwise_and))
                        chain.link(nc.vector.tensor_copy(lo_f, lo_i))
                        chain.link(nc.vector.tensor_scalar(lo_i, dst_i, 7, None, ALU.logical_shift_right))
                        chain.link(nc.vector.tensor_copy(hi_f, lo_i))

                        def one_hots(i, begin):
                            for g in range(4):
                                if not begin:
                                    dve.wait_ge(hot_used, 4 * i + g - 3)
                                for s in range(4 * g, 4 * g + 4):
                                    col = 16 * i + s
                                    nc.vector.tensor_scalar(hot_lo[:, s, :], iota_k[:, 0:P],
                                                            lo_f[:, bass.ds(col, 1)], None, ALU.is_equal)
                                    last = nc.vector.tensor_scalar(hot_hi[:, s, :], iota_k[:, 0:NBW],
                                                                   hi_f[:, bass.ds(col, 1)], None, ALU.is_equal)
                                last.then_inc(hot_made, 1)

                        one_hots(0, True)
                        with dve.Fori(1, TILES // 16) as i:
                            one_hots(i, False)
                        dve.wait_ge(hot_used, TILES // 4)
                        nc.vector.tensor_copy(deg[:, :], ps_all[:, 0:NBW])

                    @block.tensor
                    def _(pe):
                        def count(i, begin, end):
                            for g in range(4):
                                pe.wait_ge(hot_made, 4 * i + g + 1)
                                for s in range(4 * g, 4 * g + 4):
                                    mm = nc.tensor.matmul(ps_all[:, 0:NBW], hot_lo[:, s, :], hot_hi[:, s, :],
                                                          start=begin and s == 0, stop=end and s == 15,
                                                          skip_group_check=True)
                                mm.then_inc(hot_used, 1)

                        count(0, True, False)
                        with pe.Fori(1, TILES // 16 - 1) as i:
                            count(i, False, False)
                        count(TILES // 16 - 1, False, True)

        def normalise():
            var_ready, std_ready, step_v = sem("var_ready"), sem("std_ready"), sem("step_v")
            with nc.Block() as block:
                @block.scalar
                def _(act):
                    act.wait_ge(var_ready, 1)
                    nc.scalar.activation(stat[:, 1, :], stat[:, 0, :], ACT.Sqrt).then_inc(std_ready, 1)

                @block.vector
                def _(dve):
                    chain = Chain(dve, step_v)
                    nc.vector.tensor_scalar(stat[:, 0, :], deg[:, 0:NB], 1.0, None, ALU.add).then_inc(var_ready, 1)
                    dve.wait_ge(std_ready, 1)
                    chain.link(nc.vector.reciprocal(dinv[:, :], stat[:, 1, :]))
                    chain.link(nc.vector.tensor_tensor(Hf[:, :, :], X[:, :, :], over(dinv[:, :]), ALU.mult))

        def load_pair(sp, j, b, loaded):
            sp.dma_start(region[:, b, :], counts_dram[bass.ds(j, 1), :, :].rearrange("o p n -> (o p) n")) \
                .then_inc(loaded[b], 16)

        def two_parts(tag, loaded):
            tops_made = sem("tops_made" + tag)
            worst, spread, powers, sent, hi_made, low_made, step_t = (
                sem(n + tag) for n in ("worst", "spread", "powers", "sent", "hi", "low", "step_t"))
            cuts = [(UB * 2 * k, UB * 2 * (k + 1)) for k in range(UNITS // 2)]
            with nc.psum_tensor("ps_max" + tag, [P, 512], F32) as ps_max, \
                    nc.psum_tensor("ps_pow" + tag, [P, 512], F32) as ps_pow, \
                    nc.sbuf_tensor("top" + tag, [P, 1], F32) as top, \
                    nc.sbuf_tensor("bits" + tag, [1, 5], I32) as bits:
                with nc.Block() as block:
                    if loaded:
                        @block.sync
                        def _(sp):
                            for b in range(3):
                                load_pair(sp, b, b, loaded)

                    @block.tensor
                    def _(pe):
                        pe.wait_ge(worst, 1)
                        nc.tensor.transpose(ps_max[0:1, 0:P], top[:, :], ident[:, :]).then_inc(spread, 1)
                        pe.wait_ge(powers, 1)
                        nc.tensor.matmul(ps_pow[:, 0:2], ones[0:1, :], bits[:, 3:5].bitcast(F32), start=True,
                                         stop=True).then_inc(sent, 1)

                    @block.scalar
                    def _(act):
                        act.wait_ge(step_t, 5)
                        for lo, up in cuts:
                            nc.scalar.activation(HL[:, lo:up, 0:F], Hf[:, lo:up, :], ACT.Copy,
                                                 scale=scales[:, 0:1]).then_inc(hi_made, 1)

                    @block.vector
                    def _(dve):
                        chain = Chain(dve, step_t)
                        if not loaded:
                            for u in range(UNITS):
                                last = nc.vector.tensor_reduce(
                                    tops[:, u:u + 1], Hf[:, UB * u:UB * u + UB, :].rearrange("p a b -> p (a b)"), AX,
                                    ALU.max, apply_absolute_value=True)
                            last.then_inc(tops_made, 1)
                            dve.wait_ge(tops_made, 1)
                        nc.vector.tensor_reduce(top[:, :], tops[:, :], AX, ALU.max).then_inc(worst, 1)
                        dve.wait_ge(spread, 1)
                        chain.link(nc.vector.tensor_reduce(bits[:, 0:1].bitcast(F32), ps_max[0:1, 0:P], AX, ALU.max))
                        chain.link(nc.vector.tensor_scalar(bits[:, 1:2], bits[:, 0:1], 255 * EXP1, None,
                                                           ALU.bitwise_and))
                        chain.link(nc.vector.tensor_scalar(bits[:, 2:3], bits[:, 1:2], 30.0 * EXP1, None, ALU.max))
                        chain.link(nc.vector.tensor_scalar(bits[:, 3:4], bits[:, 2:3], -1.0, 268.0 * EXP1, ALU.mult,
                                                           ALU.add))
                        nc.vector.tensor_scalar(bits[:, 4:5], bits[:, 2:3], -14.0 * EXP1, None,
                                                ALU.add).then_inc(powers, 1)
                        dve.wait_ge(sent, 1)
                        chain.link(nc.vector.tensor_copy(scales[:, :], ps_pow[:, 0:2]))
                        nc.vector.tensor_scalar(merge[:, :], stack[:, :], scales[:, 1:2], None, ALU.mult)
                        for k, (lo, up) in enumerate(cuts):
                            dve.wait_ge(hi_made, k + 1)
                            nc.vector.scalar_tensor_tensor(HL[:, lo:up, F:2 * F], Hf[:, lo:up, :], scales[:, 0:1],
                                                           HL[:, lo:up, 0:F], ALU.mult,
                                                           ALU.subtract).then_inc(low_made, 1)

        def every_pair(eng, body):
            for b in range(3):
                body(b, 0, b)
            with eng.Fori(1, NP // 3) as i:
                for b in range(3):
                    body(3 * i + b, i, b)
            for b in range(NP % 3):
                body(NP // 3 * 3 + b, NP // 3, b)

        def add_pair(j, sums, add):
            mine = Hf[:, bass.ds(2 * j, 2), :]
            got = sums.rearrange("p (a f) -> p a f", f=F)
            if add:
                return nc.vector.tensor_tensor(mine, mine, got, ALU.add)
            return nc.vector.tensor_copy(mine, got)

        class Finish:
            A, B = 3, 8

            def __init__(self):
                self.shifted, self.exped = sem("shifted"), sem("exped")
                self.step_a, self.step_b = sem("step_a"), sem("step_b")

            def exponent(self, act, j, b):
                act.wait_ge(self.shifted, j + 1)
                nc.scalar.activation(soft[:, b, :, :], soft[:, b, :, :], ACT.Exp).then_inc(self.exped, 1)

            def shift(self, dve, j, b, sums, added):
                chain = Chain(dve, self.step_a, self.A * j)
                part = soft[:, b, :, :]
                own = bass.ds(2 * j, 2)
                if sums is None:
                    nc.vector.tensor_copy(part, Hf[:, own, :]).then_inc(added, 1)
                else:
                    nc.vector.tensor_tensor(part, Hf[:, own, :], sums.rearrange("p (a f) -> p a f", f=F),
                                            ALU.add).then_inc(added, 1)
                dve.wait_ge(added, j + 1)
                chain.link(nc.vector.tensor_tensor(part, part, over(dinv[:, own]), ALU.mult))
                chain.link(nc.vector.tensor_tensor(part, part, each(b_fuse, 2), ALU.add))
                chain.link(nc.vector.tensor_reduce(soft_sums[:, b, 0, :], part, AX, ALU.max))
                nc.vector.tensor_tensor(part, part, over(soft_sums[:, b, 0, :]), ALU.subtract) \
                    .then_inc(self.shifted, 1)

            def centre(self, dve, j, b):
                chain = Chain(dve, self.step_b, self.B * j)
                part = soft[:, b, :, :]
                mine = X[:, bass.ds(2 * j, 2), :]
                dve.wait_ge(self.exped, j + 1)
                chain.link(nc.vector.tensor_reduce(soft_sums[:, b, 1, :], part, AX, ALU.add))
                chain.link(nc.vector.reciprocal(soft_sums[:, b, 2, :], soft_sums[:, b, 1, :]))
                chain.link(nc.vector.tensor_tensor(part, part, over(soft_sums[:, b, 2, :]), ALU.mult))
                chain.link(nc.vector.tensor_tensor(part, part, mine, ALU.add))
                chain.link(nc.vector.tensor_reduce(soft_sums[:, b, 3, :], part, AX, ALU.add))
                chain.link(nc.vector.scalar_tensor_tensor(mine, over(soft_sums[:, b, 3, :]), -1.0 / F, part,
                                                          ALU.mult, ALU.add))
                chain.link(nc.vector.tensor_tensor(part, mine, mine, ALU.mult))
                chain.link(nc.vector.tensor_reduce(stat[:, 1, bass.ds(2 * j, 2)], part, AX, ALU.add))


            def alone(self):
                added = sem("finish_added")
                with nc.Block() as block:
                    @block.scalar
                    def _(act):
                        every_pair(act, lambda j, i, b: self.exponent(act, j, b))

                    @block.vector
                    def _(dve):
                        def pair(j, i, b):
                            self.shift(dve, j, b, None, added)
                            self.centre(dve, j, b)

                        every_pair(dve, pair)

        def merge_parts(to, sums_t):
            for c in range(2):
                mm = nc.tensor.matmul(to[:, F * c:F * c + F], sums_t[:, P * c:P * c + P], merge[:, :], start=True,
                                      stop=True)
            return mm

        def first_sum():
            RING, HOTS, LAG, GAP = 3, 16, 8, 3
            SLOTS = PW - GAP
            BATCH = 16
            DUOS = PW // 2
            DVE_DUOS = [9, 25]
            BEHIND = 11
            ACT_DUOS = [k for k in range(DUOS) if k not in DVE_DUOS]
            with nc.psum_tensor("ps_cnt", [P, 2 * RING, 512], F32) as ps_cnt, \
                    nc.psum_tensor("ps_out", [P, 512], F32) as ps_out, \
                    nc.psum_tensor("ps_node", [P, 512], F32) as ps_node, \
                    nc.sbuf_tensor("hot_k", [P, HOTS, KEYS], BF16) as hot_k, \
                    nc.sbuf_tensor("hot_l", [P, 2, BATCH // LANES, P, LANES], BF16) as hot_l, \
                    nc.sbuf_tensor("win_lo", [P, PW], F16) as win_lo, \
                    nc.sbuf_tensor("win_key", [P, PW], F32) as win_key, \
                    nc.sbuf_tensor("sums_t", [P, DP], F32) as sums_t:
                cols_copied, hots_made, duos_made = sem("cols_copied"), sem("hots_made"), sem("duos_made")
                act_evicted, dve_evicted = sem("act_evicted"), sem("dve_evicted")
                stored = [sem(f"counts_stored{b}") for b in range(3)]
                summed, copied, merged, added = (
                    sem("pair_" + n) for n in ("summed", "copied", "merged", "added"))

                def duo_in(b, k):
                    r = (DUOS * b + k) % RING
                    return ps_cnt[:, 2 * r:2 * r + 2, 0:KEYS].rearrange("p w (h d) -> p w h d", d=WN)

                def duo_out(b, k):
                    return counts8[b].rearrange("p h (w d) -> p w h d", d=WN)[:, 2 * k:2 * k + 2, :, :]

                def buffer_free(eng, j, i, b):
                    wait_past(eng, stored[b], 16 * i)
                    wait_past(eng, summed, j - 2)

                with nc.Block() as block:
                    @block.sync
                    def _(sp):
                        def store(j, i, b):
                            wait_apart(sp, (act_evicted, len(ACT_DUOS) * (j + 1)),
                                       (dve_evicted, len(DVE_DUOS) * (j + 1)))
                            sp.dma_start(counts_dram[bass.ds(j, 1), :, :].rearrange("o p n -> (o p) n"),
                                         region[:, b, :]).then_inc(stored[b], 16)

                        every_pair(sp, store)
                        for b in range(3):
                            sp.wait_ge(stored[b], 16 * (NP // 3 + (b < NP % 3)))

                    @block.vector
                    def _(dve):
                        def take(j):
                            dve.wait_ge(merged, j + 1)
                            add_pair(j, ps_node[:, 0:2 * F], True).then_inc(added, 1)

                        def evict(j, b, k):
                            wait_apart(dve, (duos_made, DUOS * j + k + 1))
                            nc.vector.tensor_scalar(duo_out(b, k), duo_in(b, k), 1.0, None, ALU.mult,
                                                    saturate=False).then_inc(dve_evicted, 1)

                        def make(j, i, b):
                            early = isinstance(j, int) and j == 0
                            if not early:
                                dve.wait_ge(hots_made, PW * j)
                            nc.vector.tensor_copy(win_lo[:, :], loT[:, bass.ds(PW * j, PW)])
                            nc.vector.tensor_copy(win_key[:, :], keyT[:, bass.ds(PW * j, PW)]) \
                                .then_inc(cols_copied, 1)
                            dve.wait_ge(cols_copied, j + 1)
                            buffer_free(dve, j, i, b)
                            for k in range(PW):
                                if k % 2 == 0 and not (early and k < HOTS):
                                    dve.wait_ge(duos_made, DUOS * j + k // 2 + 1 - HOTS // 2)
                                if k % BATCH == 0:
                                    n = BATCH // LANES
                                    nc.vector.tensor_tensor(
                                        hot_l[:, k // BATCH % 2, :, :, :],
                                        win_lo[:, k:k + BATCH].rearrange("p (a q) -> p a q", q=LANES)
                                        .unsqueeze(2).broadcast_to((P, n, P, LANES)),
                                        iota_l[:, :, :].unsqueeze(1).broadcast_to((P, n, P, LANES)), ALU.is_equal)
                                nc.vector.tensor_scalar(hot_k[:, k % HOTS, :], iota_k[:, :], win_key[:, k:k + 1],
                                                        None, ALU.is_equal).then_inc(hots_made, 1)
                                if k % 2 and (k - BEHIND) // 2 in DVE_DUOS:
                                    evict(j, b, (k - BEHIND) // 2)
                                if k == PW // 2 and not (isinstance(j, int) and j < 2):
                                    take(j - 2)

                        every_pair(dve, make)
                        take(NP - 2)
                        take(NP - 1)

                    @block.scalar
                    def _(act):
                        def copy(j):
                            act.wait_ge(summed, j + 1)
                            wait_past(act, merged, j)
                            nc.scalar.activation(sums_t[:, :], ps_out[:, 0:DP], ACT.Copy).then_inc(copied, 1)

                        def evict(j, i, b):
                            buffer_free(act, j, i, b)
                            for k in ACT_DUOS:
                                if k == LAG // 2 - 1 and not (isinstance(j, int) and j < 2):
                                    copy(j - 2)
                                wait_apart(act, (duos_made, DUOS * j + k + 1))
                                nc.scalar.activation(duo_out(b, k), duo_in(b, k), ACT.Copy,
                                                     saturate=False).then_inc(act_evicted, 1)

                        every_pair(act, evict)
                        copy(NP - 2)
                        copy(NP - 1)

                    @block.tensor
                    def _(pe):
                        def wait_evicted(j, n):
                            k = n % DUOS
                            for duos, evicted in ((ACT_DUOS, act_evicted), (DVE_DUOS, dve_evicted)):
                                if k in duos:
                                    pe.wait_ge(evicted, len(duos) * (j + n // DUOS) + duos.index(k) + 1)

                        def start_sums(j):
                            taken = [] if isinstance(j, int) and j < 1 else [(copied, j)]
                            wait_apart(pe, (act_evicted, len(ACT_DUOS) * (j + 1)),
                                       (dve_evicted, len(DVE_DUOS) * (j + 1)), *taken)

                        def slot(n):
                            return range(NB * n // SLOTS, NB * (n + 1) // SLOTS)

                        def sums(j, b, part):
                            for h in part:
                                mm = nc.tensor.matmul(ps_out[:, 0:DP], HL[:, h, :], counts8[b][:, h, :],
                                                      start=h == 0, stop=h == NB - 1, skip_group_check=True)
                                if h == NB - 1:
                                    mm.then_inc(summed, 1)

                        def turn(j):
                            pe.wait_ge(copied, j + 1)
                            wait_past(pe, added, j)
                            merge_parts(ps_node, sums_t).then_inc(merged, 1)

                        def make(j, i, b):
                            early = isinstance(j, int) and j == 0
                            for k in range(PW):
                                n = k // 2
                                if k % 2 == 0 and not (early and n < RING):
                                    wait_evicted(j, n - RING)
                                pe.wait_ge(hots_made, PW * j + k + 1)
                                mm = nc.tensor.matmul(
                                    ps_cnt[:, 2 * ((DUOS * b + n) % RING) + k % 2, 0:KEYS],
                                    hot_l[:, k // BATCH % 2, k % BATCH // LANES, :, k % LANES],
                                    hot_k[:, k % HOTS, :], start=True, stop=True)
                                if k % 2:
                                    mm.then_inc(duos_made, 1)
                                if k == LAG and not early:
                                    start_sums(j - 1)
                                if k >= LAG and not early:
                                    sums(j - 1, (b - 1) % 3, slot(k - LAG))
                                if k < LAG - GAP and not (isinstance(j, int) and j < 2):
                                    sums(j - 2, (b - 2) % 3, slot(k + PW - LAG))
                                if k == LAG + 8 and not (isinstance(j, int) and j < 2):
                                    turn(j - 2)

                        every_pair(pe, make)
                        sums(NP - 2, (NP - 2) % 3, range(NB * (PW - LAG) // SLOTS, NB))
                        start_sums(NP - 1)
                        turn(NP - 2)
                        sums(NP - 1, (NP - 1) % 3, range(NB))
                        turn(NP - 1)

        def later_sum(tag, finish, loaded):
            with nc.psum_tensor("ps_sum" + tag, [P, 3, 512], F32) as ps_sum, \
                    nc.psum_tensor("ps_node" + tag, [P, 3, 512], F32) as ps_node, \
                    nc.sbuf_tensor("sums_t" + tag, [P, 3, DP], F32) as sums_t:
                summed, copied, merged, added = (
                    sem("pair_" + n + tag) for n in ("summed", "copied", "merged", "added"))

                with nc.Block() as block:
                    @block.sync
                    def _(sp):
                        def load(j, i, b):
                            if not isinstance(j, int) or j >= 3:
                                wait_apart(sp, (summed, j - 2))
                                load_pair(sp, j, b, loaded)

                        every_pair(sp, load)

                    @block.tensor
                    def _(pe):
                        def turn(j, b):
                            pe.wait_ge(copied, j + 1)
                            wait_past(pe, added, j - 2)
                            merge_parts(ps_node[:, b, :], sums_t[:, b, :]).then_inc(merged, 1)

                        def sums(j, i, b):
                            if isinstance(j, int) and j < 3:
                                pe.wait_ge(loaded[b], 16)
                            else:
                                wait_apart(pe, (loaded[b], 16 * (i + 1)), (copied, j - 2))
                            for h in range(NB):
                                mm = nc.tensor.matmul(ps_sum[:, b, 0:DP], HL[:, h, :], counts8[b][:, h, :],
                                                      start=h == 0, stop=h == NB - 1)
                            mm.then_inc(summed, 1)
                            if not isinstance(j, int) or j > 0:
                                turn(j - 1, (b - 1) % 3)

                        every_pair(pe, sums)
                        turn(NP - 1, (NP - 1) % 3)

                    @block.scalar
                    def _(act):
                        def copy(j, i, b):
                            act.wait_ge(summed, j + 1)
                            wait_past(act, merged, j - 2)
                            nc.scalar.activation(sums_t[:, b, :], ps_sum[:, b, 0:DP], ACT.Copy).then_inc(copied, 1)
                            if finish and not (isinstance(j, int) and j < 2):
                                finish.exponent(act, j - 2, (b - 2) % 3)

                        every_pair(act, copy)
                        if finish:
                            finish.exponent(act, NP - 2, (NP - 2) % 3)
                            finish.exponent(act, NP - 1, (NP - 1) % 3)

                    @block.vector
                    def _(dve):
                        def take(j, i, b):
                            dve.wait_ge(merged, j + 1)
                            if not finish:
                                add_pair(j, ps_node[:, b, 0:2 * F], False).then_inc(added, 1)
                                return
                            finish.shift(dve, j, b, ps_node[:, b, 0:2 * F], added)
                            if not isinstance(j, int) or j > 0:
                                finish.centre(dve, j - 1, (b - 1) % 3)

                        every_pair(dve, take)
                        if finish:
                            finish.centre(dve, NP - 1, (NP - 1) % 3)

        def general_sum(tag, add):
            src_i = scratch(0, TILES, I32)
            own = []

            def sem(name):
                own.append(nc.alloc_semaphore(name=name))
                return own[-1]

            dst_i = scratch(4 * TILES, TILES, I32)
            sum_thirds = sum_dram.rearrange("(c p n) f -> c p (n f)", c=3, p=P)
            zero = scratch(8 * TILES, SUMROWS // 3 // P * F, F32)
            with nc.psum_tensor("ps_dst" + tag, [P, 512], F32) as ps_dst, \
                    nc.psum_tensor("ps_rows" + tag, [P, 512], F32) as ps_rows, \
                    nc.sbuf_tensor("rows_in" + tag, [P, F], F32) as rows_in, \
                    nc.sbuf_tensor("rows_out" + tag, [P, F], F32) as rows_out, \
                    nc.sbuf_tensor("diag" + tag, [P, P], F32) as diag, \
                    nc.sbuf_tensor("same" + tag, [P, P], F32) as same, \
                    nc.sbuf_tensor("earlier" + tag, [P, P], F32) as earlier, \
                    nc.sbuf_tensor("cols" + tag, [P, 5], F32) as cols, \
                    nc.sbuf_tensor("src_col" + tag, [P, 1], U32) as src_col, \
                    nc.sbuf_tensor("to_col" + tag, [P, 1], U32) as to_col:
                tables_ready, zero_made = sem("tables_ready" + tag), sem("zero_made" + tag)
                gathered, scattered = sem("rows_gathered" + tag), sem("rows_scattered" + tag)
                src_ready, diag_ready, dst_spread = (sem(n + tag) for n in ("src_ready", "diag_ready", "dst_spread"))
                same_ready, to_ready, summed = (sem(n + tag) for n in ("same_ready", "to_ready", "summed"))
                rows_ready, step_g = sem("rows_ready" + tag), sem("step_g" + tag)
                with nc.Block() as block:
                    @block.sync
                    def _(sp):
                        sp.dma_start(src_i, a["src_grid"]).then_inc(tables_ready, 16)
                        sp.dma_start(dst_i, a["dst_grid"]).then_inc(tables_ready, 16)
                        sp.dma_start(feat_blocks, Hf[:, :, :]).then_inc(tables_ready, 16)
                        sp.wait_ge(zero_made, 1)
                        for c in range(3):
                            sp.dma_start(sum_thirds[c], zero).then_inc(tables_ready, 16)
                        sp.wait_ge(tables_ready, 16 * 6)

                    @block.vector
                    def _(dve):
                        nc.vector.memset(zero, 0.0).then_inc(zero_made, 1)

                with nc.Block() as block:
                    @block.vector
                    def _(dve):
                        def tile(t):
                            chain = Chain(dve, step_g, 6 * t)
                            dve.wait_ge(gathered, 16 * t)
                            dve.wait_ge(scattered, 16 * t)
                            dve.wait_ge(summed, t)
                            nc.vector.tensor_copy(src_col[:, :].bitcast(I32), src_i[:, bass.ds(t, 1)]) \
                                .then_inc(src_ready, 1)
                            chain.link(nc.vector.tensor_copy(cols[:, 0:1], dst_i[:, bass.ds(t, 1)]))
                            nc.vector.tensor_scalar(diag[:, :], ident[:, :], cols[:, 0:1], None,
                                                    ALU.mult).then_inc(diag_ready, 1)
                            dve.wait_ge(dst_spread, t + 1)
                            nc.vector.tensor_scalar(same[:, :], ps_dst[:, 0:P], cols[:, 0:1], None,
                                                    ALU.is_equal).then_inc(same_ready, 1)
                            dve.wait_ge(same_ready, t + 1)
                            chain.link(nc.vector.tensor_tensor(earlier[:, :], same[:, :], before[:, :], ALU.mult))
                            chain.link(nc.vector.tensor_reduce(cols[:, 1:2], earlier[:, :], AX, ALU.max))
                            chain.link(nc.vector.tensor_tensor(cols[:, 2:3], trash[:, :], cols[:, 0:1], ALU.subtract))
                            chain.link(nc.vector.tensor_tensor(cols[:, 3:4], cols[:, 2:3], cols[:, 1:2], ALU.mult))
                            chain.link(nc.vector.tensor_tensor(cols[:, 4:5], cols[:, 3:4], cols[:, 0:1], ALU.add))
                            nc.vector.tensor_copy(to_col[:, :], cols[:, 4:5]).then_inc(to_ready, 1)
                            assert chain.n == 6

                        tile(0)
                        with dve.Fori(1, TILES) as t:
                            tile(t)

                    @block.gpsimd
                    def _(pool):
                        def tile(t):
                            wait_apart(pool, (src_ready, t + 1), (summed, t))
                            nc.gpsimd.indirect_dma_start(
                                out=rows_in[:, :], out_offset=None, in_=feat_dram,
                                in_offset=bass.IndirectOffsetOnAxis(ap=src_col[:, :], axis=0)).then_inc(gathered, 16)
                            wait_apart(pool, (rows_ready, t + 1), (to_ready, t + 1), (scattered, 16 * t))
                            nc.gpsimd.indirect_dma_start(
                                out=sum_dram, out_offset=bass.IndirectOffsetOnAxis(ap=to_col[:, :], axis=0),
                                in_=rows_out[:, :], in_offset=None, compute_op=ALU.add).then_inc(scattered, 16)

                        tile(0)
                        with pool.Fori(1, TILES) as t:
                            tile(t)
                        pool.wait_ge(scattered, 16 * TILES)

                    @block.tensor
                    def _(pe):
                        def tile(t):
                            pe.wait_ge(diag_ready, t + 1)
                            nc.tensor.matmul(ps_dst[:, 0:P], ones[:, :], diag[:, :], start=True,
                                             stop=True).then_inc(dst_spread, 1)
                            pe.wait_ge(same_ready, t + 1)
                            pe.wait_ge(gathered, 16 * (t + 1))
                            pe.wait_ge(rows_ready, t)
                            nc.tensor.matmul(ps_rows[:, 0:F], same[:, :], rows_in[:, :], start=True,
                                             stop=True).then_inc(summed, 1)

                        tile(0)
                        with pe.Fori(1, TILES) as t:
                            tile(t)

                    @block.scalar
                    def _(act):
                        def tile(t):
                            act.wait_ge(summed, t + 1)
                            act.wait_ge(scattered, 16 * t)
                            nc.scalar.activation(rows_out[:, :], ps_rows[:, 0:F], ACT.Copy).then_inc(rows_ready, 1)

                        tile(0)
                        with act.Fori(1, TILES) as t:
                            tile(t)

                fetched, totalled = sem("fetched" + tag), sem("totalled" + tag)
                got = scratch(0, NB * F, F32).rearrange("p (j f) -> p j f", f=F)
                with nc.Block() as block:
                    @block.sync
                    def _(sp):
                        sp.dma_start(got if add else Hf[:, :, :], sum_blocks).then_inc(fetched, 16)
                        sp.wait_ge(fetched, 16)

                    @block.vector
                    def _(dve):
                        if add:
                            dve.wait_ge(fetched, 16)
                            nc.vector.tensor_tensor(Hf[:, :, :], Hf[:, :, :], got, ALU.add).then_inc(totalled, 1)

            nc.clear_and_free_semaphores(own)
            nc.all_engine_barrier()

        def gcn_dense():
            with nc.psum_tensor("ps_t", [P, 2, EVEN * P], F32) as ps_t, \
                    nc.psum_tensor("ps_h", [P, 2, 2, 512], F32) as ps_h, \
                    nc.psum_tensor("ps_f", [P, 512], F32) as ps_f:
                bufs = [share((P, 2 * EVEN, F), (P, EVEN * P), (P, 2, UN), (P, 2, UN), (P, 2, UN), start=c * GCN_BYTES)
                        for c in range(2)]
                agg, agg_t, neg, lin, hid = zip(*bufs)
                padded = sem("padded")
                scaled, turned, copied, hidden = sem("d_scaled"), sem("d_turned"), sem("d_copied"), sem("d_hidden")
                neg_made, exp_made, lin_made = sem("neg_made"), sem("exp_made"), sem("lin_made")
                elu_made, fused, out_made = sem("elu_made"), sem("fused"), sem("fused_out")

                with nc.Block() as block:
                    @block.gpsimd
                    def _(pool):
                        def scale(u, c):
                            wait_past(pool, turned, u - 1)
                            nc.gpsimd.tensor_tensor(agg[c][:, 0:UB, :], Hf[:, bass.ds(UB * u, UB), :],
                                                    over(dinv[:, bass.ds(UB * u, UB)]),
                                                    ALU.mult).then_inc(scaled, 1)

                        stagger(pool, [(0, scale)], UNITS)

                    @block.vector
                    def _(dve):
                        for c in range(2):
                            nc.vector.memset(agg[c][:, UB:2 * EVEN, :], 0.0).then_inc(padded, 1)

                        def negative(u, c):
                            wait_past(dve, elu_made, 2 * u - 2)
                            for m in range(2):
                                dve.wait_ge(lin_made, 2 * u + m + 1)
                                nc.vector.tensor_scalar(neg[c][:, m, :], lin[c][:, m, :], 0.0, None,
                                                        ALU.min).then_inc(neg_made, 1)

                        def elu(u, c):
                            wait_past(dve, fused, u - 1)
                            for m in range(2):
                                dve.wait_ge(exp_made, 2 * u + m + 1)
                                nc.vector.scalar_tensor_tensor(hid[c][:, m, :], neg[c][:, m, :], -1.0,
                                                               lin[c][:, m, :], ALU.add,
                                                               ALU.max).then_inc(elu_made, 1)

                        def leave(u, c):
                            dve.wait_ge(fused, u + 1)
                            nc.vector.tensor_tensor(Hf[:, bass.ds(UB * u, UB), :],
                                                    ps_f[:, 0:UB * F].rearrange("p (j f) -> p j f", f=F),
                                                    over(dinv[:, bass.ds(UB * u, UB)]),
                                                    ALU.mult).then_inc(out_made, 1)
                            dve.wait_ge(out_made, u + 1)
                            nc.vector.tensor_reduce(
                                tops[:, bass.ds(u, 1)],
                                Hf[:, bass.ds(UB * u, UB), :].rearrange("p j f -> p (j f)"), AX, ALU.max,
                                apply_absolute_value=True)

                        stagger(dve, [(3, elu), (4, leave), (2, negative)], UNITS)

                    @block.tensor
                    def _(pe):
                        def turn(u, c):
                            wait_apart(pe, (scaled, u + 1), *([(copied, u - 1)] if not isinstance(u, int) or u > 1 else []))
                            for k in range(EVEN):
                                mm = nc.tensor.transpose(
                                    ps_t[:, c, P * k:P * k + P],
                                    agg[c][:, 2 * k:2 * k + 2, :].rearrange("p j f -> p (j f)"), ident[:, :])
                            mm.then_inc(turned, 1)

                        def hide(u, c):
                            pe.wait_ge(copied, u + 1)
                            for m in range(2):
                                wait_past(pe, lin_made, 2 * u - 1 + m)
                                for h, n in enumerate((EVEN, UB - EVEN)):
                                    mm = nc.tensor.matmul(ps_h[:, m, h, 0:n * P], w_gcn[:, h, m * H:(m + 1) * H],
                                                          agg_t[c][:, 0:n * P], start=True, stop=True)
                                mm.then_inc(hidden, 1)

                        def fuse(u, c):
                            pe.wait_ge(elu_made, 2 * u + 2)
                            wait_past(pe, out_made, u)
                            for k in range(UB):
                                for m in range(2):
                                    mm = nc.tensor.matmul(ps_f[:, F * k:F * k + F], hid[c][:, m, place(k):place(k) + P],
                                                          w_fuse[:, m, :], start=m == 0, stop=m == 1)
                            mm.then_inc(fused, 1)

                        pe.wait_ge(padded, 2)
                        stagger(pe, [(4, fuse), (0, turn), (1, hide)], UNITS)

                    @block.scalar
                    def _(act):
                        def copy(u, c):
                            act.wait_ge(turned, u + 1)
                            wait_past(act, hidden, 2 * u - 2)
                            nc.scalar.activation(agg_t[c], ps_t[:, c, :], ACT.Copy).then_inc(copied, 1)

                        def linear(u, c):
                            wait_past(act, elu_made, 2 * u - 2)
                            for m in range(2):
                                act.wait_ge(hidden, 2 * u + m + 1)
                                nc.scalar.activation(
                                    lin[c][:, m, :], ps_h[:, m, :, :].rearrange("p a b -> p (a b)")[:, 0:UN],
                                    ACT.Identity, bias=b_gcn[:, m:m + 1]).then_inc(lin_made, 1)

                        def exp(u, c):
                            for m in range(2):
                                act.wait_ge(neg_made, 2 * u + m + 1)
                                nc.scalar.activation(neg[c][:, m, :], neg[c][:, m, :], ACT.Exp).then_inc(exp_made, 1)

                        stagger(act, [(1, copy), (3, exp), (2, linear)], UNITS)

        def mlp(tag, width, w1, w2, w3, hb, b3, last):
            with nc.psum_tensor("ps_t" + tag, [P, 2, 512], F32) as ps_t, \
                    nc.psum_tensor("ps_1" + tag, [P, 2, 512], F32) as ps_1, \
                    nc.psum_tensor("ps_2" + tag, [P, 2, 512], F32) as ps_2, \
                    nc.psum_tensor("ps_3" + tag, [P, 512], F32) as ps_3:
                slots, cols = (UB, UN) if last else (2 * EVEN, EVEN * P)
                bufs = [share((P, slots, width), (P, cols), (P, UN), (P, UN), (P, UB, F), (P, 4, UB),
                              start=c * MLP_BYTES) for c in range(2)]
                into, into_t, hid_1, hid_2, res, sums = zip(*bufs)
                taken, kept, turned, copied = (sem(n + tag) for n in ("m_taken", "m_kept", "m_turned", "m_copied"))
                one, one_act, two, two_act = (sem(n + tag) for n in ("m_one", "m_one_act", "m_two", "m_two_act"))
                three, biased = (sem(n + tag) for n in ("m_three", "m_biased"))
                halves = ((0, 512), (512, UN))

                def layer(ps, w, src):
                    for c, (lo, up) in enumerate(halves):
                        mm = nc.tensor.matmul(ps[:, c, 0:up - lo], w[:, :], src[:, lo:up], start=True, stop=True)
                    return mm

                def stacked_layer(ps, w, src):
                    for h, n in enumerate((EVEN, UB - EVEN)):
                        mm = nc.tensor.matmul(ps[:, h, 0:n * P], w[:, h, :], src[:, 0:n * P], start=True, stop=True)
                    return mm

                def at(k):
                    return P * k if last else place(k)

                def whole(ps, n=UN):
                    return ps[:, :, :].rearrange("p a b -> p (a b)")[:, 0:n]

                def unit(t, u):
                    return t[:, bass.ds(UB * u, UB), :]

                if last:
                    centred, squared, var_made, std_made, finished, stored, step_l = (
                        sem("l_" + n) for n in ("centred", "squared", "var_made", "std_made", "finished", "stored",
                                                "step"))
                    step_v, step_r = sem("l_step_v"), sem("l_step_r")
                else:
                    var_made, std_made, step_l = sem("n_var_made"), sem("n_std_made"), sem("n_step")
                    padded = sem("n_padded")

                with nc.Block() as block:
                    @block.gpsimd
                    def _(pool):
                        def take(u, c):
                            wait_past(pool, turned, u - 1)
                            nc.gpsimd.tensor_copy(into[c][:, :, F:2 * F], unit(Hf, u))
                            nc.gpsimd.tensor_copy(into[c][:, :, 0:F], unit(X, u)).then_inc(taken, 1)

                        def keep(u, c):
                            pool.wait_ge(taken, u + 1)
                            nc.gpsimd.tensor_copy(unit(X, u), into[c][:, 0:UB, :]).then_inc(kept, 1)

                        stagger(pool, [(0, take if last else keep)], UNITS)

                    @block.tensor
                    def _(pe):
                        def turn(u, c):
                            wait_apart(pe, (taken, u + 1), *([(copied, u)] if not isinstance(u, int) or u else []))
                            for k in range(UB if last else EVEN):
                                what = into[c][:, k, :] if last else \
                                    into[c][:, 2 * k:2 * k + 2, :].rearrange("p j f -> p (j f)")
                                mm = nc.tensor.transpose(ps_t[:, k // 4, k % 4 * P:k % 4 * P + P], what, ident[:, :])
                            mm.then_inc(turned, 1)

                        def first(u, c):
                            pe.wait_ge(copied, u + 1)
                            wait_past(pe, one_act, u)
                            (layer if last else stacked_layer)(ps_1, w1, into_t[c]).then_inc(one, 1)

                        def second(u, c):
                            pe.wait_ge(one_act, u + 1)
                            wait_past(pe, two_act, u)
                            layer(ps_2, w2, hid_1[c]).then_inc(two, 1)

                        def third(u, c):
                            pe.wait_ge(two_act, u + 1)
                            wait_past(pe, biased, u)
                            for k in range(UB):
                                mm = nc.tensor.matmul(ps_3[:, F * k:F * k + F], hid_2[c][:, at(k):at(k) + P], w3[:, :],
                                                      start=True, stop=True)
                            mm.then_inc(three, 1)

                        if not last:
                            pe.wait_ge(padded, 2)
                        stagger(pe, [(4, third), (0, turn), (2, second), (1, first)], UNITS)

                    @block.scalar
                    def _(act):
                        def copy(u, c):
                            act.wait_ge(turned, u + 1)
                            wait_past(act, one, u - 1)
                            nc.scalar.activation(into_t[c], whole(ps_t, cols), ACT.Copy).then_inc(copied, 1)

                        def relu(u, c):
                            act.wait_ge(one, u + 1)
                            wait_past(act, two, u - 1)
                            nc.scalar.activation(hid_1[c], whole(ps_1), ACT.Relu,
                                                 bias=b_hid[:, hb:hb + 1]).then_inc(one_act, 1)

                        def square(u, c):
                            act.wait_ge(centred, u + 1)
                            nc.scalar.activation(res[c], unit(X, u), ACT.Square).then_inc(squared, 1)

                        def root(u, c):
                            act.wait_ge(var_made, u + 1)
                            nc.scalar.activation(sums[c][:, 2, :], sums[c][:, 1, :], ACT.Sqrt).then_inc(std_made, 1)

                        if not last:
                            act.wait_ge(var_made, 1)
                            nc.scalar.activation(stat[:, 2, :], stat[:, 0, :], ACT.Sqrt).then_inc(std_made, 1)
                        stagger(act, [(1, copy), (2, relu)] + ([(6, root), (5, square)] if last else []), UNITS)

                    @block.vector
                    def _(dve):
                        def norm(u, c):
                            wait_past(dve, turned, u - 1)
                            wait_past(dve, kept, u - 1)
                            nc.vector.tensor_tensor(into[c][:, 0:UB, :], unit(X, u), over(stat[:, 1, bass.ds(UB * u, UB)]),
                                                    ALU.mult).then_inc(taken, 1)

                        def relu(u, c):
                            dve.wait_ge(two, u + 1)
                            wait_past(dve, three, u - 1)
                            nc.vector.tensor_scalar(hid_2[c], whole(ps_2), b_hid[:, hb + 1:hb + 2], 0.0, ALU.add,
                                                    ALU.max).then_inc(two_act, 1)

                        def leave(u, c):
                            dve.wait_ge(three, u + 1)
                            if last:
                                wait_past(dve, finished, u - 1)
                            to = res[c] if last else unit(Hf, u)
                            nc.vector.tensor_tensor(to, ps_3[:, 0:UB * F].rearrange("p (j f) -> p j f", f=F),
                                                    each(b3, UB), ALU.add).then_inc(biased, 1)
                            dve.wait_ge(biased, u + 1)
                            if not last:
                                nc.vector.tensor_reduce(tops[:, bass.ds(u, 1)], to.rearrange("p j f -> p (j f)"), AX,
                                                        ALU.max, apply_absolute_value=True)
                                return
                            chain = Chain(dve, step_l, 2 * u)
                            chain.link(nc.vector.tensor_tensor(res[c], res[c], unit(X, u), ALU.add))
                            chain.link(nc.vector.tensor_reduce(sums[c][:, 0, :], res[c], AX, ALU.add))
                            nc.vector.scalar_tensor_tensor(unit(X, u), over(sums[c][:, 0, :]), -1.0 / F, res[c],
                                                           ALU.mult, ALU.add).then_inc(centred, 1)

                        def variance(u, c):
                            chain = Chain(dve, step_v, u)
                            dve.wait_ge(squared, u + 1)
                            chain.link(nc.vector.tensor_reduce(sums[c][:, 3, :], res[c], AX, ALU.add))
                            nc.vector.tensor_scalar(sums[c][:, 1, :], sums[c][:, 3, :], 1.0 / F, EPS, ALU.mult,
                                                    ALU.add).then_inc(var_made, 1)

                        def normed(u, c):
                            chain = Chain(dve, step_r, u)
                            dve.wait_ge(std_made, u + 1)
                            chain.link(nc.vector.reciprocal(sums[c][:, 0, :], sums[c][:, 2, :]))
                            nc.vector.tensor_tensor(unit(X, u), unit(X, u), over(sums[c][:, 0, :]),
                                                    ALU.mult).then_inc(finished, 1)

                        if last:
                            stagger(dve, [(3, relu), (6, normed), (4, leave), (5, variance)], UNITS)
                        else:
                            chain = Chain(dve, step_l)
                            for c in range(2):
                                nc.vector.memset(into[c][:, UB:slots, :], 0.0).then_inc(padded, 1)
                            nc.vector.tensor_scalar(stat[:, 0, :], stat[:, 1, :], 1.0 / F, EPS, ALU.mult,
                                                    ALU.add).then_inc(var_made, 1)
                            dve.wait_ge(std_made, 1)
                            chain.link(nc.vector.reciprocal(stat[:, 1, :], stat[:, 2, :]))
                            stagger(dve, [(0, norm), (3, relu), (4, leave)], UNITS)

                    if last:
                        full = out[0:(NB - 1) * P, :].rearrange("(j p) f -> p j f", p=P)

                        @block.sync
                        def _(sp):
                            def store(u, blocks):
                                wait_apart(sp, (finished, u + 1))
                                sp.dma_start(full[:, bass.ds(UB * u, blocks), :],
                                             X[:, bass.ds(UB * u, blocks), :]).then_inc(stored, 16)

                            store(0, UB)
                            with sp.Fori(1, UNITS - 1) as u:
                                store(u, UB)
                            store(UNITS - 1, UB - 1)
                            sp.dma_start(out[(NB - 1) * P:NODES, :], X[0:LAST, NB - 1, :]).then_inc(stored, 16)
                            sp.wait_ge(stored, 16 * (UNITS + 1))

        prepare()
        general = nc.alloc_registers("general")
        nc.regs_load(general, flag[0:1, 0:1])
        with nc.If_ne(general, 0):
            nc.all_engine_barrier()
            general_degrees()
        normalise()
        with nc.If_ne(general, 0):
            nc.all_engine_barrier()
            general_sum("_g1", True)
        with nc.Else():
            nc.all_engine_barrier()
            two_parts("_1", None)
            first_sum()
        gcn_dense()
        finish = Finish()
        with nc.If_ne(general, 0):
            nc.all_engine_barrier()
            general_sum("_g2", True)
            finish.alone()
        with nc.Else():
            nc.all_engine_barrier()
            loaded = [sem(f"counts_loaded{b}_2") for b in range(3)]
            two_parts("_2", loaded)
            later_sum("_2", finish, loaded)
        mlp("_m", F, wm1, wm2, wm3, 0, b_m3, False)
        with nc.If_ne(general, 0):
            nc.all_engine_barrier()
            general_sum("_g3", False)
        with nc.Else():
            nc.all_engine_barrier()
            loaded = [sem(f"counts_loaded{b}_3") for b in range(3)]
            two_parts("_3", loaded)
            later_sum("_3", None, loaded)
        mlp("_u", 2 * F, wu1, wu2, wu3, 2, b_u3, True)


WEIGHTS = ["L0_gnn_W_nuc", "L0_gnn_b_nuc", "L0_gnn_W_surf", "L0_gnn_b_surf", "L0_gnn_W_fuse", "L0_gnn_b_fuse",
           "L1_gnn_WM1", "L1_gnn_bM1", "L1_gnn_WM2", "L1_gnn_bM2", "L1_gnn_WM3", "L1_gnn_bM3",
           "L1_gnn_WU1", "L1_gnn_bU1", "L1_gnn_WU2", "L1_gnn_bU2", "L1_gnn_WU3", "L1_gnn_bU3"]


def kernel(**inputs):
    import numpy as np
    import concourse.bacc as bacc
    from concourse.bass_utils import run_bass_kernel_spmd

    x, src, dst = (np.asarray(inputs[n]) for n in ("x", "src", "dst"))
    edges = TILES * P
    src_pad = (np.arange(edges + P) % NODES).astype(src.dtype)
    dst_pad = np.full(edges + P, PAD_DST, dst.dtype)
    src_pad[:EDGES], dst_pad[:EDGES] = src, dst
    rows = np.stack([src_pad.reshape(-1, P), dst_pad.reshape(-1, P)], axis=1)
    x_blocks = np.zeros((NB * P, F), x.dtype)
    x_blocks[:NODES] = x
    arrays = {
        "x_blocks": x_blocks,
        "src_grid": np.ascontiguousarray(src_pad[:edges].reshape(P, TILES)),
        "dst_grid": np.ascontiguousarray(dst_pad[:edges].reshape(P, TILES)),
        "row_first": np.ascontiguousarray(dst_pad[:edges:P]),
        "edge_rows": np.ascontiguousarray(np.concatenate([rows[:-1], rows[1:]], axis=1).reshape(TILES, 4 * P)),
    }
    for name in WEIGHTS:
        arrays[name.split("gnn_")[1]] = np.ascontiguousarray(inputs[name])
    nc = bacc.Bacc("TRN2", target_bir_lowering=False, num_devices=1)
    aps = {n: nc.dram_tensor(n + "_in", v.shape, mybir.dt.from_np(v.dtype), kind="ExternalInput").ap()
           for n, v in arrays.items()}
    out = nc.dram_tensor("out_dram", (NODES, F), F32, kind="ExternalOutput").ap()
    build(nc, aps, out)
    r = run_bass_kernel_spmd(nc, [{n + "_in": v for n, v in arrays.items()}], core_ids=[0])
    return r.results[0]["out_dram"]
```

```python
from contextlib import ExitStack

import concourse.bass as bass
from concourse import mybir

ALU = mybir.AluOpType
ACT = mybir.ActivationFunctionType
F32 = mybir.dt.float32
F16 = mybir.dt.float16
BF16 = mybir.dt.bfloat16
F8 = mybir.dt.float8e4
I32 = mybir.dt.int32
U32 = mybir.dt.uint32
U8 = mybir.dt.uint8
AX = mybir.AxisListType.X

P = 128
NODES = 12500
EDGES = 212500
F = 64
H = 128
NB = -(-NODES // P)
LAST = NODES - (NB - 1) * P
TILES = 1664
WN = 4
WB = P // WN
NBW = -(-NB // 4) * 4
GROUPS = NBW * WB // P
GC = 5
KEYS = NB * WN
PAD_DST = 16383
SINK = PAD_DST + 1
SUMROWS = SINK + P
DP = 2 * P
NP = NB // 2
PW = 2 * WB
MAXCOUNT = 16
REACH = 12
NEAR = MAXCOUNT - (P - 1 - MAXCOUNT) // REACH
EXP1 = 1 << 23
FAR = float(1 << 22)
MIDDLE = (WN - 1) / 2
UB = 7
UNITS = NB // UB
UN = UB * P
EVEN = (UB + 1) // 2
MLP_BYTES = 4 * (UB * F + 4 * UN + 4 * UB)
GCN_BYTES = 4 * (2 * EVEN * F + EVEN * P + 4 * UN)
EPS = 1e-5


class Chain:

    def __init__(self, eng, sem, base=0):
        self.eng, self.sem, self.base, self.n = eng, sem, base, 0

    def link(self, ins):
        self.n += 1
        ins.then_inc(self.sem, 1)
        self.eng.wait_ge(self.sem, self.base + self.n)


def stagger(eng, stages, count):
    depth = max(k for k, _ in stages)
    early = (depth + 3) // 2 * 2

    def step(s, odd, low, high):
        for k, body in stages:
            if low <= k <= high:
                body(s - k, (odd - k) % 2)

    for s in range(early):
        step(s, s % 2, 0, s)
    with eng.Fori(early // 2, count // 2) as i:
        for odd in range(2):
            step(2 * i + odd, odd, 0, depth)
    for s in range(count, count + depth):
        step(s, s % 2, s - count + 1, depth)


def wait_apart(eng, *waits):
    for _, value in waits:
        eng.compute_val(value)
    eng.wait_ge(waits[0][0], 1)
    for sem, value in waits:
        eng.wait_ge(sem, value)


def wait_past(eng, sem, value):
    if not (isinstance(value, int) and value < 1):
        eng.wait_ge(sem, value)


def place(k):
    return P * (k // 2 + k % 2 * EVEN)


def over(col):
    return col.unsqueeze(2).broadcast_to((P, col.shape[1], F))


def each(row, blocks):
    return row[:, :].unsqueeze(1).broadcast_to((P, blocks, F))


def build(nc, a, out):
    with ExitStack() as ctx:
        def sb(name, shape, dt):
            return ctx.enter_context(nc.sbuf_tensor(name, shape, dt))

        def sem(name):
            return ctx.enter_context(nc.semaphore(name))

        counts_dram = nc.dram_tensor("counts_dram", (NP, P, NB * DP), U8).ap()
        feat_dram = nc.dram_tensor("feat_dram", (NB * P, F), F32).ap()
        sum_dram = nc.dram_tensor("sum_dram", (SUMROWS, F), F32).ap()

        X = sb("X", [P, NB, F], F32)
        Hf = sb("Hf", [P, NB, F], F32)
        HL = sb("HL", [P, NB, 2 * F], F16)
        region = sb("region", [P, 3, NB * DP], U8)
        keyT = sb("keyT", [P, GROUPS * P], F32)
        loT = sb("loT", [P, GROUPS * P], F16)
        deg = sb("deg", [P, NBW], F32)
        dinv = sb("dinv", [P, NB], F32)
        stat = sb("stat", [P, 3, NB], F32)
        ident = sb("ident", [P, P], F32)
        ones = sb("ones", [P, P], F32)
        iota_k = sb("iota_k", [P, KEYS], F16)
        stack = sb("stack", [P, F], F32)
        scales = sb("scales", [P, 2], F32)
        tops = sb("tops", [P, UNITS], F32)
        top = sb("top", [P, 1], F32)
        bits = sb("bits", [1, 5], I32)
        soft = sb("soft", [P, 3, 2, F], F32)
        soft_sums = sb("soft_sums", [P, 3, 4, 2], F32)
        merge = sb("merge", [P, F], F32)
        flag = sb("flag", [1, 1], I32)
        w_fuse = sb("w_fuse", [P, 2, F], F32)
        w_gcn = sb("w_gcn", [P, 2, 2 * H], F32)
        b_gcn = sb("b_gcn", [P, 2], F32)
        b_fuse = sb("b_fuse", [P, F], F32)
        wm1 = sb("wm1", [P, 2, H], F32)
        wm2 = sb("wm2", [H, H], F32)
        wm3 = sb("wm3", [H, F], F32)
        wu1 = sb("wu1", [2 * F, H], F32)
        wu2 = sb("wu2", [H, H], F32)
        wu3 = sb("wu3", [H, F], F32)
        b_hid = sb("b_hid", [P, 4], F32)
        b_m3 = sb("b_m3", [P, F], F32)
        b_u3 = sb("b_u3", [P, F], F32)

        counts8 = [region[:, b, :].bitcast(F8).rearrange("p (h d) -> p h d", d=DP) for b in range(3)]
        flat = region[:, :, :].rearrange("p a b -> p (a b)")

        def scratch(at, n, dt):
            return flat[:, at:at + 4 * n].bitcast(dt)

        def share(*shapes, start=0):
            at, views = start, []
            for rows, *dims in shapes:
                n = 1
                for d in dims:
                    n *= d
                view = scratch(at, n, F32)[0:rows, :]
                if len(dims) == 2:
                    view = view.rearrange("p (a b) -> p a b", b=dims[1])
                views.append(view)
                at += 4 * n
            return views

        x_blocks = a["x_blocks"].rearrange("(j p) f -> p j f", p=P)
        feat_blocks = feat_dram.rearrange("(j p) f -> p j f", p=P)
        sum_blocks = sum_dram[0:NB * P, :].rearrange("(j p) f -> p j f", p=P)

        iota_i = Hf[:, 0:7, :].bitcast(I32).rearrange("p a b -> p (a b)")
        tri_i = Hf[:, 7:9, :].bitcast(I32).rearrange("p a b -> p (a b)")
        sel_i = Hf[:, 9:11, :].bitcast(I32).rearrange("p a b -> p (a b)")
        base_i = Hf[:, 11:12, 0:GROUPS].bitcast(I32).rearrange("p a b -> p (a b)")
        before = sb("before", [P, P], F32)
        first = sb("first", [P, GROUPS], F32)
        less = sb("less", [P, 3, GROUPS], F32)
        trash = sb("trash", [P, 1], F32)
        LANES = 4
        iota_l = sb("iota_l", [P, P, LANES], F16)

        def prepare():
            loads = [(w_fuse[:, 0, :], a["W_fuse"][0:P, :]), (w_fuse[:, 1, :], a["W_fuse"][P:2 * P, :]),
                     (w_gcn[0:32, 0, 0:H], a["W_nuc"]), (w_gcn[32:64, 0, H:2 * H], a["W_surf"]),
                     (w_gcn[64:96, 1, 0:H], a["W_nuc"]), (w_gcn[96:128, 1, H:2 * H], a["W_surf"]),
                     (wm1[0:F, 0, :], a["WM1"]), (wm1[F:P, 1, :], a["WM1"]), (wm2[:, :], a["WM2"]), (wm3[:, :], a["WM3"]),
                     (wu1[:, :], a["WU1"]), (wu2[:, :], a["WU2"]), (wu3[:, :], a["WU3"])]
            columns = [(b_gcn[:, 0:1], "b_nuc"), (b_gcn[:, 1:2], "b_surf"), (b_hid[:, 0:1], "bM1"),
                       (b_hid[:, 1:2], "bM2"), (b_hid[:, 2:3], "bU1"), (b_hid[:, 3:4], "bU2")]
            rows = [(b_fuse, "b_fuse"), (b_m3, "bM3"), (b_u3, "bU3")]
            CHUNKS = GROUPS // GC
            DVE_GC = 1
            N = GC * P
            row_i = scratch(0, TILES, I32)
            row_f = scratch(4 * TILES, TILES, F32)
            below = scratch(8 * TILES, TILES // 2, F32).bitcast(BF16)
            signs = scratch(10 * TILES, TILES // 2, F32).bitcast(BF16)
            code_i = scratch(12 * TILES, N, I32).rearrange("p (g e) -> p g e", g=GC)
            low_half = scratch(12 * TILES, N, F32).bitcast(mybir.dt.uint16) \
                .rearrange("p (g e h) -> p g e h", g=GC, h=2)[:, :, :, 0]
            at = 12 * TILES + 4 * N
            got = [scratch(at + c * 4 * 4 * N, 4 * N, I32).rearrange("p (g r e) -> p g r e", g=GC, r=4)
                   for c in range(2)]
            at += 32 * N
            spare = Hf[:, 36:36 + 4 * N // F, :].rearrange("p a b -> p (a b)")
            rels = [t.rearrange("p (g r e) -> p g r e", g=GC, r=2)
                    for t in (scratch(at, 2 * N, F32), spare[:, 0:2 * N])]
            pens = [t.rearrange("p (g r e) -> p g r e", g=GC, r=2)
                    for t in (scratch(at + 8 * N, 2 * N, F32), spare[:, 2 * N:4 * N])]
            low_i = scratch(at + 16 * N, 2 * N, I32).rearrange("p (g r e) -> p g r e", g=GC, r=2)
            at += 24 * N
            select = scratch(at, 8 * P, F32).bitcast(BF16).rearrange("p (k e) -> p k e", e=P)
            at += 32 * P
            masks = scratch(at, 2 * N, F32).bitcast(BF16).rearrange("p (k m) -> p k m", k=WN)
            code = Hf[:, 16:16 + 2 * 2 * GC, :].rearrange("p (c g a) b -> p c g (a b)", c=2, g=GC)
            parts = HL[:, :, :].rearrange("p a b -> p (a b)")
            same = parts[:, 0:REACH * N].bitcast(BF16).rearrange("p (t g e) -> p t g e", t=REACH, g=GC)
            code_16 = parts[:, REACH * N:(REACH + 1) * N].bitcast(mybir.dt.uint16) \
                .rearrange("p (g e) -> p g e", g=GC)
            with nc.psum_tensor("ps_key", [P, 2, 2, 512], F32) as ps_key, \
                    nc.psum_tensor("ps_win", [P, 512], F32) as ps_win, \
                    nc.psum_tensor("ps_deg", [P, 512], F32) as ps_deg, \
                    nc.psum_tensor("ps_bad", [P, 512], F32) as ps_bad, \
                    nc.sbuf_tensor("rows_below", [P, GROUPS], F32) as rows_below, \
                    nc.sbuf_tensor("win_deg", [P, GROUPS * WN], BF16) as win_deg, \
                    nc.sbuf_tensor("ones_16", [P, 2], BF16) as ones_16, \
                    nc.sbuf_tensor("pairs", [P, GROUPS // GC], F32) as pairs, \
                    nc.sbuf_tensor("bad", [P, 3], F32) as bad, nc.sbuf_tensor("sums", [1, 4], F32) as sums, \
                    nc.sbuf_tensor("row_of", [P, GROUPS], U32) as row_of:
                rows_loaded, x_loaded, weights_loaded = sem("rows_loaded"), sem("x_loaded"), sem("weights_loaded")
                iotas_made, zeroed, ones_made = sem("iotas_made"), sem("zeroed"), sem("ones_made")
                rows_ready, step_p, first_made = sem("rows_ready"), sem("step_p"), sem("first_made")
                row_f_made, signs_summed, rel_made = (
                    sem(n) for n in ("row_f_made", "signs_summed", "rel_made"))
                ints_made, code_i_read = sem("ints_made"), sem("code_i_read")
                gathered = [sem(f"gathered{c}") for c in range(CHUNKS)]
                codes_made, turned, codes_read = sem("codes_made"), sem("turned"), sem("codes_read")
                same_made, same_read, masks_made, masks_read = (
                    sem(n) for n in ("same_made", "same_read", "masks_made", "masks_read"))
                win_ready, deg_made, bad_made, bad_summed = (
                    sem(n) for n in ("win_ready", "deg_made", "bad_made", "bad_summed"))

                with nc.Block() as block:
                    @block.sync
                    def _(sp):
                        sp.dma_start(row_i, a["row_first"].partition_broadcast(P)).then_inc(rows_loaded, 16)
                        sp.wait_ge(zeroed, 2)
                        sp.wait_ge(gathered[1], 16 * GC)
                        for to, what in loads:
                            sp.dma_start(to, what).then_inc(weights_loaded, 16)
                        for to, name in columns:
                            sp.dma_start(to, a[name].rearrange("(p o) -> p o", o=1)).then_inc(weights_loaded, 16)
                        for to, name in rows:
                            sp.dma_start(to[:, :], a[name].partition_broadcast(P)).then_inc(weights_loaded, 16)
                        sp.dma_start(X[:, :, :], x_blocks).then_inc(x_loaded, 16)
                        sp.wait_ge(x_loaded, 16)
                        sp.wait_ge(weights_loaded, 16 * (len(loads) + len(columns) + len(rows)))

                    @block.gpsimd
                    def _(pool):
                        nc.gpsimd.iota(base_i, pattern=[[WN * P, GROUPS]], base=0,
                                       channel_multiplier=WN).then_inc(iotas_made, 1)
                        nc.gpsimd.iota(iota_i[:, 0:KEYS], pattern=[[1, KEYS]], base=0,
                                       channel_multiplier=0).then_inc(iotas_made, 1)
                        nc.gpsimd.iota(tri_i[:, 0:P], pattern=[[1, P]], base=0,
                                       channel_multiplier=-1).then_inc(iotas_made, 1)
                        nc.gpsimd.iota(sel_i[:, 0:P], pattern=[[-1, P]], base=0,
                                       channel_multiplier=WN).then_inc(iotas_made, 1)
                        nc.gpsimd.memset(w_gcn[:, :, :], 0.0).then_inc(zeroed, 1)
                        nc.gpsimd.memset(wm1[:, :, :], 0.0).then_inc(zeroed, 1)
                        nc.gpsimd.memset(ones[:, :], 1.0).then_inc(ones_made, 1)
                        nc.gpsimd.memset(ones_16[:, :], 1.0).then_inc(ones_made, 1)
                        nc.gpsimd.memset(same, 0.0).then_inc(ones_made, 1)
                        for c in range(CHUNKS):
                            pool.wait_ge(rows_ready, c + 1)
                            if c >= 2:
                                pool.wait_ge(codes_made, c - 1)
                            for g in range(GC):
                                nc.gpsimd.indirect_dma_start(
                                    out=got[c % 2][:, g, :, :].rearrange("p r e -> p (r e)"), out_offset=None,
                                    in_=a["edge_rows"],
                                    in_offset=bass.IndirectOffsetOnAxis(
                                        ap=row_of[:, GC * c + g:GC * c + g + 1], axis=0)).then_inc(gathered[c], 16)

                    @block.scalar
                    def _(act):
                        act.wait_ge(first_made, 1)
                        act.wait_ge(row_f_made, 1)

                        def find_rows(c):
                            for n in range(GC * c + DVE_GC, GC * c + GC):
                                nc.scalar.activation(signs, row_f, ACT.Sign, bias=less[:, 0, n:n + 1],
                                                     accum_out=rows_below[:, n:n + 1]).then_inc(signs_summed, 1)
                                act.wait_ge(signs_summed, (GC - DVE_GC) * c + n - GC * c - DVE_GC + 1)

                        def relate(c):
                            dst = got[c % 2][:, :, 1:4:2, :]
                            rel, pen = rels[c % 2], pens[c % 2]
                            act.wait_ge(gathered[c], 16 * GC)
                            if c >= 2:
                                act.wait_ge(codes_made, c - 1)
                            for g in range(GC):
                                n = GC * c + g
                                nc.scalar.activation(pen[:, g, :, :], dst[:, g, :, :], ACT.Square,
                                                     bias=less[:, 1, n:n + 1])
                                last = nc.scalar.activation(rel[:, g, :, :], dst[:, g, :, :], ACT.Identity,
                                                            scale=float(P), bias=less[:, 2, n:n + 1])
                            last.then_inc(rel_made, 1)

                        def to_ints(c):
                            act.wait_ge(codes_made, c + 1)
                            if c:
                                act.wait_ge(code_i_read, c)
                            nc.scalar.activation(code_i, code[:, c % 2, :, :], ACT.Copy).then_inc(ints_made, 1)

                        def count_same(c):
                            act.wait_ge(same_made, c + 1)
                            nc.scalar.activation(same[:, :, :, :], same[:, :, :, :], ACT.Copy,
                                                 accum_out=pairs[:, c:c + 1]).then_inc(same_read, 1)

                        find_rows(0)
                        find_rows(1)
                        relate(0)
                        for c in range(CHUNKS):
                            to_ints(c)
                            if c + 2 < CHUNKS:
                                find_rows(c + 2)
                            if c + 1 < CHUNKS:
                                relate(c + 1)
                            count_same(c)

                    @block.tensor
                    def _(pe):
                        for c in range(CHUNKS):
                            pe.wait_ge(codes_made, c + 1)
                            if c >= 2:
                                pe.wait_ge(codes_read, c - 1)
                            for g in range(GC):
                                last = nc.tensor.transpose(
                                    ps_key[:, c % 2, g // 4, g % 4 * P:g % 4 * P + P], code[:, c % 2, g, :],
                                    ident[:, :])
                            last.then_inc(turned, 1)
                            pe.wait_ge(masks_made, c + 1)
                            if c == 0:
                                pe.wait_ge(ones_made, 2)
                            for g in range(GC):
                                for k in range(WN):
                                    col = WN * (GC * c + g) + k
                                    last = nc.tensor.matmul(ps_win[:, col:col + 1], masks[:, k, P * g:P * g + P],
                                                            ones_16[:, 0:1], start=True, stop=True)
                            last.then_inc(masks_read, 1)
                        pe.wait_ge(win_ready, 1)
                        by_place = win_deg[:, :].rearrange("p (g k) -> p k g", k=WN)
                        for q in range(4):
                            for k in range(WN):
                                last = nc.tensor.matmul(ps_deg[:, 32 * q:32 * q + GROUPS], select[:, 4 * q + k, :],
                                                        by_place[:, k, :], start=k == 0, stop=k == WN - 1)
                        last.then_inc(deg_made, 1)
                        pe.wait_ge(bad_made, 1)
                        nc.tensor.matmul(ps_bad[:, 0:2], ones[:, :], bad[:, 0:2], start=True,
                                         stop=True).then_inc(bad_summed, 1)

                    @block.vector
                    def _(dve):
                        chain = Chain(dve, step_p)
                        dve.wait_ge(iotas_made, 4)
                        nc.vector.tensor_scalar(less[:, 0, :], base_i, -1.0, 0.5, ALU.mult, ALU.add)
                        nc.vector.tensor_scalar(less[:, 1, :], base_i, -1.0, -MIDDLE, ALU.mult, ALU.add)
                        nc.vector.tensor_scalar(less[:, 2, :], base_i, -float(P), -MIDDLE * P, ALU.mult, ALU.add)
                        nc.vector.tensor_scalar(trash[:, :], base_i[:, 0:1], 1.0 / WN, float(SINK), ALU.mult, ALU.add)
                        nc.vector.tensor_copy(first[:, :], base_i).then_inc(first_made, 1)
                        dve.wait_ge(rows_loaded, 16)
                        nc.vector.tensor_copy(row_f, row_i).then_inc(row_f_made, 1)
                        dve.wait_ge(row_f_made, 1)

                        def find_rows(c):
                            for n in range(GC * c, GC * c + DVE_GC):
                                chain.link(nc.vector.tensor_scalar(below, row_f, first[:, n:n + 1], 0.0, ALU.is_lt,
                                                                   ALU.add, accum_out=rows_below[:, n:n + 1]))

                        def locate_rows(c):
                            dve.wait_ge(signs_summed, (GC - DVE_GC) * (c + 1))
                            signed = rows_below[:, GC * c + DVE_GC:GC * c + GC]
                            chain.link(nc.vector.tensor_scalar(signed, signed, -0.5, TILES / 2.0, ALU.mult, ALU.add))
                            own = slice(GC * c, GC * c + GC)
                            nc.vector.tensor_scalar(row_of[:, own], rows_below[:, own], -1.0, 0.0, ALU.add,
                                                    ALU.max).then_inc(rows_ready, 1)

                        def make_codes(c):
                            src = got[c % 2][:, :, 0:4:2, :]
                            rel, pen = rels[c % 2], pens[c % 2]
                            dve.wait_ge(gathered[c], 16 * GC)
                            chain.link(nc.vector.tensor_scalar(low_i, src, 127, None, ALU.bitwise_and))
                            dve.wait_ge(rel_made, c + 1)
                            chain.link(nc.vector.tensor_scalar(pen[:, :, :, :], pen[:, :, :, :], MIDDLE * MIDDLE, FAR,
                                                               ALU.is_gt, ALU.mult))
                            chain.link(nc.vector.tensor_tensor(rel[:, :, :, :], rel[:, :, :, :], pen[:, :, :, :],
                                                               ALU.add))
                            chain.link(nc.vector.scalar_tensor_tensor(rel[:, :, :, :], low_i, -(WN - 1.0),
                                                                      rel[:, :, :, :], ALU.mult, ALU.add))
                            chain.link(nc.vector.scalar_tensor_tensor(rel[:, :, :, :], src, float(WN),
                                                                      rel[:, :, :, :], ALU.mult, ALU.add))
                            nc.vector.tensor_tensor(code[:, c % 2, :, :], rel[:, :, 0, :], rel[:, :, 1, :],
                                                    ALU.min).then_inc(codes_made, 1)
                            dve.wait_ge(codes_made, c + 1)

                        def compare_codes(c):
                            if c == 0:
                                dve.wait_ge(ones_made, 3)
                            dve.wait_ge(ints_made, c + 1)
                            nc.vector.tensor_copy(code_16, low_half).then_inc(code_i_read, 1)
                            dve.wait_ge(code_i_read, c + 1)
                            if c:
                                dve.wait_ge(same_read, c)
                            for t in range(REACH):
                                last = nc.vector.tensor_tensor(same[:, t, :, 0:P - 1 - t],
                                                               code_16[:, :, 0:P - 1 - t],
                                                               code_16[:, :, t + 1:P], ALU.is_equal)
                            last.then_inc(same_made, 1)

                        def split_codes(c):
                            to = slice(N * c, N * c + N)
                            dve.wait_ge(turned, c + 1)
                            ci = low_i.rearrange("p g r e -> p (g r e)")
                            for h, n in ((0, 4), (1, GC - 4)):
                                last = nc.vector.tensor_scalar(ci[:, 4 * P * h:4 * P * h + n * P],
                                                               ps_key[:, c % 2, h, 0:n * P], MIDDLE * P, None,
                                                               ALU.add)
                            last.then_inc(codes_read, 1)
                            dve.wait_ge(codes_read, c + 1)
                            cj = ci[:, N:2 * N]
                            ci = ci[:, 0:N]
                            chain.link(nc.vector.tensor_scalar(cj, ci, 127, None, ALU.bitwise_and))
                            chain.link(nc.vector.tensor_copy(loT[:, to], cj))
                            chain.link(nc.vector.tensor_scalar(cj, ci, 7, None, ALU.logical_shift_right))
                            nc.vector.tensor_copy(keyT[:, to], cj)
                            chain.link(nc.vector.tensor_scalar(ci, cj, -1 - (P * WN - WN), None, ALU.bitwise_and))
                            if c:
                                dve.wait_ge(masks_read, c)
                            for k in range(WN):
                                last = nc.vector.tensor_scalar(masks[:, k, :], ci, float(k), None, ALU.is_equal)
                            last.then_inc(masks_made, 1)
                            dve.wait_ge(masks_made, c + 1)

                        find_rows(0)
                        find_rows(1)
                        locate_rows(0)
                        nc.vector.tensor_copy(iota_k[:, :], iota_i[:, 0:KEYS])
                        for q in range(LANES):
                            nc.vector.tensor_copy(iota_l[:, :, q], iota_i[:, 0:P])
                        chain.link(nc.vector.tensor_scalar(ident[:, :], tri_i[:, 0:P], 0.0, None, ALU.is_equal))
                        nc.vector.tensor_tensor(stack[:, :], ident[:, 0:F], ident[:, F:2 * F], ALU.add)
                        nc.vector.tensor_scalar(before[:, :], tri_i[:, 0:P], 0.0, None, ALU.is_lt)
                        locate_rows(1)
                        for q in range(4):
                            for k in range(WN):
                                chain.link(nc.vector.tensor_scalar(select[:, 4 * q + k, :], sel_i[:, 0:P],
                                                                   float(P * q - k), None, ALU.is_equal))
                        for c in range(CHUNKS):
                            make_codes(c)
                            if c + 2 < CHUNKS:
                                find_rows(c + 2)
                            split_codes(c)
                            if c + 2 < CHUNKS:
                                locate_rows(c + 2)
                            compare_codes(c)

                        dve.wait_ge(masks_read, CHUNKS)
                        nc.vector.tensor_copy(win_deg[:, :], ps_win[:, 0:GROUPS * WN]).then_inc(win_ready, 1)
                        dve.wait_ge(x_loaded, 16)
                        for u in range(UNITS):
                            nc.vector.tensor_reduce(
                                tops[:, u:u + 1], X[:, UB * u:UB * u + UB, :].rearrange("p a b -> p (a b)"), AX,
                                ALU.max, apply_absolute_value=True)
                        dve.wait_ge(deg_made, 1)
                        chain.link(nc.vector.tensor_copy(
                            deg[:, :].rearrange("p (g q) -> p q g", q=4),
                            ps_deg[:, 0:P].rearrange("p (q g) -> p q g", q=4)[:, :, 0:GROUPS]))
                        chain.link(nc.vector.tensor_reduce(bad[:, 0:1], deg[:, :], AX, ALU.add))
                        dve.wait_ge(same_read, CHUNKS)
                        chain.link(nc.vector.tensor_reduce(bad[:, 2:3], pairs[:, :], AX, ALU.max))
                        nc.vector.tensor_scalar(bad[:, 1:2], bad[:, 2:3], NEAR - 0.5, None,
                                                ALU.is_gt).then_inc(bad_made, 1)
                        dve.wait_ge(bad_summed, 1)
                        chain.link(nc.vector.tensor_copy(sums[:, 0:2], ps_bad[0:1, 0:2]))
                        chain.link(nc.vector.tensor_scalar(sums[:, 2:3], sums[:, 0:1], float(EDGES), None,
                                                           ALU.not_equal))
                        chain.link(nc.vector.tensor_tensor(sums[:, 3:4], sums[:, 1:2], sums[:, 2:3], ALU.add))
                        chain.link(nc.vector.tensor_copy(flag[:, :], sums[:, 3:4]))

        def general_degrees():
            dst_i = scratch(0, TILES, I32)
            lo_i = scratch(4 * TILES, TILES, I32)
            lo_f = scratch(8 * TILES, TILES, F32)
            hi_f = scratch(12 * TILES, TILES, F32)
            at = 16 * TILES
            hot_lo = scratch(at, 8 * P, F32).bitcast(BF16).rearrange("p (s n) -> p s n", s=16)
            hot_hi = scratch(at + 32 * P, 8 * NBW, F32).bitcast(BF16).rearrange("p (s n) -> p s n", s=16)
            dst_loaded, hot_made, hot_used, step_d = (sem(n) for n in ("dst_loaded", "hot_made", "hot_used", "step_d"))
            with nc.psum_tensor("ps_all", [P, 512], F32) as ps_all:
                with nc.Block() as block:
                    @block.sync
                    def _(sp):
                        sp.dma_start(dst_i, a["dst_grid"]).then_inc(dst_loaded, 16)

                    @block.vector
                    def _(dve):
                        chain = Chain(dve, step_d)
                        dve.wait_ge(dst_loaded, 16)
                        chain.link(nc.vector.tensor_scalar(lo_i, dst_i, 127, None, ALU.bitwise_and))
                        chain.link(nc.vector.tensor_copy(lo_f, lo_i))
                        chain.link(nc.vector.tensor_scalar(lo_i, dst_i, 7, None, ALU.logical_shift_right))
                        chain.link(nc.vector.tensor_copy(hi_f, lo_i))

                        def one_hots(i, begin):
                            for g in range(4):
                                if not begin:
                                    dve.wait_ge(hot_used, 4 * i + g - 3)
                                for s in range(4 * g, 4 * g + 4):
                                    col = 16 * i + s
                                    nc.vector.tensor_scalar(hot_lo[:, s, :], iota_k[:, 0:P],
                                                            lo_f[:, bass.ds(col, 1)], None, ALU.is_equal)
                                    last = nc.vector.tensor_scalar(hot_hi[:, s, :], iota_k[:, 0:NBW],
                                                                   hi_f[:, bass.ds(col, 1)], None, ALU.is_equal)
                                last.then_inc(hot_made, 1)

                        one_hots(0, True)
                        with dve.Fori(1, TILES // 16) as i:
                            one_hots(i, False)
                        dve.wait_ge(hot_used, TILES // 4)
                        nc.vector.tensor_copy(deg[:, :], ps_all[:, 0:NBW])

                    @block.tensor
                    def _(pe):
                        def count(i, begin, end):
                            for g in range(4):
                                pe.wait_ge(hot_made, 4 * i + g + 1)
                                for s in range(4 * g, 4 * g + 4):
                                    mm = nc.tensor.matmul(ps_all[:, 0:NBW], hot_lo[:, s, :], hot_hi[:, s, :],
                                                          start=begin and s == 0, stop=end and s == 15,
                                                          skip_group_check=True)
                                mm.then_inc(hot_used, 1)

                        count(0, True, False)
                        with pe.Fori(1, TILES // 16 - 1) as i:
                            count(i, False, False)
                        count(TILES // 16 - 1, False, True)

        def normalise():
            SPLIT = NB * 2 // 3
            var_ready, std_ready, dinv_made = sem("var_ready"), sem("std_ready"), sem("dinv_made")
            with nc.Block() as block:
                @block.scalar
                def _(act):
                    act.wait_ge(var_ready, 1)
                    nc.scalar.activation(stat[:, 1, :], stat[:, 0, :], ACT.Sqrt).then_inc(std_ready, 1)

                @block.vector
                def _(dve):
                    nc.vector.tensor_scalar(stat[:, 0, :], deg[:, 0:NB], 1.0, None, ALU.add).then_inc(var_ready, 1)
                    dve.wait_ge(std_ready, 1)
                    nc.vector.reciprocal(dinv[:, :], stat[:, 1, :]).then_inc(dinv_made, 1)
                    dve.wait_ge(dinv_made, 1)
                    nc.vector.tensor_tensor(Hf[:, 0:SPLIT, :], X[:, 0:SPLIT, :], over(dinv[:, 0:SPLIT]), ALU.mult)

                @block.gpsimd
                def _(pool):
                    pool.wait_ge(dinv_made, 1)
                    nc.gpsimd.tensor_tensor(Hf[:, SPLIT:NB, :], X[:, SPLIT:NB, :], over(dinv[:, SPLIT:NB]), ALU.mult)

        def load_pair(sp, j, b, loaded):
            sp.dma_start(region[:, b, :], counts_dram[bass.ds(j, 1), :, :].rearrange("o p n -> (o p) n")) \
                .then_inc(loaded[b], 16)

        class Parts:
            CUT = 2 * UB

            def __init__(self, tag, ps_max, ps_pow):
                self.worst, self.spread, self.powers, self.sent, self.hi_made, self.low_made = (
                    sem(n + tag) for n in ("worst", "spread", "powers", "sent", "hi", "low"))
                self.step = sem("step_t" + tag)
                self.ps_max, self.ps_pow = ps_max, ps_pow
                self.cuts = [slice(lo, lo + self.CUT) for lo in range(0, NB, self.CUT)]

            def tensor(self, pe):
                pe.wait_ge(self.worst, 1)
                nc.tensor.transpose(self.ps_max[0:1, 0:P], top[:, :], ident[:, :]).then_inc(self.spread, 1)
                pe.wait_ge(self.powers, 1)
                nc.tensor.matmul(self.ps_pow[:, 0:2], ones[0:1, :], bits[:, 3:5].bitcast(F32), start=True,
                                 stop=True).then_inc(self.sent, 1)

            def scalar(self, act):
                act.wait_ge(self.step, 5)
                for own in self.cuts:
                    nc.scalar.activation(HL[:, own, 0:F], Hf[:, own, :], ACT.Copy,
                                         scale=scales[:, 0:1]).then_inc(self.hi_made, 1)

            def vector(self, dve):
                chain = Chain(dve, self.step)
                nc.vector.tensor_reduce(top[:, :], tops[:, :], AX, ALU.max).then_inc(self.worst, 1)
                dve.wait_ge(self.spread, 1)
                chain.link(nc.vector.tensor_reduce(bits[:, 0:1].bitcast(F32), self.ps_max[0:1, 0:P], AX, ALU.max))
                chain.link(nc.vector.tensor_scalar(bits[:, 1:2], bits[:, 0:1], 255 * EXP1, None, ALU.bitwise_and))
                chain.link(nc.vector.tensor_scalar(bits[:, 2:3], bits[:, 1:2], 30.0 * EXP1, None, ALU.max))
                chain.link(nc.vector.tensor_scalar(bits[:, 3:4], bits[:, 2:3], -1.0, 268.0 * EXP1, ALU.mult, ALU.add))
                nc.vector.tensor_scalar(bits[:, 4:5], bits[:, 2:3], -14.0 * EXP1, None,
                                        ALU.add).then_inc(self.powers, 1)
                dve.wait_ge(self.sent, 1)
                chain.link(nc.vector.tensor_copy(scales[:, :], self.ps_pow[:, 0:2]))
                nc.vector.tensor_scalar(merge[:, :], stack[:, :], scales[:, 1:2], None, ALU.mult)
                for k, own in enumerate(self.cuts):
                    dve.wait_ge(self.hi_made, k + 1)
                    nc.vector.scalar_tensor_tensor(HL[:, own, F:2 * F], Hf[:, own, :], scales[:, 0:1],
                                                   HL[:, own, 0:F], ALU.mult, ALU.subtract).then_inc(self.low_made, 1)

        def first_parts():
            with nc.psum_tensor("ps_max", [P, 512], F32) as ps_max, nc.psum_tensor("ps_pow", [P, 512], F32) as ps_pow:
                parts = Parts("_1", ps_max, ps_pow)
                with nc.Block() as block:
                    block.tensor(parts.tensor)
                    block.scalar(parts.scalar)
                    block.vector(parts.vector)

        def every_pair(eng, body):
            for b in range(3):
                body(b, 0, b)
            with eng.Fori(1, NP // 3) as i:
                for b in range(3):
                    body(3 * i + b, i, b)
            for b in range(NP % 3):
                body(NP // 3 * 3 + b, NP // 3, b)

        def add_pair(j, sums, add):
            mine = Hf[:, bass.ds(2 * j, 2), :]
            got = sums.rearrange("p (a f) -> p a f", f=F)
            if add:
                return nc.vector.tensor_tensor(mine, mine, got, ALU.add)
            return nc.vector.tensor_copy(mine, got)

        class Finish:
            A, B = 3, 8

            def __init__(self):
                self.shifted, self.exped = sem("shifted"), sem("exped")
                self.step_a, self.step_b = sem("step_a"), sem("step_b")

            def exponent(self, act, t, b):
                act.wait_ge(self.shifted, t + 1)
                nc.scalar.activation(soft[:, b, :, :], soft[:, b, :, :], ACT.Exp).then_inc(self.exped, 1)

            def shift(self, dve, t, j, b, sums, added):
                chain = Chain(dve, self.step_a, self.A * t)
                part = soft[:, b, :, :]
                own = bass.ds(2 * j, 2)
                if sums is None:
                    nc.vector.tensor_copy(part, Hf[:, own, :]).then_inc(added, 1)
                else:
                    nc.vector.tensor_tensor(part, Hf[:, own, :], sums.rearrange("p (a f) -> p a f", f=F),
                                            ALU.add).then_inc(added, 1)
                dve.wait_ge(added, t + 1)
                chain.link(nc.vector.tensor_tensor(part, part, over(dinv[:, own]), ALU.mult))
                chain.link(nc.vector.tensor_tensor(part, part, each(b_fuse, 2), ALU.add))
                chain.link(nc.vector.tensor_reduce(soft_sums[:, b, 0, :], part, AX, ALU.max))
                nc.vector.tensor_tensor(part, part, over(soft_sums[:, b, 0, :]), ALU.subtract) \
                    .then_inc(self.shifted, 1)

            def centre(self, dve, t, j, b):
                chain = Chain(dve, self.step_b, self.B * t)
                part = soft[:, b, :, :]
                mine = X[:, bass.ds(2 * j, 2), :]
                dve.wait_ge(self.exped, t + 1)
                chain.link(nc.vector.tensor_reduce(soft_sums[:, b, 1, :], part, AX, ALU.add))
                chain.link(nc.vector.reciprocal(soft_sums[:, b, 2, :], soft_sums[:, b, 1, :]))
                chain.link(nc.vector.tensor_tensor(part, part, over(soft_sums[:, b, 2, :]), ALU.mult))
                chain.link(nc.vector.tensor_tensor(part, part, mine, ALU.add))
                chain.link(nc.vector.tensor_reduce(soft_sums[:, b, 3, :], part, AX, ALU.add))
                chain.link(nc.vector.scalar_tensor_tensor(mine, over(soft_sums[:, b, 3, :]), -1.0 / F, part,
                                                          ALU.mult, ALU.add))
                chain.link(nc.vector.tensor_tensor(part, mine, mine, ALU.mult))
                chain.link(nc.vector.tensor_reduce(stat[:, 1, bass.ds(2 * j, 2)], part, AX, ALU.add))


            def alone(self):
                added = sem("finish_added")
                with nc.Block() as block:
                    @block.scalar
                    def _(act):
                        every_pair(act, lambda j, i, b: self.exponent(act, j, b))

                    @block.vector
                    def _(dve):
                        def pair(j, i, b):
                            self.shift(dve, j, j, b, None, added)
                            self.centre(dve, j, j, b)

                        every_pair(dve, pair)

        def merge_parts(to, sums_t):
            for c in range(2):
                mm = nc.tensor.matmul(to[:, F * c:F * c + F], sums_t[:, P * c:P * c + P], merge[:, :], start=True,
                                      stop=True)
            return mm

        def first_sum():
            RING, HOTS, LAG, GAP = 3, 16, 8, 2
            SLOTS = PW - GAP
            BATCH = 16
            DUOS = PW // 2
            DVE_DUOS = [9, 25]
            BEHIND = 11
            ACT_DUOS = [k for k in range(DUOS) if k not in DVE_DUOS]
            with nc.psum_tensor("ps_cnt", [P, 2 * RING, 512], F32) as ps_cnt, \
                    nc.psum_tensor("ps_out", [P, 512], F32) as ps_out, \
                    nc.psum_tensor("ps_node", [P, 512], F32) as ps_node, \
                    nc.sbuf_tensor("hot_k", [P, HOTS, KEYS], BF16) as hot_k, \
                    nc.sbuf_tensor("hot_l", [P, 2, BATCH // LANES, P, LANES], BF16) as hot_l, \
                    nc.sbuf_tensor("win_lo", [P, PW], F16) as win_lo, \
                    nc.sbuf_tensor("win_key", [P, PW], F32) as win_key, \
                    nc.sbuf_tensor("sums_t", [P, DP], F32) as sums_t:
                cols_copied, hots_made, duos_made = sem("cols_copied"), sem("hots_made"), sem("duos_made")
                act_evicted, dve_evicted = sem("act_evicted"), sem("dve_evicted")
                stored = [sem(f"counts_stored{b}") for b in range(3)]
                summed, copied, merged, added = (
                    sem("pair_" + n) for n in ("summed", "copied", "merged", "added"))

                def duo_in(b, k):
                    r = (DUOS * b + k) % RING
                    return ps_cnt[:, 2 * r:2 * r + 2, 0:KEYS].rearrange("p w (h d) -> p w h d", d=WN)

                def duo_out(b, k):
                    return counts8[b].rearrange("p h (w d) -> p w h d", d=WN)[:, 2 * k:2 * k + 2, :, :]

                def buffer_free(eng, j, i, b):
                    wait_past(eng, stored[b], 16 * i)
                    wait_past(eng, summed, j - 2)

                with nc.Block() as block:
                    @block.sync
                    def _(sp):
                        def store(j, i, b):
                            wait_apart(sp, (act_evicted, len(ACT_DUOS) * (j + 1)),
                                       (dve_evicted, len(DVE_DUOS) * (j + 1)))
                            sp.dma_start(counts_dram[bass.ds(j, 1), :, :].rearrange("o p n -> (o p) n"),
                                         region[:, b, :]).then_inc(stored[b], 16)

                        every_pair(sp, store)
                        for b in range(3):
                            sp.wait_ge(stored[b], 16 * (NP // 3 + (b < NP % 3)))

                    @block.vector
                    def _(dve):
                        def take(j):
                            dve.wait_ge(merged, j + 1)
                            add_pair(j, ps_node[:, 0:2 * F], True).then_inc(added, 1)

                        def evict(j, b, k):
                            wait_apart(dve, (duos_made, DUOS * j + k + 1))
                            nc.vector.tensor_scalar(duo_out(b, k), duo_in(b, k), 1.0, None, ALU.mult,
                                                    saturate=False).then_inc(dve_evicted, 1)

                        def make(j, i, b):
                            early = isinstance(j, int) and j == 0
                            if not early:
                                dve.wait_ge(hots_made, PW * j)
                            nc.vector.tensor_copy(win_lo[:, :], loT[:, bass.ds(PW * j, PW)])
                            nc.vector.tensor_copy(win_key[:, :], keyT[:, bass.ds(PW * j, PW)]) \
                                .then_inc(cols_copied, 1)
                            dve.wait_ge(cols_copied, j + 1)
                            buffer_free(dve, j, i, b)
                            for k in range(PW):
                                if k % 2 == 0 and not (early and k < HOTS):
                                    dve.wait_ge(duos_made, DUOS * j + k // 2 + 1 - HOTS // 2)
                                if k % BATCH == 0:
                                    n = BATCH // LANES
                                    nc.vector.tensor_tensor(
                                        hot_l[:, k // BATCH % 2, :, :, :],
                                        win_lo[:, k:k + BATCH].rearrange("p (a q) -> p a q", q=LANES)
                                        .unsqueeze(2).broadcast_to((P, n, P, LANES)),
                                        iota_l[:, :, :].unsqueeze(1).broadcast_to((P, n, P, LANES)), ALU.is_equal)
                                nc.vector.tensor_scalar(hot_k[:, k % HOTS, :], iota_k[:, :], win_key[:, k:k + 1],
                                                        None, ALU.is_equal).then_inc(hots_made, 1)
                                if k % 2 and (k - BEHIND) // 2 in DVE_DUOS:
                                    evict(j, b, (k - BEHIND) // 2)
                                if k == PW // 2 and not (isinstance(j, int) and j < 2):
                                    take(j - 2)

                        every_pair(dve, make)
                        take(NP - 2)
                        take(NP - 1)

                    @block.scalar
                    def _(act):
                        def copy(j):
                            act.wait_ge(summed, j + 1)
                            wait_past(act, merged, j)
                            nc.scalar.activation(sums_t[:, :], ps_out[:, 0:DP], ACT.Copy).then_inc(copied, 1)

                        def evict(j, i, b):
                            buffer_free(act, j, i, b)
                            for k in ACT_DUOS:
                                if k == LAG // 2 - 1 and not (isinstance(j, int) and j < 2):
                                    copy(j - 2)
                                wait_apart(act, (duos_made, DUOS * j + k + 1))
                                nc.scalar.activation(duo_out(b, k), duo_in(b, k), ACT.Copy,
                                                     saturate=False).then_inc(act_evicted, 1)

                        every_pair(act, evict)
                        copy(NP - 2)
                        copy(NP - 1)

                    @block.tensor
                    def _(pe):
                        def wait_evicted(j, n):
                            k = n % DUOS
                            for duos, evicted in ((ACT_DUOS, act_evicted), (DVE_DUOS, dve_evicted)):
                                if k in duos:
                                    pe.wait_ge(evicted, len(duos) * (j + n // DUOS) + duos.index(k) + 1)

                        def start_sums(j):
                            taken = [] if isinstance(j, int) and j < 1 else [(copied, j)]
                            wait_apart(pe, (act_evicted, len(ACT_DUOS) * (j + 1)),
                                       (dve_evicted, len(DVE_DUOS) * (j + 1)), *taken)

                        def slot(n):
                            return range(NB * n // SLOTS, NB * (n + 1) // SLOTS)

                        def sums(j, b, part):
                            for h in part:
                                mm = nc.tensor.matmul(ps_out[:, 0:DP], HL[:, h, :], counts8[b][:, h, :],
                                                      start=h == 0, stop=h == NB - 1, skip_group_check=True)
                                if h == NB - 1:
                                    mm.then_inc(summed, 1)

                        def turn(j):
                            pe.wait_ge(copied, j + 1)
                            wait_past(pe, added, j)
                            merge_parts(ps_node, sums_t).then_inc(merged, 1)

                        def make(j, i, b):
                            early = isinstance(j, int) and j == 0
                            for k in range(PW):
                                n = k // 2
                                if k % 2 == 0 and not (early and n < RING):
                                    wait_evicted(j, n - RING)
                                pe.wait_ge(hots_made, PW * j + k + 1)
                                mm = nc.tensor.matmul(
                                    ps_cnt[:, 2 * ((DUOS * b + n) % RING) + k % 2, 0:KEYS],
                                    hot_l[:, k // BATCH % 2, k % BATCH // LANES, :, k % LANES],
                                    hot_k[:, k % HOTS, :], start=True, stop=True)
                                if k % 2:
                                    mm.then_inc(duos_made, 1)
                                if k == LAG and not early:
                                    start_sums(j - 1)
                                if k >= LAG and not early:
                                    sums(j - 1, (b - 1) % 3, slot(k - LAG))
                                if k < LAG - GAP and not (isinstance(j, int) and j < 2):
                                    sums(j - 2, (b - 2) % 3, slot(k + PW - LAG))
                                if k == LAG + 8 and not (isinstance(j, int) and j < 2):
                                    turn(j - 2)

                        every_pair(pe, make)
                        sums(NP - 2, (NP - 2) % 3, range(NB * (PW - LAG) // SLOTS, NB))
                        start_sums(NP - 1)
                        turn(NP - 2)
                        sums(NP - 1, (NP - 1) % 3, range(NB))
                        turn(NP - 1)

        def later_sum(tag, finish, held):
            with nc.psum_tensor("ps_sum" + tag, [P, 3, 512], F32) as ps_sum, \
                    nc.psum_tensor("ps_node" + tag, [P, 3, 512], F32) as ps_node, \
                    nc.psum_tensor("ps_max" + tag, [P, 512], F32) as ps_max, \
                    nc.psum_tensor("ps_pow" + tag, [P, 512], F32) as ps_pow, \
                    nc.sbuf_tensor("sums_t" + tag, [P, 3, DP], F32) as sums_t:
                loaded = [sem(f"counts_loaded{b}{tag}") for b in range(3)]
                summed, copied, merged, added = (
                    sem("pair_" + n + tag) for n in ("summed", "copied", "merged", "added"))
                parts = Parts(tag, ps_max, ps_pow)

                def pair(t):
                    if isinstance(t, int) and t == 0:
                        return held
                    return t if isinstance(t, int) and t > held else t - 1

                with nc.Block() as block:
                    @block.sync
                    def _(sp):
                        def load(t, i, b):
                            if isinstance(t, int) and t == 0:
                                return
                            if not isinstance(t, int) or t >= 3:
                                wait_apart(sp, (summed, t - 2))
                            load_pair(sp, pair(t), b, loaded)

                        every_pair(sp, load)

                    @block.tensor
                    def _(pe):
                        def turn(t, b):
                            pe.wait_ge(copied, t + 1)
                            wait_past(pe, added, t - 2)
                            merge_parts(ps_node[:, b, :], sums_t[:, b, :]).then_inc(merged, 1)

                        def sums(t, i, b):
                            begin = isinstance(t, int) and t == 0
                            if isinstance(t, int) and t < 3:
                                if not begin:
                                    pe.wait_ge(loaded[b], 16)
                            else:
                                wait_apart(pe, (loaded[b], 16 * (i + (b > 0))), (copied, t - 2))
                            for h in range(NB):
                                if begin and h % parts.CUT == 0:
                                    pe.wait_ge(parts.low_made, h // parts.CUT + 1)
                                mm = nc.tensor.matmul(ps_sum[:, b, 0:DP], HL[:, h, :], counts8[b][:, h, :],
                                                      start=h == 0, stop=h == NB - 1)
                            mm.then_inc(summed, 1)
                            if not begin:
                                turn(t - 1, (b - 1) % 3)

                        parts.tensor(pe)
                        every_pair(pe, sums)
                        turn(NP - 1, (NP - 1) % 3)

                    @block.scalar
                    def _(act):
                        def copy(t, i, b):
                            act.wait_ge(summed, t + 1)
                            wait_past(act, merged, t - 2)
                            nc.scalar.activation(sums_t[:, b, :], ps_sum[:, b, 0:DP], ACT.Copy).then_inc(copied, 1)
                            if finish and not (isinstance(t, int) and t < 1):
                                finish.exponent(act, t - 1, (b - 1) % 3)

                        parts.scalar(act)
                        every_pair(act, copy)
                        if finish:
                            finish.exponent(act, NP - 1, (NP - 1) % 3)

                    @block.vector
                    def _(dve):
                        def take(t, i, b):
                            dve.wait_ge(merged, t + 1)
                            if not finish:
                                if isinstance(t, int) and t == 0:
                                    dve.wait_ge(parts.low_made, len(parts.cuts))
                                add_pair(pair(t), ps_node[:, b, 0:2 * F], False).then_inc(added, 1)
                                return
                            finish.shift(dve, t, pair(t), b, ps_node[:, b, 0:2 * F], added)
                            if not isinstance(t, int) or t > 0:
                                finish.centre(dve, t - 1, pair(t - 1), (b - 1) % 3)

                        parts.vector(dve)
                        every_pair(dve, take)
                        if finish:
                            finish.centre(dve, NP - 1, pair(NP - 1), (NP - 1) % 3)

        def general_sum(tag, add):
            src_i = scratch(0, TILES, I32)
            own = []

            def sem(name):
                own.append(nc.alloc_semaphore(name=name))
                return own[-1]

            dst_i = scratch(4 * TILES, TILES, I32)
            sum_thirds = sum_dram.rearrange("(c p n) f -> c p (n f)", c=3, p=P)
            zero = scratch(8 * TILES, SUMROWS // 3 // P * F, F32)
            with nc.psum_tensor("ps_dst" + tag, [P, 512], F32) as ps_dst, \
                    nc.psum_tensor("ps_rows" + tag, [P, 512], F32) as ps_rows, \
                    nc.sbuf_tensor("rows_in" + tag, [P, F], F32) as rows_in, \
                    nc.sbuf_tensor("rows_out" + tag, [P, F], F32) as rows_out, \
                    nc.sbuf_tensor("diag" + tag, [P, P], F32) as diag, \
                    nc.sbuf_tensor("same" + tag, [P, P], F32) as same, \
                    nc.sbuf_tensor("earlier" + tag, [P, P], F32) as earlier, \
                    nc.sbuf_tensor("cols" + tag, [P, 5], F32) as cols, \
                    nc.sbuf_tensor("src_col" + tag, [P, 1], U32) as src_col, \
                    nc.sbuf_tensor("to_col" + tag, [P, 1], U32) as to_col:
                tables_ready, zero_made = sem("tables_ready" + tag), sem("zero_made" + tag)
                gathered, scattered = sem("rows_gathered" + tag), sem("rows_scattered" + tag)
                src_ready, diag_ready, dst_spread = (sem(n + tag) for n in ("src_ready", "diag_ready", "dst_spread"))
                same_ready, to_ready, summed = (sem(n + tag) for n in ("same_ready", "to_ready", "summed"))
                rows_ready, step_g = sem("rows_ready" + tag), sem("step_g" + tag)
                with nc.Block() as block:
                    @block.sync
                    def _(sp):
                        sp.dma_start(src_i, a["src_grid"]).then_inc(tables_ready, 16)
                        sp.dma_start(dst_i, a["dst_grid"]).then_inc(tables_ready, 16)
                        sp.dma_start(feat_blocks, Hf[:, :, :]).then_inc(tables_ready, 16)
                        sp.wait_ge(zero_made, 1)
                        for c in range(3):
                            sp.dma_start(sum_thirds[c], zero).then_inc(tables_ready, 16)
                        sp.wait_ge(tables_ready, 16 * 6)

                    @block.vector
                    def _(dve):
                        nc.vector.memset(zero, 0.0).then_inc(zero_made, 1)

                with nc.Block() as block:
                    @block.vector
                    def _(dve):
                        def tile(t):
                            chain = Chain(dve, step_g, 6 * t)
                            dve.wait_ge(gathered, 16 * t)
                            dve.wait_ge(scattered, 16 * t)
                            dve.wait_ge(summed, t)
                            nc.vector.tensor_copy(src_col[:, :].bitcast(I32), src_i[:, bass.ds(t, 1)]) \
                                .then_inc(src_ready, 1)
                            chain.link(nc.vector.tensor_copy(cols[:, 0:1], dst_i[:, bass.ds(t, 1)]))
                            nc.vector.tensor_scalar(diag[:, :], ident[:, :], cols[:, 0:1], None,
                                                    ALU.mult).then_inc(diag_ready, 1)
                            dve.wait_ge(dst_spread, t + 1)
                            nc.vector.tensor_scalar(same[:, :], ps_dst[:, 0:P], cols[:, 0:1], None,
                                                    ALU.is_equal).then_inc(same_ready, 1)
                            dve.wait_ge(same_ready, t + 1)
                            chain.link(nc.vector.tensor_tensor(earlier[:, :], same[:, :], before[:, :], ALU.mult))
                            chain.link(nc.vector.tensor_reduce(cols[:, 1:2], earlier[:, :], AX, ALU.max))
                            chain.link(nc.vector.tensor_tensor(cols[:, 2:3], trash[:, :], cols[:, 0:1], ALU.subtract))
                            chain.link(nc.vector.tensor_tensor(cols[:, 3:4], cols[:, 2:3], cols[:, 1:2], ALU.mult))
                            chain.link(nc.vector.tensor_tensor(cols[:, 4:5], cols[:, 3:4], cols[:, 0:1], ALU.add))
                            nc.vector.tensor_copy(to_col[:, :], cols[:, 4:5]).then_inc(to_ready, 1)
                            assert chain.n == 6

                        tile(0)
                        with dve.Fori(1, TILES) as t:
                            tile(t)

                    @block.gpsimd
                    def _(pool):
                        def tile(t):
                            wait_apart(pool, (src_ready, t + 1), (summed, t))
                            nc.gpsimd.indirect_dma_start(
                                out=rows_in[:, :], out_offset=None, in_=feat_dram,
                                in_offset=bass.IndirectOffsetOnAxis(ap=src_col[:, :], axis=0)).then_inc(gathered, 16)
                            wait_apart(pool, (rows_ready, t + 1), (to_ready, t + 1), (scattered, 16 * t))
                            nc.gpsimd.indirect_dma_start(
                                out=sum_dram, out_offset=bass.IndirectOffsetOnAxis(ap=to_col[:, :], axis=0),
                                in_=rows_out[:, :], in_offset=None, compute_op=ALU.add).then_inc(scattered, 16)

                        tile(0)
                        with pool.Fori(1, TILES) as t:
                            tile(t)
                        pool.wait_ge(scattered, 16 * TILES)

                    @block.tensor
                    def _(pe):
                        def tile(t):
                            pe.wait_ge(diag_ready, t + 1)
                            nc.tensor.matmul(ps_dst[:, 0:P], ones[:, :], diag[:, :], start=True,
                                             stop=True).then_inc(dst_spread, 1)
                            pe.wait_ge(same_ready, t + 1)
                            pe.wait_ge(gathered, 16 * (t + 1))
                            pe.wait_ge(rows_ready, t)
                            nc.tensor.matmul(ps_rows[:, 0:F], same[:, :], rows_in[:, :], start=True,
                                             stop=True).then_inc(summed, 1)

                        tile(0)
                        with pe.Fori(1, TILES) as t:
                            tile(t)

                    @block.scalar
                    def _(act):
                        def tile(t):
                            act.wait_ge(summed, t + 1)
                            act.wait_ge(scattered, 16 * t)
                            nc.scalar.activation(rows_out[:, :], ps_rows[:, 0:F], ACT.Copy).then_inc(rows_ready, 1)

                        tile(0)
                        with act.Fori(1, TILES) as t:
                            tile(t)

                fetched, totalled = sem("fetched" + tag), sem("totalled" + tag)
                got = scratch(0, NB * F, F32).rearrange("p (j f) -> p j f", f=F)
                with nc.Block() as block:
                    @block.sync
                    def _(sp):
                        sp.dma_start(got if add else Hf[:, :, :], sum_blocks).then_inc(fetched, 16)
                        sp.wait_ge(fetched, 16)

                    @block.vector
                    def _(dve):
                        if add:
                            dve.wait_ge(fetched, 16)
                            nc.vector.tensor_tensor(Hf[:, :, :], Hf[:, :, :], got, ALU.add).then_inc(totalled, 1)

            nc.clear_and_free_semaphores(own)
            nc.all_engine_barrier()

        def gcn_dense():
            with nc.psum_tensor("ps_t", [P, 2, EVEN * P], F32) as ps_t, \
                    nc.psum_tensor("ps_h", [P, 2, 2, 512], F32) as ps_h, \
                    nc.psum_tensor("ps_f", [P, 512], F32) as ps_f:
                bufs = [share((P, 2 * EVEN, F), (P, EVEN * P), (P, 2, UN), (P, 2, UN),
                              start=NB * DP + c * GCN_BYTES)
                        for c in range(2)]
                agg, agg_t, neg, lin = zip(*bufs)
                padded = sem("padded")
                scaled, turned, copied, hidden = sem("d_scaled"), sem("d_turned"), sem("d_copied"), sem("d_hidden")
                neg_made, exp_made, lin_made = sem("neg_made"), sem("exp_made"), sem("lin_made")
                elu_made, fused, out_made = sem("elu_made"), sem("fused"), sem("fused_out")

                with nc.Block() as block:
                    @block.gpsimd
                    def _(pool):
                        def scale(u, c):
                            wait_past(pool, turned, u - 1)
                            nc.gpsimd.tensor_tensor(agg[c][:, 0:UB, :], Hf[:, bass.ds(UB * u, UB), :],
                                                    over(dinv[:, bass.ds(UB * u, UB)]),
                                                    ALU.mult).then_inc(scaled, 1)

                        stagger(pool, [(0, scale)], UNITS)

                    @block.vector
                    def _(dve):
                        for c in range(2):
                            nc.vector.memset(agg[c][:, UB:2 * EVEN, :], 0.0).then_inc(padded, 1)

                        def negative(u, c):
                            wait_past(dve, fused, u - 1)
                            for m in range(2):
                                dve.wait_ge(lin_made, 2 * u + m + 1)
                                nc.vector.tensor_scalar(neg[c][:, m, :], lin[c][:, m, :], 0.0, None,
                                                        ALU.min).then_inc(neg_made, 1)

                        def elu(u, c):
                            for m in range(2):
                                dve.wait_ge(exp_made, 2 * u + m + 1)
                                nc.vector.scalar_tensor_tensor(neg[c][:, m, :], neg[c][:, m, :], -1.0,
                                                               lin[c][:, m, :], ALU.add,
                                                               ALU.max).then_inc(elu_made, 1)

                        def leave(u, c):
                            dve.wait_ge(fused, u + 1)
                            nc.vector.tensor_tensor(Hf[:, bass.ds(UB * u, UB), :],
                                                    ps_f[:, 0:UB * F].rearrange("p (j f) -> p j f", f=F),
                                                    over(dinv[:, bass.ds(UB * u, UB)]),
                                                    ALU.mult).then_inc(out_made, 1)
                            dve.wait_ge(out_made, u + 1)
                            nc.vector.tensor_reduce(
                                tops[:, bass.ds(u, 1)],
                                Hf[:, bass.ds(UB * u, UB), :].rearrange("p j f -> p (j f)"), AX, ALU.max,
                                apply_absolute_value=True)

                        stagger(dve, [(3, elu), (4, leave), (2, negative)], UNITS)

                    @block.tensor
                    def _(pe):
                        def turn(u, c):
                            wait_apart(pe, (scaled, u + 1), *([(copied, u - 1)] if not isinstance(u, int) or u > 1 else []))
                            for k in range(EVEN):
                                mm = nc.tensor.transpose(
                                    ps_t[:, c, P * k:P * k + P],
                                    agg[c][:, 2 * k:2 * k + 2, :].rearrange("p j f -> p (j f)"), ident[:, :])
                            mm.then_inc(turned, 1)

                        def hide(u, c):
                            pe.wait_ge(copied, u + 1)
                            for m in range(2):
                                wait_past(pe, lin_made, 2 * u - 1 + m)
                                for h, n in enumerate((EVEN, UB - EVEN)):
                                    mm = nc.tensor.matmul(ps_h[:, m, h, 0:n * P], w_gcn[:, h, m * H:(m + 1) * H],
                                                          agg_t[c][:, 0:n * P], start=True, stop=True)
                                mm.then_inc(hidden, 1)

                        def fuse(u, c):
                            pe.wait_ge(elu_made, 2 * u + 2)
                            wait_past(pe, out_made, u)
                            for k in range(UB):
                                for m in range(2):
                                    mm = nc.tensor.matmul(ps_f[:, F * k:F * k + F], neg[c][:, m, place(k):place(k) + P],
                                                          w_fuse[:, m, :], start=m == 0, stop=m == 1)
                            mm.then_inc(fused, 1)

                        pe.wait_ge(padded, 2)
                        stagger(pe, [(4, fuse), (0, turn), (1, hide)], UNITS)

                    @block.scalar
                    def _(act):
                        def copy(u, c):
                            act.wait_ge(turned, u + 1)
                            wait_past(act, hidden, 2 * u - 2)
                            nc.scalar.activation(agg_t[c], ps_t[:, c, :], ACT.Copy).then_inc(copied, 1)

                        def linear(u, c):
                            wait_past(act, elu_made, 2 * u - 2)
                            for m in range(2):
                                act.wait_ge(hidden, 2 * u + m + 1)
                                nc.scalar.activation(
                                    lin[c][:, m, :], ps_h[:, m, :, :].rearrange("p a b -> p (a b)")[:, 0:UN],
                                    ACT.Identity, bias=b_gcn[:, m:m + 1]).then_inc(lin_made, 1)

                        def exp(u, c):
                            for m in range(2):
                                act.wait_ge(neg_made, 2 * u + m + 1)
                                nc.scalar.activation(neg[c][:, m, :], neg[c][:, m, :], ACT.Exp).then_inc(exp_made, 1)

                        stagger(act, [(1, copy), (3, exp), (2, linear)], UNITS)

        def mlp(tag, width, w1, w2, w3, hb, b3, last):
            with nc.psum_tensor("ps_t" + tag, [P, 2, 512], F32) as ps_t, \
                    nc.psum_tensor("ps_1" + tag, [P, 2, 512], F32) as ps_1, \
                    nc.psum_tensor("ps_2" + tag, [P, 2, 512], F32) as ps_2, \
                    nc.psum_tensor("ps_3" + tag, [P, 512], F32) as ps_3:
                slots, cols = (UB, UN) if last else (2 * EVEN, EVEN * P)
                bufs = [share((P, slots, width), (P, cols), (P, UN), (P, UN), (P, UB, F), (P, 4, UB),
                              start=NB * DP + c * MLP_BYTES) for c in range(2)]
                into, into_t, hid_1, hid_2, res, sums = zip(*bufs)
                taken, kept, turned, copied = (sem(n + tag) for n in ("m_taken", "m_kept", "m_turned", "m_copied"))
                one, one_act, two, two_act = (sem(n + tag) for n in ("m_one", "m_one_act", "m_two", "m_two_act"))
                three, biased = (sem(n + tag) for n in ("m_three", "m_biased"))
                halves = ((0, 512), (512, UN))

                def layer(ps, w, src):
                    for c, (lo, up) in enumerate(halves):
                        mm = nc.tensor.matmul(ps[:, c, 0:up - lo], w[:, :], src[:, lo:up], start=True, stop=True)
                    return mm

                def stacked_layer(ps, w, src):
                    for h, n in enumerate((EVEN, UB - EVEN)):
                        mm = nc.tensor.matmul(ps[:, h, 0:n * P], w[:, h, :], src[:, 0:n * P], start=True, stop=True)
                    return mm

                def at(k):
                    return P * k if last else place(k)

                def whole(ps, n=UN):
                    return ps[:, :, :].rearrange("p a b -> p (a b)")[:, 0:n]

                def unit(t, u):
                    return t[:, bass.ds(UB * u, UB), :]

                if last:
                    taken_x = sem("l_taken_x")
                    centred, squared, var_made, std_made, finished, stored, step_l = (
                        sem("l_" + n) for n in ("centred", "squared", "var_made", "std_made", "finished", "stored",
                                                "step"))
                    step_v, step_r = sem("l_step_v"), sem("l_step_r")
                else:
                    var_made, std_made, step_l = sem("n_var_made"), sem("n_std_made"), sem("n_step")
                    padded = sem("n_padded")

                with nc.Block() as block:
                    @block.gpsimd
                    def _(pool):
                        def take(u, c):
                            wait_past(pool, turned, u - 1)
                            nc.gpsimd.tensor_copy(into[c][:, :, F:2 * F], unit(Hf, u)).then_inc(taken, 1)

                        def keep(u, c):
                            pool.wait_ge(taken, u + 1)
                            nc.gpsimd.tensor_copy(unit(X, u), into[c][:, 0:UB, :]).then_inc(kept, 1)

                        stagger(pool, [(0, take if last else keep)], UNITS)

                    @block.tensor
                    def _(pe):
                        def turn(u, c):
                            wait_apart(pe, (taken, u + 1), *([(taken_x, u + 1)] if last else []),
                                       *([(copied, u)] if not isinstance(u, int) or u else []))
                            for k in range(UB if last else EVEN):
                                what = into[c][:, k, :] if last else \
                                    into[c][:, 2 * k:2 * k + 2, :].rearrange("p j f -> p (j f)")
                                mm = nc.tensor.transpose(ps_t[:, k // 4, k % 4 * P:k % 4 * P + P], what, ident[:, :])
                            mm.then_inc(turned, 1)

                        def first(u, c):
                            pe.wait_ge(copied, u + 1)
                            wait_past(pe, one_act, u)
                            (layer if last else stacked_layer)(ps_1, w1, into_t[c]).then_inc(one, 1)

                        def second(u, c):
                            pe.wait_ge(one_act, u + 1)
                            wait_past(pe, two_act, u)
                            layer(ps_2, w2, hid_1[c]).then_inc(two, 1)

                        def third(u, c):
                            pe.wait_ge(two_act, u + 1)
                            wait_past(pe, biased, u)
                            for k in range(UB):
                                mm = nc.tensor.matmul(ps_3[:, F * k:F * k + F], hid_2[c][:, at(k):at(k) + P], w3[:, :],
                                                      start=True, stop=True)
                            mm.then_inc(three, 1)

                        if not last:
                            pe.wait_ge(padded, 2)
                        stagger(pe, [(4, third), (0, turn), (2, second), (1, first)], UNITS)

                    @block.scalar
                    def _(act):
                        def copy(u, c):
                            act.wait_ge(turned, u + 1)
                            wait_past(act, one, u - 1)
                            nc.scalar.activation(into_t[c], whole(ps_t, cols), ACT.Copy).then_inc(copied, 1)

                        def relu(u, c):
                            act.wait_ge(one, u + 1)
                            wait_past(act, two, u - 1)
                            nc.scalar.activation(hid_1[c], whole(ps_1), ACT.Relu,
                                                 bias=b_hid[:, hb:hb + 1]).then_inc(one_act, 1)

                        def square(u, c):
                            act.wait_ge(centred, u + 1)
                            nc.scalar.activation(res[c], unit(X, u), ACT.Square).then_inc(squared, 1)

                        def root(u, c):
                            act.wait_ge(var_made, u + 1)
                            nc.scalar.activation(sums[c][:, 2, :], sums[c][:, 1, :], ACT.Sqrt).then_inc(std_made, 1)

                        def take_x(u, c):
                            wait_past(act, turned, u - 1)
                            nc.scalar.activation(into[c][:, :, 0:F], unit(X, u), ACT.Copy).then_inc(taken_x, 1)

                        if not last:
                            act.wait_ge(var_made, 1)
                            nc.scalar.activation(stat[:, 2, :], stat[:, 0, :], ACT.Sqrt).then_inc(std_made, 1)
                        stagger(act, [(0, take_x), (1, copy), (2, relu), (6, root), (5, square)] if last else
                                [(1, copy), (2, relu)], UNITS)

                    @block.vector
                    def _(dve):
                        def norm(u, c):
                            wait_past(dve, turned, u - 1)
                            wait_past(dve, kept, u - 1)
                            nc.vector.tensor_tensor(into[c][:, 0:UB, :], unit(X, u), over(stat[:, 1, bass.ds(UB * u, UB)]),
                                                    ALU.mult).then_inc(taken, 1)

                        def relu(u, c):
                            dve.wait_ge(two, u + 1)
                            wait_past(dve, three, u - 1)
                            nc.vector.tensor_scalar(hid_2[c], whole(ps_2), b_hid[:, hb + 1:hb + 2], 0.0, ALU.add,
                                                    ALU.max).then_inc(two_act, 1)

                        def leave(u, c):
                            dve.wait_ge(three, u + 1)
                            if last:
                                wait_past(dve, finished, u - 1)
                            to = res[c] if last else unit(Hf, u)
                            nc.vector.tensor_tensor(to, ps_3[:, 0:UB * F].rearrange("p (j f) -> p j f", f=F),
                                                    each(b3, UB), ALU.add).then_inc(biased, 1)
                            dve.wait_ge(biased, u + 1)
                            if not last:
                                nc.vector.tensor_reduce(tops[:, bass.ds(u, 1)], to.rearrange("p j f -> p (j f)"), AX,
                                                        ALU.max, apply_absolute_value=True)
                                return
                            chain = Chain(dve, step_l, 2 * u)
                            chain.link(nc.vector.tensor_tensor(res[c], res[c], unit(X, u), ALU.add))
                            chain.link(nc.vector.tensor_reduce(sums[c][:, 0, :], res[c], AX, ALU.add))
                            nc.vector.scalar_tensor_tensor(unit(X, u), over(sums[c][:, 0, :]), -1.0 / F, res[c],
                                                           ALU.mult, ALU.add).then_inc(centred, 1)

                        def variance(u, c):
                            chain = Chain(dve, step_v, u)
                            dve.wait_ge(squared, u + 1)
                            chain.link(nc.vector.tensor_reduce(sums[c][:, 3, :], res[c], AX, ALU.add))
                            nc.vector.tensor_scalar(sums[c][:, 1, :], sums[c][:, 3, :], 1.0 / F, EPS, ALU.mult,
                                                    ALU.add).then_inc(var_made, 1)

                        def normed(u, c):
                            chain = Chain(dve, step_r, u)
                            dve.wait_ge(std_made, u + 1)
                            chain.link(nc.vector.reciprocal(sums[c][:, 0, :], sums[c][:, 2, :]))
                            nc.vector.tensor_tensor(unit(X, u), unit(X, u), over(sums[c][:, 0, :]),
                                                    ALU.mult).then_inc(finished, 1)

                        if last:
                            stagger(dve, [(3, relu), (6, normed), (4, leave), (5, variance)], UNITS)
                        else:
                            chain = Chain(dve, step_l)
                            for c in range(2):
                                nc.vector.memset(into[c][:, UB:slots, :], 0.0).then_inc(padded, 1)
                            nc.vector.tensor_scalar(stat[:, 0, :], stat[:, 1, :], 1.0 / F, EPS, ALU.mult,
                                                    ALU.add).then_inc(var_made, 1)
                            dve.wait_ge(std_made, 1)
                            chain.link(nc.vector.reciprocal(stat[:, 1, :], stat[:, 2, :]))
                            stagger(dve, [(0, norm), (3, relu), (4, leave)], UNITS)

                    if last:
                        full = out[0:(NB - 1) * P, :].rearrange("(j p) f -> p j f", p=P)

                        @block.sync
                        def _(sp):
                            def store(u, blocks):
                                wait_apart(sp, (finished, u + 1))
                                sp.dma_start(full[:, bass.ds(UB * u, blocks), :],
                                             X[:, bass.ds(UB * u, blocks), :]).then_inc(stored, 16)

                            store(0, UB)
                            with sp.Fori(1, UNITS - 1) as u:
                                store(u, UB)
                            store(UNITS - 1, UB - 1)
                            sp.dma_start(out[(NB - 1) * P:NODES, :], X[0:LAST, NB - 1, :]).then_inc(stored, 16)
                            sp.wait_ge(stored, 16 * (UNITS + 1))

        prepare()
        general = nc.alloc_registers("general")
        nc.regs_load(general, flag[0:1, 0:1])
        with nc.If_ne(general, 0):
            nc.all_engine_barrier()
            general_degrees()
        normalise()
        with nc.If_ne(general, 0):
            nc.all_engine_barrier()
            general_sum("_g1", True)
        with nc.Else():
            nc.all_engine_barrier()
            first_parts()
            first_sum()
        gcn_dense()
        finish = Finish()
        with nc.If_ne(general, 0):
            nc.all_engine_barrier()
            general_sum("_g2", True)
            finish.alone()
        with nc.Else():
            nc.all_engine_barrier()
            later_sum("_2", finish, NP - 1)
        mlp("_m", F, wm1, wm2, wm3, 0, b_m3, False)
        with nc.If_ne(general, 0):
            nc.all_engine_barrier()
            general_sum("_g3", False)
        with nc.Else():
            nc.all_engine_barrier()
            later_sum("_3", None, NP - 2)
        mlp("_u", 2 * F, wu1, wu2, wu3, 2, b_u3, True)


WEIGHTS = ["L0_gnn_W_nuc", "L0_gnn_b_nuc", "L0_gnn_W_surf", "L0_gnn_b_surf", "L0_gnn_W_fuse", "L0_gnn_b_fuse",
           "L1_gnn_WM1", "L1_gnn_bM1", "L1_gnn_WM2", "L1_gnn_bM2", "L1_gnn_WM3", "L1_gnn_bM3",
           "L1_gnn_WU1", "L1_gnn_bU1", "L1_gnn_WU2", "L1_gnn_bU2", "L1_gnn_WU3", "L1_gnn_bU3"]


def kernel(**inputs):
    import numpy as np
    import concourse.bacc as bacc
    from concourse.bass_utils import run_bass_kernel_spmd

    x, src, dst = (np.asarray(inputs[n]) for n in ("x", "src", "dst"))
    edges = TILES * P
    src_pad = (np.arange(edges + P) % NODES).astype(src.dtype)
    dst_pad = np.full(edges + P, PAD_DST, dst.dtype)
    src_pad[:EDGES], dst_pad[:EDGES] = src, dst
    rows = np.stack([src_pad.reshape(-1, P), dst_pad.reshape(-1, P)], axis=1)
    x_blocks = np.zeros((NB * P, F), x.dtype)
    x_blocks[:NODES] = x
    arrays = {
        "x_blocks": x_blocks,
        "src_grid": np.ascontiguousarray(src_pad[:edges].reshape(P, TILES)),
        "dst_grid": np.ascontiguousarray(dst_pad[:edges].reshape(P, TILES)),
        "row_first": np.ascontiguousarray(dst_pad[:edges:P]),
        "edge_rows": np.ascontiguousarray(np.concatenate([rows[:-1], rows[1:]], axis=1).reshape(TILES, 4 * P)),
    }
    for name in WEIGHTS:
        arrays[name.split("gnn_")[1]] = np.ascontiguousarray(inputs[name])
    nc = bacc.Bacc("TRN2", target_bir_lowering=False, num_devices=1)
    aps = {n: nc.dram_tensor(n + "_in", v.shape, mybir.dt.from_np(v.dtype), kind="ExternalInput").ap()
           for n, v in arrays.items()}
    out = nc.dram_tensor("out_dram", (NODES, F), F32, kind="ExternalOutput").ap()
    build(nc, aps, out)
    r = run_bass_kernel_spmd(nc, [{n + "_in": v for n, v in arrays.items()}], core_ids=[0])
    return r.results[0]["out_dram"]
```
